# Optimizing a Trainium2 kernel written in Bass

```python
import numpy as np
import jax
import jax.numpy as jnp

def _softmax(x, axis=-1):
    return jax.nn.softmax(x, axis=axis)

def _gelu(x):
    return jax.nn.gelu(x, approximate=True)

def _silu(x):
    return jax.nn.silu(x)

def _sigmoid(x):
    return jax.nn.sigmoid(x)

def _layernorm(x, axis=-1, eps=1e-05):
    m = jnp.mean(x, axis=axis, keepdims=True)
    v = jnp.var(x, axis=axis, keepdims=True)
    return (x - m) / jnp.sqrt(v + eps)

def _scatter_add(tgt, idx, src, axis=0):
    return tgt.at[idx].add(src)

def _segment_sum(src, seg, n):
    return jax.ops.segment_sum(src, seg, n)
kernel_name = 'mk_perceiver_d1_seqx_r4_977b57'

def setup_inputs(seed: int=0):
    np.random.seed(seed)
    _w = jnp.asarray

    def _rec_inputs():
        import jax
        import jax.numpy as jnp
        _rk = jax.random.key(seed)
        x = -0.0002928 + 1 * jax.random.normal(jax.random.fold_in(_rk, 1), (4, 256, 256), jnp.float32)
        _lenS = 256 - jax.random.randint(jax.random.fold_in(_rk, 7), (4,), 0, max(1, 256 // 4) + 1, jnp.int32)
        _lenS2 = 4096 - jax.random.randint(jax.random.fold_in(_rk, 8), (4,), 0, max(1, 4096 // 4) + 1, jnp.int32)
        _ctx_1024P = jax.random.normal(jax.random.fold_in(_rk, 11), (4, 16, 256), jnp.float32)
        _ctx_1024c = jax.random.dirichlet(jax.random.fold_in(_rk, 511), 0.3 * jnp.ones((16,), jnp.float32), (4, 4096))
        _ctx_1024t = jnp.einsum('bsk,bkd->bsd', _ctx_1024c, _ctx_1024P)
        _ctx_1024t = _ctx_1024t * jax.lax.rsqrt(jnp.mean(jnp.square(_ctx_1024t)) + 1e-12) * 0.953939
        ctx_1024 = -1.39393e-06 + 0.999914 * (_ctx_1024t + 0.3 * jax.random.normal(jax.random.fold_in(_rk, 611), (4, 4096, 256), jnp.float32))
        return (x, ctx_1024)
    x, ctx_1024 = _rec_inputs()

    def _L0_xattn_setup():
        import jax, jax.numpy as jnp
        import numpy as np
        import math
        D_MODEL = 256
        N_HEADS = 16
        HEAD_DIM = D_MODEL // N_HEADS
        TOP_K = 32
        SCALE = math.sqrt(HEAD_DIM)

        def _split_heads(t, n):
            B, L, _ = t.shape
            return t.reshape(B, L, N_HEADS, HEAD_DIM).transpose(0, 2, 1, 3)
        key = jax.random.key(seed)
        ks = jax.random.split(key, 12)
        B, S, N = (2, 512, 512)
        std = 1.0 / math.sqrt(D_MODEL)
        inp = {'x': jax.random.normal(ks[0], (B, S, D_MODEL), dtype=jnp.float32), 'knowledge_embeddings': jax.random.normal(ks[1], (B, N, D_MODEL), dtype=jnp.float32), 'Wq': jax.random.normal(ks[2], (D_MODEL, D_MODEL), dtype=jnp.float32) * std, 'bq': jnp.zeros((D_MODEL,), dtype=jnp.float32), 'Wk': jax.random.normal(ks[3], (D_MODEL, D_MODEL), dtype=jnp.float32) * std, 'bk': jnp.zeros((D_MODEL,), dtype=jnp.float32), 'Wv': jax.random.normal(ks[4], (D_MODEL, D_MODEL), dtype=jnp.float32) * std, 'bv': jnp.zeros((D_MODEL,), dtype=jnp.float32), 'Wo': jax.random.normal(ks[5], (D_MODEL, D_MODEL), dtype=jnp.float32) * std, 'bo': jnp.zeros((D_MODEL,), dtype=jnp.float32)}
        return inp
    _L0_xattn_all = _L0_xattn_setup()
    _L0_xattn_in = {k: v for k, v in _L0_xattn_all.items() if k in ('Wq', 'bq', 'Wk', 'bk', 'Wv', 'bv', 'Wo', 'bo')}
    del _L0_xattn_all

    def _L0_attn_setup():
        import jax, jax.numpy as jnp
        import numpy as np
        B, L, D, H = (2, 256, 256, 8)
        HD = D // H

        def _deltanet(x, Wq, Wk, Wv, Wb, ln_w, ln_b):
            Bb, Ll, Dd = x.shape
            q = (x @ Wq).reshape(Bb, Ll, H, HD)
            k = (x @ Wk).reshape(Bb, Ll, H, HD)
            k = k / jnp.maximum(jnp.linalg.norm(k, axis=-1, keepdims=True), 1e-12)
            v = jax.nn.silu(x @ Wv).reshape(Bb, Ll, H, HD)
            beta = jax.nn.sigmoid(x @ Wb)
            qs = jnp.moveaxis(q, 1, 0)
            ks_ = jnp.moveaxis(k, 1, 0)
            vs = jnp.moveaxis(v, 1, 0)
            bs = jnp.moveaxis(beta, 1, 0)

            def step(S, inp):
                qt, kt, vt, bt = inp
                Sk = jnp.einsum('bhk,bhkv->bhv', kt, S)
                S = S + jnp.einsum('bh,bhk,bhv->bhkv', bt, kt, vt - Sk)
                ot = jnp.einsum('bhk,bhkv->bhv', qt, S)
                return (S, ot)
            S0 = jnp.zeros((Bb, H, HD, HD), x.dtype)
            _, os_ = jax.lax.scan(step, S0, (qs, ks_, vs, bs))
            o = jnp.moveaxis(os_, 0, 1).reshape(Bb, Ll, Dd)
            mu = jnp.mean(o, axis=-1, keepdims=True)
            var = jnp.var(o, axis=-1, keepdims=True)
            return (o - mu) / jnp.sqrt(var + 1e-05) * ln_w + ln_b
        key = jax.random.key(seed)
        ks = jax.random.split(key, 5)
        s = 1.0 / np.sqrt(D)
        x = jax.random.normal(ks[0], (B, L, D), jnp.float32)
        Wq = jax.random.uniform(ks[1], (D, D), jnp.float32, -s, s)
        Wk = jax.random.uniform(ks[2], (D, D), jnp.float32, -s, s)
        Wv = jax.random.uniform(ks[3], (D, D), jnp.float32, -s, s)
        Wb = jax.random.uniform(ks[4], (D, H), jnp.float32, -s, s)
        ln_w = jnp.ones((D,), jnp.float32)
        ln_b = jnp.zeros((D,), jnp.float32)
        return {'x': x, 'Wq': Wq, 'Wk': Wk, 'Wv': Wv, 'Wb': Wb, 'ln_w': ln_w, 'ln_b': ln_b}
    _L0_attn_all = _L0_attn_setup()
    _L0_attn_in = {k: v for k, v in _L0_attn_all.items() if k in ('Wq', 'Wk', 'Wv', 'Wb', 'ln_w', 'ln_b')}
    del _L0_attn_all

    def _L0_ffn_setup():
        import math
        import jax, jax.numpy as jnp
        import numpy as np
        D_MODEL = 256
        D_FF = 1024
        N_EXPERTS = 8
        CAPACITY_FACTOR = 1.25
        L, B = (128, 8)

        def _route(tokens, router_w):
            T = tokens.shape[0]
            E = router_w.shape[0]
            capacity = int(math.ceil(T / E * CAPACITY_FACTOR))
            logits = tokens @ router_w.T
            probs = jax.nn.softmax(logits, axis=-1)
            top1_idx = jnp.argmax(probs, axis=-1)
            top1_prob = jnp.max(probs, axis=-1)
            order = jnp.lexsort((-top1_prob, top1_idx))
            sorted_e = top1_idx[order]
            counts = jnp.bincount(top1_idx, length=E)
            start = jnp.cumsum(counts) - counts
            pos_in_group = jnp.arange(T) - start[sorted_e]
            keep_sorted = pos_in_group < capacity
            keep = jnp.zeros((T,), bool).at[order].set(keep_sorted)
            return jnp.where(keep, top1_idx, 0).astype(jnp.int32)
        key = jax.random.key(seed)
        ks = jax.random.split(key, 6)
        s_in = 1.0 / math.sqrt(D_MODEL)
        s_ff = 1.0 / math.sqrt(D_FF)
        return {'x': jax.random.normal(ks[0], (L, B, D_MODEL), dtype=jnp.float32), 'router_w': jax.random.uniform(ks[1], (N_EXPERTS, D_MODEL), minval=-s_in, maxval=s_in), 'W1': jax.random.uniform(ks[2], (N_EXPERTS, D_MODEL, D_FF), minval=-s_in, maxval=s_in), 'b1': jax.random.uniform(ks[3], (N_EXPERTS, D_FF), minval=-s_in, maxval=s_in), 'W2': jax.random.uniform(ks[4], (N_EXPERTS, D_FF, D_MODEL), minval=-s_ff, maxval=s_ff), 'b2': jax.random.uniform(ks[5], (N_EXPERTS, D_MODEL), minval=-s_ff, maxval=s_ff)}
    _L0_ffn_all = _L0_ffn_setup()
    _L0_ffn_in = {k: v for k, v in _L0_ffn_all.items() if k in ('router_w', 'W1', 'b1', 'W2', 'b2')}
    del _L0_ffn_all
    return {'x': x, 'ctx_1024': ctx_1024, 'L0_xattn_Wq': _L0_xattn_in['Wq'], 'L0_xattn_bq': _L0_xattn_in['bq'], 'L0_xattn_Wk': _L0_xattn_in['Wk'], 'L0_xattn_bk': _L0_xattn_in['bk'], 'L0_xattn_Wv': _L0_xattn_in['Wv'], 'L0_xattn_bv': _L0_xattn_in['bv'], 'L0_xattn_Wo': _L0_xattn_in['Wo'], 'L0_xattn_bo': _L0_xattn_in['bo'], 'L0_attn_Wq': _L0_attn_in['Wq'], 'L0_attn_Wk': _L0_attn_in['Wk'], 'L0_attn_Wv': _L0_attn_in['Wv'], 'L0_attn_Wb': _L0_attn_in['Wb'], 'L0_attn_ln_w': _L0_attn_in['ln_w'], 'L0_attn_ln_b': _L0_attn_in['ln_b'], 'L0_ffn_router_w': _L0_ffn_in['router_w'], 'L0_ffn_W1': _L0_ffn_in['W1'], 'L0_ffn_b1': _L0_ffn_in['b1'], 'L0_ffn_W2': _L0_ffn_in['W2'], 'L0_ffn_b2': _L0_ffn_in['b2']}

def reference(x, ctx_1024, L0_xattn_Wq, L0_xattn_bq, L0_xattn_Wk, L0_xattn_bk, L0_xattn_Wv, L0_xattn_bv, L0_xattn_Wo, L0_xattn_bo, L0_attn_Wq, L0_attn_Wk, L0_attn_Wv, L0_attn_Wb, L0_attn_ln_w, L0_attn_ln_b, L0_ffn_router_w, L0_ffn_W1, L0_ffn_b1, L0_ffn_W2, L0_ffn_b2):
    import jax
    import jax.numpy as jnp

    def _L0_xattn_ref(x, knowledge_embeddings, Wq, bq, Wk, bk, Wv, bv, Wo, bo):
        import jax, jax.numpy as jnp
        import numpy as np
        import math
        D_MODEL = 256
        N_HEADS = 16
        HEAD_DIM = D_MODEL // N_HEADS
        TOP_K = 32
        SCALE = math.sqrt(HEAD_DIM)

        def _split_heads(t, n):
            B, L, _ = t.shape
            return t.reshape(B, L, N_HEADS, HEAD_DIM).transpose(0, 2, 1, 3)
        B, S, _ = x.shape
        N = knowledge_embeddings.shape[1]
        Q = _split_heads(x @ Wq.T + bq, N_HEADS)
        K = _split_heads(knowledge_embeddings @ Wk.T + bk, N_HEADS)
        V = _split_heads(knowledge_embeddings @ Wv.T + bv, N_HEADS)
        scores = jnp.einsum('bhsd,bhnd->bhsn', Q, K) / SCALE
        k = min(TOP_K, N)
        topk_scores, topk_indices = jax.lax.top_k(scores, k)
        sparse_weights = jax.nn.softmax(topk_scores, axis=-1)
        sel_V = jnp.take_along_axis(V[:, :, None, :, :], topk_indices[..., None], axis=3)
        context = jnp.einsum('bhsk,bhskd->bhsd', sparse_weights, sel_V)
        context = context.transpose(0, 2, 1, 3).reshape(B, S, D_MODEL)
        return context @ Wo.T + bo

    def _L0_attn_ref(x, Wq, Wk, Wv, Wb, ln_w, ln_b):
        import jax, jax.numpy as jnp
        import numpy as np
        B, L, D, H = (2, 256, 256, 8)
        HD = D // H

        def _deltanet(x, Wq, Wk, Wv, Wb, ln_w, ln_b):
            Bb, Ll, Dd = x.shape
            q = (x @ Wq).reshape(Bb, Ll, H, HD)
            k = (x @ Wk).reshape(Bb, Ll, H, HD)
            k = k / jnp.maximum(jnp.linalg.norm(k, axis=-1, keepdims=True), 1e-12)
            v = jax.nn.silu(x @ Wv).reshape(Bb, Ll, H, HD)
            beta = jax.nn.sigmoid(x @ Wb)
            qs = jnp.moveaxis(q, 1, 0)
            ks_ = jnp.moveaxis(k, 1, 0)
            vs = jnp.moveaxis(v, 1, 0)
            bs = jnp.moveaxis(beta, 1, 0)

            def step(S, inp):
                qt, kt, vt, bt = inp
                Sk = jnp.einsum('bhk,bhkv->bhv', kt, S)
                S = S + jnp.einsum('bh,bhk,bhv->bhkv', bt, kt, vt - Sk)
                ot = jnp.einsum('bhk,bhkv->bhv', qt, S)
                return (S, ot)
            S0 = jnp.zeros((Bb, H, HD, HD), x.dtype)
            _, os_ = jax.lax.scan(step, S0, (qs, ks_, vs, bs))
            o = jnp.moveaxis(os_, 0, 1).reshape(Bb, Ll, Dd)
            mu = jnp.mean(o, axis=-1, keepdims=True)
            var = jnp.var(o, axis=-1, keepdims=True)
            return (o - mu) / jnp.sqrt(var + 1e-05) * ln_w + ln_b
        return _deltanet(x, Wq, Wk, Wv, Wb, ln_w, ln_b)

    def _L0_ffn_ref(x, router_w, W1, b1, W2, b2):
        import math
        import jax, jax.numpy as jnp
        import numpy as np
        D_MODEL = 256
        D_FF = 1024
        N_EXPERTS = 8
        CAPACITY_FACTOR = 1.25
        L, B = (128, 8)

        def _route(tokens, router_w):
            T = tokens.shape[0]
            E = router_w.shape[0]
            capacity = int(math.ceil(T / E * CAPACITY_FACTOR))
            logits = tokens @ router_w.T
            probs = jax.nn.softmax(logits, axis=-1)
            top1_idx = jnp.argmax(probs, axis=-1)
            top1_prob = jnp.max(probs, axis=-1)
            order = jnp.lexsort((-top1_prob, top1_idx))
            sorted_e = top1_idx[order]
            counts = jnp.bincount(top1_idx, length=E)
            start = jnp.cumsum(counts) - counts
            pos_in_group = jnp.arange(T) - start[sorted_e]
            keep_sorted = pos_in_group < capacity
            keep = jnp.zeros((T,), bool).at[order].set(keep_sorted)
            return jnp.where(keep, top1_idx, 0).astype(jnp.int32)
        Lx, Bx, D = x.shape
        T = Lx * Bx
        E = router_w.shape[0]
        tokens = x.reshape(T, D)
        final_e = _route(tokens, router_w)
        out = jnp.zeros_like(tokens)
        for e in range(E):
            h = jax.nn.relu(tokens @ W1[e] + b1[e])
            y = h @ W2[e] + b2[e]
            out = out + jnp.where((final_e == e)[:, None], y, 0.0)
        return out.reshape(Lx, Bx, D)
    x = x + _L0_xattn_ref(_layernorm(x, axis=-1), ctx_1024, L0_xattn_Wq, L0_xattn_bq, L0_xattn_Wk, L0_xattn_bk, L0_xattn_Wv, L0_xattn_bv, L0_xattn_Wo, L0_xattn_bo)
    x = x + _L0_attn_ref(_layernorm(x, axis=-1), L0_attn_Wq, L0_attn_Wk, L0_attn_Wv, L0_attn_Wb, L0_attn_ln_w, L0_attn_ln_b)
    x = x + _L0_ffn_ref(_layernorm(x, axis=-1), L0_ffn_router_w, L0_ffn_W1, L0_ffn_b1, L0_ffn_W2, L0_ffn_b2)
    return x

_drawn_inputs = setup_inputs


def setup_inputs(seed=0):
    import zlib

    import numpy as np

    out = dict(_drawn_inputs(seed))
    spreads = {'L0_xattn_bq': (0.0, 0.1),
     'L0_xattn_bk': (0.0, 0.8),
     'L0_xattn_bv': (0.0, 0.1),
     'L0_xattn_bo': (0.0, 0.1),
     'L0_attn_ln_w': (1.0, 0.2),
     'L0_attn_ln_b': (0.0, 0.1)}
    factors = {'L0_ffn_b1': 6.777, 'L0_ffn_b2': 5.338}
    for name, (base, spread) in spreads.items():
        noise = np.random.default_rng([zlib.crc32(name.encode()), seed]).standard_normal(out[name].shape)
        drawn = base * np.exp(spread * noise) if base else spread * noise
        out[name] = jnp.asarray(drawn.astype(out[name].dtype))
    for name, factor in factors.items():
        out[name] = (out[name] * factor).astype(out[name].dtype)
    return out
```

```python
import numpy as np
import concourse.bass as bass
from concourse import mybir
from contextlib import ExitStack

F32 = mybir.dt.float32
BF16 = mybir.dt.bfloat16
I32 = mybir.dt.int32
ACT = mybir.ActivationFunctionType
ALU = mybir.AluOpType
AX = mybir.AxisListType

P = 128
B, S, D = 4, 256, 256
N = 4096
H, HD = 16, 16
TOPK = 32
HEADS = B * H
TOK = B * S
TT = TOK // P
DC = D // P
ST = S // P
EPS_LN = 1e-5
NEG = -3.0e38
BIG = 1.0e30

PARTS = 3
KROWS = 6 * HD
TROWS = PARTS
CHUNK = 128
NCH = N // CHUNK
BANK = 512
SB_N = N // BANK
KEYS_T = 512
NKB = B * N // KEYS_T
UNIT = 4
UNITS = N // P // UNIT
VW = 32
FIRST = 3 * NCH
REST = 5 * NCH
CANDS = 8 + FIRST + REST


class Shared:
    pass


class Chain:

    def __init__(self, eng, sem):
        self.eng, self.sem, self.n = eng, sem, 0

    def __call__(self, ins):
        self.n += 1
        ins.then_inc(self.sem, 1)
        self.eng.wait_ge(self.sem, self.n)


def clear_semaphores(nc, sems):
    with nc.Block() as block:
        @block.sync
        def _(sp):
            for s in sems:
                sp.sem_clear(s)


def ident_step(pool, mat, one, sem, fill=1.0):
    one(pool.memset(mat, 0.0))
    one(pool.affine_select(out=mat, in_=mat, compare_op=ALU.not_equal, fill=fill, base=0,
                           pattern=[[-1, P]], channel_multiplier=1))


def stage_setup(nc, g):
    ctx = ExitStack()
    with ctx:
        def sb(n, s, d=F32):
            return ctx.enter_context(nc.sbuf_tensor(n, s, d))

        mine = []

        def sem(n):
            mine.append(ctx.enter_context(nc.semaphore(n)))
            return mine[-1]

        w_nat = sb("w_nat", [P, 3, DC, D])
        wq_t = sb("wq_t", [P, DC, D])
        bq4 = sb("bq4", [P, DC])
        stats = sb("stats", [P, TT, 6])
        mv = sb("mv", [P, TT, 2])
        veps = sb("veps", [P, TT])
        minus_half = sb("minus_half", [P, TT])
        rstd = sb("rstd", [P, TT])
        xn = sb("xn", [P, TT, D])
        xn_t = sb("xn_t", [P, DC, TOK])
        q32 = sb("q32", [P, DC, TOK])
        qres = sb("qres", [P, DC, TOK])
        qp = sb("qp", [P, PARTS, DC, TOK], BF16)
        ps = ctx.enter_context(nc.psum_tensor("ps_setup", [P, 8, BANK], F32))

        x_in, w_in, small_in = sem("x_in"), sem("w_in"), sem("small_in")
        pool_step, dve_step = sem("setup_pool_step"), sem("setup_dve_step")
        ident_made, stats_made, rstd_made, xn_made = sem("ident_made"), sem("stats_made"), sem("rstd_made"), sem("xn_made")
        w_turned, w_kept, x_turned, x_kept = sem("w_turned"), sem("w_kept"), sem("x_turned"), sem("x_kept")
        q_ready, q_kept, q_split, q_out = sem("q_ready"), sem("q_kept"), sem("q_split"), sem("q_out")
        bq_scaled = sem("bq_scaled")

        with nc.Block() as block:
            @block.sync
            def _(sp):
                sp.dma_start(g.x_sb[:, :, :], g.x.rearrange("(t p) d -> p t d", p=P)).then_inc(x_in, 16)
                for i, w in enumerate((g.xWq, g.xWk, g.xWv)):
                    sp.dma_start(w_nat[:, i], w.rearrange("(c p) d -> p c d", p=P)).then_inc(w_in, 16)
                with nc.allow_non_contiguous_dma("one column of a vector to each partition"):
                    sp.dma_start(g.bq[:, :], g.xbq.rearrange("(c p) -> p c", p=P)).then_inc(small_in, 16)
                    sp.dma_start(g.bk[:, :], g.xbk.rearrange("(c p) -> p c", p=P)).then_inc(small_in, 16)
                sp.dma_start(g.bv_bc[:, :], g.xbv[None, :].to_broadcast([P, D])).then_inc(small_in, 16)
                sp.wait_ge(q_split, PARTS)
                for j in range(PARTS):
                    for m in range(DC):
                        for b in range(B):
                            sp.dma_start(
                                g.qq[b * H + m * 8:b * H + (m + 1) * 8, j],
                                qp[:, j, m, b * S:(b + 1) * S]).then_inc(q_out, 16)
                sp.wait_ge(q_out, 16 * PARTS * DC * B)

            @block.gpsimd
            def _(pool):
                one = Chain(pool, pool_step)
                ident_step(pool, g.ident[:, :], one, pool_step)
                ident_step(pool, g.ident_b[:, :], one, pool_step)
                ident_step(pool, g.minus_b[:, :], one, pool_step, fill=-1.0)
                one(pool.memset(minus_half[:, :], -0.5))
                pool.memset(g.flags[:, :, :], 0.0).then_inc(ident_made, 1)
                pool.wait_ge(stats_made, 1)
                one(nc.gpsimd.tensor_scalar(veps[:, :], mv[:, :, 1], EPS_LN, None, ALU.add))
                nc.gpsimd.tensor_tensor(rstd[:, :], veps[:, :], minus_half[:, :], ALU.pow).then_inc(rstd_made, 1)

            @block.vector
            def _(dve):
                one = Chain(dve, dve_step)
                dve.wait_ge(small_in, 48)
                nc.vector.tensor_scalar(bq4[:, :], g.bq[:, :], 0.25, None, ALU.mult).then_inc(bq_scaled, 1)
                dve.wait_ge(x_in, 16)
                for t in range(TT):
                    one(nc.vector.bn_stats(stats[:, t, :], g.x_sb[:, t, :]))
                    ins = nc.vector.bn_aggr(mv[:, t, :], stats[:, t, :])
                    if t == TT - 1:
                        ins.then_inc(stats_made, 1)
                dve.wait_ge(stats_made, 1)
                dve.wait_ge(rstd_made, 1)
                for t in range(TT):
                    ins = nc.vector.tensor_scalar(xn[:, t, :], g.x_sb[:, t, :], mv[:, t, 0:1], rstd[:, t:t + 1],
                                                  ALU.subtract, ALU.mult)
                ins.then_inc(xn_made, 1)
                dve.wait_ge(q_kept, 4)
                split3(nc, dve, one, q32[:, :, :], qres[:, :, :], [qp[:, j] for j in range(PARTS)], q_split)

            @block.tensor
            def _(pe):
                pe.wait_ge(ident_made, 1)
                pe.wait_ge(w_in, 48)
                for i in range(3):
                    for c in range(DC):
                        for e in range(DC):
                            ins = nc.tensor.transpose(ps[:, i, c * D + e * P:c * D + (e + 1) * P],
                                                      w_nat[:, i, e, c * P:(c + 1) * P], g.ident[:, :])
                    ins.then_inc(w_turned, 1)
                pe.wait_ge(xn_made, 1)
                for c in range(DC):
                    for half in range(2):
                        for t in range(4):
                            ins = nc.tensor.transpose(ps[:, 4 + c * 2 + half, t * P:(t + 1) * P],
                                                      xn[:, half * 4 + t, c * P:(c + 1) * P], g.ident[:, :])
                        ins.then_inc(x_turned, 1)
                pe.wait_ge(w_kept, 3)
                pe.wait_ge(x_kept, 4)
                for m in range(DC):
                    for half in range(2):
                        for c in range(DC):
                            ins = nc.tensor.matmul(ps[:, m * 2 + half, :], wq_t[:, c, m * P:(m + 1) * P],
                                                   xn_t[:, c, half * 512:(half + 1) * 512], start=c == 0, stop=c == DC - 1)
                        ins.then_inc(q_ready, 1)

            @block.scalar
            def _(act):
                for i, dst in enumerate((wq_t, g.wk_t, g.wv_t)):
                    act.wait_ge(w_turned, i + 1)
                    nc.scalar.activation(dst[:, :, :].rearrange("p c d -> p (c d)"), ps[:, i, :], ACT.Copy).then_inc(w_kept, 1)
                for c in range(DC):
                    for half in range(2):
                        act.wait_ge(x_turned, c * 2 + half + 1)
                        nc.scalar.activation(xn_t[:, c, half * 512:(half + 1) * 512], ps[:, 4 + c * 2 + half, :],
                                             ACT.Copy).then_inc(x_kept, 1)
                act.wait_ge(bq_scaled, 1)
                for m in range(DC):
                    for half in range(2):
                        act.wait_ge(q_ready, m * 2 + half + 1)
                        nc.scalar.activation(q32[:, m, half * 512:(half + 1) * 512], ps[:, m * 2 + half, :],
                                             ACT.Identity, bias=bq4[:, m:m + 1], scale=0.25).then_inc(q_kept, 1)

        clear_semaphores(nc, mine)


def split3(nc, dve, one, full, res, parts, done):
    nc.vector.tensor_copy(parts[0], full).then_inc(done, 1)
    dve.wait_ge(done, 1)
    one(nc.vector.tensor_tensor(res, full, parts[0], ALU.subtract))
    nc.vector.tensor_copy(parts[1], res).then_inc(done, 1)
    dve.wait_ge(done, 2)
    nc.vector.tensor_tensor(parts[2], res, parts[1], ALU.subtract).then_inc(done, 1)


def stage_keys(nc, g):
    ctx = ExitStack()
    with ctx:
        def sb(n, s, d=F32):
            return ctx.enter_context(nc.sbuf_tensor(n, s, d))

        mine = []

        def sem(n):
            mine.append(ctx.enter_context(nc.semaphore(n)))
            return mine[-1]

        c_in = sb("c_in", [P, 2, 4, D])
        c_t = sb("c_t", [P, 2, DC, KEYS_T])
        k32 = sb("k32", [P, 2, DC, KEYS_T])
        kres = sb("kres", [P, DC, KEYS_T])
        kp = sb("kp", [P, 2, PARTS, DC, KEYS_T], BF16)
        v_sb = sb("v_sb", [P, 2, H, 4, HD])
        ps_t = ctx.enter_context(nc.psum_tensor("ps_t", [P, DC, KEYS_T], F32))
        ps_k = ctx.enter_context(nc.psum_tensor("ps_k", [P, DC, KEYS_T], F32))
        ps_v = ctx.enter_context(nc.psum_tensor("ps_v", [P, 4, D], F32))
        load_seen = sem("load_seen")
        ctx_in, turned, turned_kept = [sem("ctx_in0"), sem("ctx_in1")], sem("ctx_turned"), sem("ctx_turned_kept")
        k_ready, v_ready, k_kept = sem("k_ready"), sem("v_ready"), sem("k_kept")
        k1_made, kres_made, k2_made, k_split = sem("k1_made"), sem("kres_made"), sem("k2_made"), sem("k_split")
        v_kept, kv_out = sem("v_kept"), [sem("kv_out0"), sem("kv_out1")]
        OUTS = 16 * (PARTS * DC + 1)

        def steps(eng, step):
            step(0, 0, 0, True, False)
            step(1, 1, 0, True, False)
            with eng.Fori(1, NKB // 2 - 1) as k:
                step(k * 2, 0, k, False, False)
                step(k * 2 + 1, 1, k, False, False)
            k = NKB // 2 - 1
            step(k * 2, 0, k, False, False)
            step(k * 2 + 1, 1, k, False, True)

        with nc.Block() as block:
            @block.sync
            def _(sp):
                def store(b, tb, t, j):
                    sp.wait_ge(k_split, t + 1)
                    for q in range(PARTS):
                        for m in range(DC):
                            sp.dma_start(g.kk[bass.ds(b * H + m * 8, 8), q, :, bass.ds(tb * KEYS_T, KEYS_T)],
                                         kp[:, j, q, m, :]).then_inc(kv_out[j], 16)
                    sp.wait_ge(v_kept, t + 1)
                    sp.dma_start(g.vv[bass.ds(b * H, H), :, bass.ds(tb * 4 * HD, 4 * HD)].rearrange("h p c -> p h c"),
                                 v_sb[:, j].rearrange("p h c d -> p h (c d)")).then_inc(kv_out[j], 16)

                with sp.Fori(0, B) as b:
                    with sp.Fori(0, N // KEYS_T // 2) as k:
                        for j in range(2):
                            store(b, k * 2 + j, b * (N // KEYS_T) + k * 2 + j, j)
                sp.wait_ge(kv_out[0], OUTS * NKB // 2)
                sp.wait_ge(kv_out[1], OUTS * NKB // 2)

            @block.gpsimd
            def _(pool):
                def load(t, j):
                    pool.dma_start(c_in[:, j], g.ctx[bass.ds(t * KEYS_T, KEYS_T), :].rearrange("(c p) d -> p c d", p=P)).then_inc(ctx_in[j], 16)

                load(0, 0)
                load(1, 1)
                with pool.Fori(1, NKB // 2) as k:
                    for j in range(2):
                        pool.wait_ge(turned, k * 2 + j - 1)
                        pool.sem_inc(load_seen, 1)
                        load(k * 2 + j, j)

            @block.tensor
            def _(pe):
                def turn(t, j, k, first):
                    pe.wait_ge(ctx_in[j], 16 * (k + 1))
                    if not first:
                        pe.wait_ge(turned_kept, t)
                    for c in range(DC):
                        for n in range(4):
                            ins = nc.tensor.transpose(ps_t[:, c, n * P:(n + 1) * P], c_in[:, j, n, c * P:(c + 1) * P],
                                                      g.ident[:, :])
                    ins.then_inc(turned, 1)

                turn(0, 0, 0, True)

                def step(t, j, k, first, last):
                    if not last:
                        turn(t + 1, 1 - j, k + j, False)
                    pe.wait_ge(turned_kept, t + 1)
                    if not (first and j == 0):
                        pe.wait_ge(k_kept, t)
                    for m in range(DC):
                        for c in range(DC):
                            ins = nc.tensor.matmul(ps_k[:, m, :], g.wk_t[:, c, m * P:(m + 1) * P], c_t[:, j, c, :],
                                                   start=c == 0, stop=c == DC - 1)
                    ins.then_inc(k_ready, 1)
                    if not (first and j == 0):
                        pe.wait_ge(v_kept, t)
                    for n in range(4):
                        for c in range(DC):
                            ins = nc.tensor.matmul(ps_v[:, n, :], c_t[:, j, c, n * P:(n + 1) * P], g.wv_t[:, c, :],
                                                   start=c == 0, stop=c == DC - 1)
                    ins.then_inc(v_ready, 1)
                steps(pe, step)

            @block.scalar
            def _(act):
                def step(t, j, k, first, last):
                    if not first:
                        act.wait_ge(v_ready, t - 1)
                    act.wait_ge(turned, t + 1)
                    nc.scalar.activation(c_t[:, j].rearrange("p c n -> p (c n)"), ps_t[:, :, :].rearrange("p c n -> p (c n)"),
                                         ACT.Copy).then_inc(turned_kept, 1)
                    act.wait_ge(k_ready, t + 1)
                    if not first:
                        act.wait_ge(k_split, t - 1)
                    for m in range(DC):
                        ins = nc.scalar.activation(k32[:, j, m, :], ps_k[:, m, :], ACT.Identity, bias=g.bk[:, m:m + 1])
                    ins.then_inc(k_kept, 1)
                steps(act, step)

            @block.vector
            def _(dve):
                def step(t, j, k, first, last):
                    dve.wait_ge(k_kept, t + 1)
                    if not first:
                        dve.wait_ge(kv_out[j], k * OUTS)
                    full = k32[:, j]
                    nc.vector.tensor_copy(kp[:, j, 0], full).then_inc(k1_made, 1)
                    dve.wait_ge(k1_made, t + 1)
                    nc.vector.tensor_tensor(kres[:, :, :], full, kp[:, j, 0], ALU.subtract).then_inc(kres_made, 1)
                    dve.wait_ge(kres_made, t + 1)
                    nc.vector.tensor_copy(kp[:, j, 1], kres[:, :, :]).then_inc(k2_made, 1)
                    dve.wait_ge(k2_made, t + 1)
                    nc.vector.tensor_tensor(kp[:, j, 2], kres[:, :, :], kp[:, j, 1], ALU.subtract).then_inc(k_split, 1)
                    dve.wait_ge(v_ready, t + 1)
                    for n in range(4):
                        ins = nc.vector.tensor_tensor(v_sb[:, j, :, n, :], ps_v[:, n, :].rearrange("p (h d) -> p h d", d=HD),
                                                      g.bv_bc[:, :].rearrange("p (h d) -> p h d", d=HD), ALU.add)
                    ins.then_inc(v_kept, 1)
                    dve.wait_ge(k_split, t + 1)
                steps(dve, step)

        clear_semaphores(nc, mine)


def stage_attention(nc, g):
    ctx = ExitStack()
    with ctx:
        def sb(n, s, d=F32):
            return ctx.enter_context(nc.sbuf_tensor(n, s, d))

        mine = []

        def sem(n):
            mine.append(ctx.enter_context(nc.semaphore(n)))
            return mine[-1]

        SL = 3
        TIE = 2.0 ** -21
        kop = sb("kop", [P, SL, N], BF16)
        qop = sb("qop", [P, SL, S], BF16)
        v_in = sb("v_in", [P, SL, N // P, HD])
        vs = sb("vs", [P, SL, N // P, VW])
        cand = sb("cand", [P, SL, ST, CANDS])
        work = sb("work", [P, ST, 8 + FIRST])
        top = sb("top", [P, SL, ST, 4, 8])
        mag = sb("mag", [P, ST])
        thr = sb("thr", [P, SL, ST])
        thr_res = sb("thr_res", [P, ST])
        thr_p = sb("thr_p", [P, ST, P], BF16)
        pen = sb("pen", [P, 2, UNIT * S], BF16)
        wgt = sb("wgt", [P, 4, UNIT * S])
        o_sb = sb("o_sb", [P, S])
        sel = sb("sel", [P, HD + 1])
        marks = sb("marks", [P, 2, ST, 8 + FIRST + NCH])
        TREE = (68, 34, 17, 16, 8, 4, 2, 1)
        sums = sb("sums", [P, 2 * ST, 68])
        cnt = sb("cnt", [P, 6, ST])
        ring = ctx.enter_context(nc.psum_tensor("ring", [P, 3, BANK], F32))
        d_ps = ctx.enter_context(nc.psum_tensor("d_ps", [P, 2, UNIT * S], F32))
        o_ps = ctx.enter_context(nc.psum_tensor("o_ps", [P, S], F32))

        k_in = [sem(f"k_in{s}") for s in range(SL)]
        q_in = [sem(f"q_in{s}") for s in range(SL)]
        v_loaded = [sem(f"v_loaded{s}") for s in range(SL)]
        consts, pool_step = sem("att_consts"), sem("att_pool_step")
        v_placed, flag_step, flagged, pool_seen = sem("v_placed"), sem("flag_step"), sem("flagged"), sem("pool_seen")
        s_ready, s_used, seen = sem("s_ready"), sem("s_used"), sem("s_seen")
        dve_step, thr_ready, thr_turned, thr_kept = sem("att_dve_step"), sem("thr_ready"), sem("thr_turned"), sem("thr_kept")
        d_ready, pen_ready, pen_added, w_ready, w_used = sem("d_ready"), sem("pen_ready"), sem("pen_added"), sem("w_ready"), sem("w_used")
        o_kept, u_ready, u_kept = sem("o_kept"), sem("u_ready"), sem("u_kept")


        def steps(eng, step):
            for i in range(SL):
                step(i, i, 0, i)
            with eng.Fori(1, HEADS // SL) as k:
                for j in range(SL):
                    step(k * SL + j, j, k, None)
            for i in range(HEADS // SL * SL, HEADS + 3):
                step(i, i % SL, i // SL, i)

        def has_head(i, back=0):
            return i is None or 0 <= i - back < HEADS

        def pair_of(p):
            return (2, 4 + 2 * p) if p < 2 else (1, 2 * (p - 2))

        order = [("s", 0), ("s", 1), ("u", 0)] + [("s", s) for s in range(2, 7)] + [("t", 0)] + [("s", s) for s in range(7, 16)]
        place = {use: n for n, use in enumerate(order)}

        with nc.Block() as block:
            @block.sync
            def _(sp):
                def step(n, j, k, i):
                    if not has_head(i):
                        return
                    if i is None or i >= SL:
                        sp.wait_ge(d_ready, (n - 2) * UNITS)
                    sp.dma_start(kop[0:3 * HD, j, :], g.kk[bass.ds(n, 1), 0:3].rearrange("o q r n -> (o q r) n")).then_inc(k_in[j], 16)
                    sp.dma_start(kop[3 * HD:5 * HD, j, :], g.kk[bass.ds(n, 1), 0:2].rearrange("o q r n -> (o q r) n")).then_inc(k_in[j], 16)
                    sp.dma_start(kop[5 * HD:6 * HD, j, :], g.kk[bass.ds(n, 1), 0:1].rearrange("o q r n -> (o q r) n")).then_inc(k_in[j], 16)
                    for row, (q, times) in zip((0, 1, 2, 3, 4, 5), ((0, 1), (0, 1), (0, 1), (1, 1), (1, 1), (2, 1))):
                        sp.dma_start(qop[row * HD:(row + 1) * HD, j, :],
                                     g.qq[bass.ds(n, 1), q:q + 1].rearrange("o q r n -> (o q r) n")).then_inc(q_in[j], 16)
                    if i is None or i >= SL:
                        sp.wait_ge(v_placed, n - 2)
                    sp.dma_start(v_in[:, j], g.vv[bass.ds(n, 1)].rearrange("o p (c d) -> (o p) c d", d=HD)).then_inc(v_loaded[j], 16)
                steps(sp, step)

            @block.gpsimd
            def _(pool):
                one = Chain(pool, pool_step)
                one(pool.memset(vs[:, :, :, :], 0.0))
                one(pool.memset(vs[:, :, :, HD:HD + 1], 1.0))
                one(pool.memset(kop[96:P, :, :], -1.0))
                one(pool.memset(thr_p[:, :, :], 0.0))
                one(pool.memset(marks[:, :, :, :], 0.0))
                one(pool.memset(sel[:, :], 0.0))
                for q in range(4):
                    one(pool.affine_select(out=sel[:, :], in_=sel[:, :], compare_op=ALU.not_equal, fill=1.0,
                                           base=-32 * q, pattern=[[-1, HD + 1]], channel_multiplier=1))
                pool.memset(cnt[:, :, :], 0.0).then_inc(consts, 1)
                pool.wait_ge(consts, 1)

                def step(n, j, k, i):
                    def one(ins, c):
                        ins.then_inc(flag_step, 1)
                        pool.wait_ge(flag_step, c)

                    if not has_head(i):
                        return
                    pool.wait_ge(v_loaded[j], 16 * (k + 1))
                    if i is None or i >= SL:
                        pool.wait_ge(w_used, (n - 2) * UNITS)
                    pool.sem_inc(pool_seen, 1)
                    nc.gpsimd.tensor_copy(vs[:, j, :, 0:HD], v_in[:, j]).then_inc(v_placed, 1)
                    pool.wait_ge(thr_ready, n + 1)
                    pool.sem_inc(pool_seen, 1)
                    pool.sem_clear(flag_step)
                    for t in range(ST):
                        nc.gpsimd.tensor_scalar(marks[:, 0, t, 0:8 + FIRST], cand[:, j, t, 0:8 + FIRST], thr[:, j, t:t + 1], None, ALU.is_ge)
                        nc.gpsimd.tensor_scalar(marks[:, 0, t, 8 + FIRST:], cand[:, j, t, CANDS - NCH:], thr[:, j, t:t + 1], 64.0,
                                                ALU.is_ge, ALU.mult)
                        ins = nc.gpsimd.tensor_scalar(marks[:, 1, t, 0:8 + FIRST], cand[:, j, t, 0:8 + FIRST], top[:, j, t, 3, 7:8],
                                                      None, ALU.is_ge)
                    one(ins, 1)
                    src, c = marks[:, :, :, :].rearrange("p k t c -> p (k t) c"), 2
                    for width in TREE:
                        dst = sums[:, :, 0:width]
                        if width == 16:
                            dst, width = sums[:, :, 0:1], 1
                            one(nc.gpsimd.tensor_tensor(dst, src[:, :, 0:1], src[:, :, 16:17], ALU.add), c)
                        else:
                            one(nc.gpsimd.tensor_tensor(dst, src[:, :, 0:width], src[:, :, width:2 * width], ALU.add), c)
                        src, c = sums, c + 1
                    nc.gpsimd.tensor_scalar(cnt[:, 0, :], sums[:, 0:ST, 0], 33.5, None, ALU.is_ge)
                    nc.gpsimd.tensor_scalar(cnt[:, 1, :], sums[:, ST:2 * ST, 0], 32.5, None, ALU.is_ge)
                    nc.gpsimd.tensor_tensor(cnt[:, 2, :], cand[:, j, :, 7], thr[:, j, :], ALU.subtract)
                    one(nc.gpsimd.tensor_tensor(cnt[:, 3, :], top[:, j, :, 0, 0], thr[:, j, :], ALU.subtract), c)
                    nc.gpsimd.tensor_scalar(cnt[:, 2, :], cnt[:, 2, :], 0.0, None, ALU.is_ge)
                    nc.gpsimd.tensor_scalar(cnt[:, 3, :], cnt[:, 3, :], 60.0, None, ALU.is_ge)
                    one(nc.gpsimd.tensor_tensor(cnt[:, 0, :], cnt[:, 0, :], cnt[:, 1, :], ALU.add), c + 1)
                    one(nc.gpsimd.tensor_tensor(cnt[:, 2, :], cnt[:, 2, :], cnt[:, 3, :], ALU.add), c + 2)
                    nc.gpsimd.tensor_tensor(g.flags[:, bass.ds(n, 1), :].rearrange("p o t -> p (o t)"), cnt[:, 0, :], cnt[:, 2, :],
                                            ALU.add).then_inc(flagged, 1)
                    pool.wait_ge(flagged, n + 1)
                    pool.sem_inc(pool_seen, 1)
                steps(pool, step)

            @block.vector
            def _(dve):
                dve.wait_ge(consts, 1)

                def refine(one, r, j, t):
                    row = cand[:, j, t, :]
                    if r == 0:
                        one(nc.vector.max(row[:, 0:8], row[:, 8 + FIRST:CANDS]))
                    elif r % 2:
                        one(nc.vector.max(top[:, j, t, r // 2, :], row[:, 0:8 + FIRST] if r == 1 else work[:, t, :]))
                    else:
                        one(nc.vector.match_replace(work[:, t, :], top[:, j, t, r // 2 - 1, :],
                                                    row[:, 0:8 + FIRST] if r == 2 else work[:, t, :], NEG))

                def threshold(one, r, n, j, i):
                    v1, v32 = top[:, j, :, 0, 0], top[:, j, :, 3, 7]
                    if r == 0:
                        one(nc.vector.scalar_tensor_tensor(mag[:, :], v32, -1.0, v1, ALU.mult, ALU.max))
                    elif r == 1:
                        one(nc.vector.scalar_tensor_tensor(thr[:, j, :], mag[:, :], -TIE, v32, ALU.mult, ALU.add))
                    elif r == 2:
                        if has_head(i, 2):
                            dve.wait_ge(thr_turned, n - 1)
                        one(nc.vector.tensor_copy(thr_p[:, :, 96], thr[:, j, :]))
                    elif r == 3:
                        one(nc.vector.tensor_tensor(thr_res[:, :], thr[:, j, :], thr_p[:, :, 96], ALU.subtract))
                    elif r == 4:
                        one(nc.vector.tensor_copy(thr_p[:, :, 97], thr_res[:, :]))
                    else:
                        nc.vector.tensor_tensor(thr_p[:, :, 98], thr_res[:, :], thr_p[:, :, 97], ALU.subtract).then_inc(thr_ready, 1)

                def step(n, j, k, i):
                    if not has_head(i) and not has_head(i, 1):
                        return
                    if has_head(i, 3) and has_head(i):
                        dve.wait_ge(flagged, n - 2)
                        dve.sem_inc(seen, 1)
                    dve.sem_clear(dve_step)
                    one = Chain(dve, dve_step)
                    before = (j - 1) % SL
                    for t in range(ST):
                        for s in range(SB_N):
                            if has_head(i):
                                dve.wait_ge(s_ready, n * (ST * SB_N) + t * SB_N + s + 1)
                                dve.sem_inc(seen, 1)
                            for c in range(BANK // CHUNK):
                                at = 8 + s * (BANK // CHUNK) + c
                                if has_head(i):
                                    ins = nc.vector.max(cand[:, j, t, at:at + 7 * NCH + 1:NCH],
                                                        ring[:, place["s", t * SB_N + s] % 3, c * CHUNK:(c + 1) * CHUNK])
                                    if c == BANK // CHUNK - 1:
                                        ins.then_inc(s_used, 1)
                                r = s * (BANK // CHUNK) + c
                                if t == 0 and has_head(i, 1):
                                    if r < 8:
                                        refine(one, r, before, 1)
                                    elif r < 14:
                                        threshold(one, r - 8, n, before, i)
                                if t == 1 and has_head(i) and r < 8:
                                    refine(one, r, j, 0)
                        if has_head(i):
                            dve.wait_ge(s_used, n * (ST * SB_N) + (t + 1) * SB_N)
                            dve.sem_inc(seen, 1)
                steps(dve, step)

            @block.tensor
            def _(pe):
                pe.wait_ge(consts, 1)

                def step(n, j, k, i):
                    def ring_free(use):
                        if i is not None and i >= HEADS:
                            pe.wait_ge(s_used, HEADS * ST * SB_N)
                            pe.wait_ge(thr_kept, min(HEADS, n - 1))
                            pe.wait_ge(u_kept, n - 3 if use[0] == "u" else n - 2)
                            return
                        at = place[use] - 3
                        back = 0 if at >= 0 else 1
                        kind, s = order[at % len(order)]
                        if kind == "s":
                            if has_head(i, back):
                                pe.wait_ge(s_used, (n - back) * (ST * SB_N) + s + 1)
                        elif kind == "t":
                            if has_head(i, back + 1):
                                pe.wait_ge(thr_kept, n - back)
                        elif has_head(i, back + 3):
                            pe.wait_ge(u_kept, n - back - 2)

                    def score(s):
                        if not has_head(i):
                            return
                        if s == 0:
                            pe.wait_ge(k_in[j], 48 * (k + 1))
                            pe.wait_ge(q_in[j], 96 * (k + 1))
                        ring_free(("s", s))
                        t, c = divmod(s, SB_N)
                        nc.tensor.matmul(ring[:, place["s", s] % 3, :], qop[0:KROWS, j, t * P:(t + 1) * P],
                                         kop[0:KROWS, j, c * BANK:(c + 1) * BANK], start=True, stop=True).then_inc(s_ready, 1)

                    def turn():
                        if not has_head(i, 1):
                            return
                        pe.wait_ge(thr_ready, n)
                        ring_free(("t", 0))
                        for t in range(ST):
                            ins = nc.tensor.matmul(ring[:, place["t", 0] % 3, t * P:(t + 1) * P], thr_p[:, t, :], g.ident_b[:, :],
                                                   start=True, stop=True)
                        ins.then_inc(thr_turned, 1)

                    def gather():
                        if not has_head(i, 3):
                            return
                        pe.wait_ge(o_kept, n - 2)
                        ring_free(("u", 0))
                        for t in range(ST):
                            ins = nc.tensor.matmul(ring[:, place["u", 0] % 3, t * (HD + 1):(t + 1) * (HD + 1)],
                                                   o_sb[:, t * P:(t + 1) * P], sel[:, :], start=True, stop=True)
                        ins.then_inc(u_ready, 1)

                    def differ(back, u):
                        if not has_head(i, back):
                            return
                        sl = (j - back) % SL
                        unit = (n - back) * UNITS + u
                        if u == 0:
                            pe.wait_ge(thr_kept, n - back + 1)
                        if u >= 2 or has_head(i, back + 1):
                            pe.wait_ge(w_ready, unit - 1)
                        for c in range(UNIT):
                            at = (u * UNIT + c) * P
                            ins = nc.tensor.matmul(d_ps[:, u % 2, c * S:(c + 1) * S], kop[0:KROWS + TROWS, sl, at:at + P],
                                             qop[0:KROWS + TROWS, sl, :], start=c * S % BANK == 0, stop=True,
                                             skip_group_check=True)
                        ins.then_inc(d_ready, 1)

                    def punish(back, u):
                        if not has_head(i, back):
                            return
                        pe.wait_ge(pen_ready, (n - back) * UNITS + u + 1)
                        for c in range(UNIT * S // BANK):
                            ins = nc.tensor.matmul(d_ps[:, u % 2, c * BANK:(c + 1) * BANK], g.minus_b[:, :],
                                                   pen[:, u % 2, c * BANK:(c + 1) * BANK], start=False, stop=True,
                                                   skip_group_check=True)
                        ins.then_inc(pen_added, 1)

                    def weigh(back, u):
                        if not has_head(i, back):
                            return
                        sl = (j - back) % SL
                        if u == 0:
                            pe.wait_ge(v_placed, n - back + 1)
                            if has_head(i, back + 1):
                                pe.wait_ge(o_kept, n - back)
                        pe.wait_ge(w_ready, (n - back) * UNITS + u + 1)
                        for c in range(UNIT):
                            ins = nc.tensor.matmul(o_ps[32 * c:32 * c + VW, :], vs[:, sl, u * UNIT + c, :],
                                                   wgt[:, u % 4, c * S:(c + 1) * S], start=u == 0, stop=u == UNITS - 1)
                        ins.then_inc(w_used, 1)

                    for p in range(4):
                        back, u = pair_of(p)
                        wback, wu = pair_of(p - 1) if p else (2, 2)
                        differ(back, u)
                        score(4 * p)
                        score(4 * p + 1)
                        if p == 0:
                            gather()
                        differ(back, u + 1)
                        weigh(wback, wu)
                        score(4 * p + 2)
                        punish(back, u)
                        if p == 1:
                            turn()
                        score(4 * p + 3)
                        weigh(wback, wu + 1)
                        punish(back, u + 1)
                steps(pe, step)

            @block.scalar
            def _(act):
                def step(n, j, k, i):
                    def penalty(back, u):
                        if not has_head(i, back):
                            return
                        act.wait_ge(d_ready, (n - back) * UNITS + u + 1)
                        nc.scalar.activation(pen[:, u % 2, :], d_ps[:, u % 2, :], ACT.Relu, scale=-BIG).then_inc(pen_ready, 1)

                    def weight(back, u):
                        if not has_head(i, back):
                            return
                        unit = (n - back) * UNITS + u
                        if u >= 4 or has_head(i, back + 1):
                            act.wait_ge(w_used, unit - 3)
                        act.wait_ge(pen_added, unit + 1)
                        nc.scalar.activation(wgt[:, u % 4, :], d_ps[:, u % 2, :], ACT.Exp).then_inc(w_ready, 1)

                    for p in range(4):
                        back, u = pair_of(p)
                        penalty(back, u)
                        penalty(back, u + 1)
                        if p == 3 and has_head(i, 2):
                            act.wait_ge(w_used, (n - 1) * UNITS)
                            if has_head(i, 3):
                                act.wait_ge(u_ready, n - 2)
                            nc.scalar.activation(o_sb[:, :], o_ps[:, :], ACT.Copy).then_inc(o_kept, 1)
                        weight(back, u)
                        if p == 1 and has_head(i, 1):
                            act.wait_ge(thr_turned, n)
                            nc.scalar.activation(qop[96:96 + TROWS, (j - 1) % SL, :], ring[96:96 + TROWS, place["t", 0] % 3, 0:S],
                                                 ACT.Copy).then_inc(thr_kept, 1)
                        if p == 0 and has_head(i, 3):
                            act.wait_ge(u_ready, n - 2)
                            nc.scalar.activation(g.u[:, bass.ds(n - 3, 1), :, :].rearrange("p o t c -> p (o t c)"),
                                                 ring[:, place["u", 0] % 3, 0:ST * (HD + 1)], ACT.Copy).then_inc(u_kept, 1)
                        weight(back, u + 1)
                steps(act, step)

        clear_semaphores(nc, mine)


def stage_exact(nc, g):
    ctx = ExitStack()
    with ctx:
        def sb(n, s, d=F32):
            return ctx.enter_context(nc.sbuf_tensor(n, s, d))

        mine = []

        def sem(n):
            mine.append(ctx.enter_context(nc.semaphore(n)))
            return mine[-1]

        kop, qop = sb("x_kop", [P, N], BF16), sb("x_qop", [P, S], BF16)
        v_in = sb("x_v", [P, N // P, HD])
        sc, left, wgt, wgt_t = sb("x_sc", [P, N]), sb("x_left", [P, N]), sb("x_wgt", [P, N]), sb("x_wgt_t", [P, N // P, P])
        top, neg_max = sb("x_top", [P, TOPK // 8, 8]), sb("x_neg_max", [P, 1])
        f_head, f_all, ones, f_int = sb("x_f_head", [P, HEADS]), sb("x_f_all", [P, 1]), sb("x_ones", [P, P]), sb("x_f_int", [P, HEADS + 1], I32)
        ps = ctx.enter_context(nc.psum_tensor("ps_x", [P, 8, BANK], F32))
        ones_made, flag_sum, f_step = sem("ex_ones_made"), sem("ex_flag_sum"), sem("ex_flag_step")
        names = ("loaded dve_step scored kept exp_done weighed turned turned_kept summed out_kept neg_made head_done").split()
        m = {n: sem("ex_" + n) for n in names}

        with nc.Block() as block:
            @block.gpsimd
            def _(pool):
                pool.memset(ones[:, :], 1.0).then_inc(ones_made, 1)

            @block.vector
            def _(dve):
                one = Chain(dve, f_step)
                dve.wait_ge(flag_sum, 1)
                one(nc.vector.tensor_reduce(f_head[:, :], ps[:, 0, 0:HEADS * ST].rearrange("p (n t) -> p n t", t=ST), axis=AX.X, op=ALU.max))
                one(nc.vector.tensor_reduce(f_all[:, :], f_head[:, :], axis=AX.X, op=ALU.max))
                one(nc.vector.tensor_scalar(f_int[:, 0:HEADS], f_head[:, :], 1.0, None, ALU.min))
                one(nc.vector.tensor_scalar(f_int[:, HEADS:HEADS + 1], f_all[:, :], 1.0, None, ALU.min))

            @block.tensor
            def _(pe):
                pe.wait_ge(ones_made, 1)
                nc.tensor.matmul(ps[:, 0, 0:HEADS * ST], ones[:, :], g.flags[:, :, :].rearrange("p n t -> p (n t)"),
                                 start=True, stop=True).then_inc(flag_sum, 1)

        def flagged_heads(eng, work):
            any_flag = eng.value_load(f_int[0:1, HEADS:HEADS + 1], min_val=0, max_val=1)
            with eng.If(any_flag > 0):
                with eng.Fori(0, HEADS) as n:
                    flag = eng.value_load(f_int[0:1, bass.ds(n, 1)], min_val=0, max_val=1)
                    with eng.If(flag > 0):
                        work(n)

        def last_wait(eng, s, value):
            eng.wait_ge(s, value)
            eng.sem_clear(s)

        with nc.Block() as block:
            @block.sync
            def _(sp):
                def head(n):
                    def rows(q):
                        return g.kk[bass.ds(n, 1), q:q + 1].rearrange("o q r n -> (o q r) n"), \
                            g.qq[bass.ds(n, 1), q:q + 1].rearrange("o q r n -> (o q r) n")
                    for at, (kq, qq) in enumerate(((0, 0), (1, 0), (2, 0), (0, 1), (1, 1), (0, 2))):
                        sp.dma_start(kop[at * HD:(at + 1) * HD, :], rows(kq)[0]).then_inc(m["loaded"], 16)
                        sp.dma_start(qop[at * HD:(at + 1) * HD, :], rows(qq)[1]).then_inc(m["loaded"], 16)
                    sp.dma_start(v_in[:, :, :], g.vv[bass.ds(n, 1)].rearrange("o p (c d) -> (o p) c d", d=HD)).then_inc(m["loaded"], 16)
                    last_wait(sp, m["head_done"], 1)
                flagged_heads(sp, head)

            @block.tensor
            def _(pe):
                def head(n):
                    last_wait(pe, m["loaded"], 16 * 13)
                    for t in range(ST):
                        if t:
                            last_wait(pe, m["out_kept"], 1)
                        for c in range(SB_N):
                            ins = nc.tensor.matmul(ps[:, c, :], qop[0:KROWS, t * P:(t + 1) * P], kop[0:KROWS, c * BANK:(c + 1) * BANK],
                                                   start=True, stop=True)
                        ins.then_inc(m["scored"], 1)
                        last_wait(pe, m["weighed"], 1)
                        for c in range(N // P):
                            ins = nc.tensor.transpose(ps[:, c // 4, (c % 4) * P:(c % 4 + 1) * P], wgt[:, c * P:(c + 1) * P], g.ident[:, :])
                        ins.then_inc(m["turned"], 1)
                        last_wait(pe, m["turned_kept"], 1)
                        for c in range(N // P):
                            ins = nc.tensor.matmul(ps[:, 0, 0:HD], wgt_t[:, c, :], v_in[:, c, :], start=c == 0, stop=c == N // P - 1)
                        ins.then_inc(m["summed"], 1)
                flagged_heads(pe, head)

            @block.scalar
            def _(act):
                def head(n):
                    for t in range(ST):
                        last_wait(act, m["scored"], 1)
                        for c in range(0, SB_N, 4):
                            ins = nc.scalar.activation(sc[:, c * BANK:(c + 4) * BANK], ps[:, c:c + 4, :].rearrange("p c n -> p (c n)"),
                                                       ACT.Copy)
                        ins.then_inc(m["kept"], 1)
                        last_wait(act, m["neg_made"], 1)
                        nc.scalar.activation(wgt[:, :], sc[:, :], ACT.Exp, bias=neg_max[:, :]).then_inc(m["exp_done"], 1)
                        last_wait(act, m["turned"], 1)
                        for c in range(0, SB_N, 4):
                            ins = nc.scalar.activation(wgt_t[:, c * 4:(c + 4) * 4, :].rearrange("p c n -> p (c n)"),
                                                       ps[:, c:c + 4, :].rearrange("p c n -> p (c n)"), ACT.Copy)
                        ins.then_inc(m["turned_kept"], 1)
                flagged_heads(act, head)

            @block.vector
            def _(dve):
                def head(n):
                    dve.sem_clear(m["dve_step"])
                    one = Chain(dve, m["dve_step"])
                    for t in range(ST):
                        last_wait(dve, m["kept"], 1)
                        src = sc
                        for r in range(TOPK // 8):
                            one(nc.vector.max(top[:, r, :], src[:, :]))
                            if r == 0:
                                nc.vector.tensor_scalar(neg_max[:, :], top[:, 0, 0:1], -1.0, None, ALU.mult).then_inc(m["neg_made"], 1)
                            one(nc.vector.match_replace(left[:, :], top[:, r, :], src[:, :], NEG))
                            src = left
                        last_wait(dve, m["exp_done"], 1)
                        one(nc.vector.scalar_tensor_tensor(wgt[:, :], left[:, :], NEG * 0.99, wgt[:, :], ALU.is_le, ALU.mult))
                        nc.vector.tensor_reduce(g.u[:, bass.ds(n, 1), t, HD], wgt[:, :], axis=AX.X, op=ALU.add).then_inc(m["weighed"], 1)
                        last_wait(dve, m["summed"], 1)
                        nc.vector.tensor_copy(g.u[:, bass.ds(n, 1), t, 0:HD].rearrange("p o d -> p (o d)"), ps[:, 0, 0:HD]) \
                            .then_inc(m["out_kept"] if t < ST - 1 else m["head_done"], 1)
                flagged_heads(dve, head)

        clear_semaphores(nc, mine)


def stage_out(nc, g):
    ctx = ExitStack()
    with ctx:
        def sb(n, s, d=F32):
            return ctx.enter_context(nc.sbuf_tensor(n, s, d))

        mine = []

        def sem(n):
            mine.append(ctx.enter_context(nc.semaphore(n)))
            return mine[-1]

        wo_nat = sb("wo_nat", [P, DC, D])
        wo_t = sb("wo_t", [P, DC, D])
        bo_bc = sb("bo_bc", [P, D])
        rec = sb("rec", [P, HEADS, ST])
        co = sb("co", [P, TT, D])
        co_t = sb("co_t", [P, DC, TOK])
        ps = ctx.enter_context(nc.psum_tensor("ps_out", [P, 8, BANK], F32))
        wo_in, bo_in, step_, turned, kept = sem("wo_in"), sem("bo_in"), sem("out_dve_step"), sem("out_turned"), sem("out_kept")
        wo_turned, wo_kept, co_made, o_ready = sem("wo_turned"), sem("wo_kept"), sem("co_made"), sem("proj_ready")
        with nc.Block() as block:
            @block.sync
            def _(sp):
                sp.dma_start(wo_nat[:, :, :], g.xWo.rearrange("(c p) d -> p c d", p=P)).then_inc(wo_in, 16)
                sp.dma_start(bo_bc[:, :], g.xbo[None, :].to_broadcast([P, D])).then_inc(bo_in, 16)
            @block.vector
            def _(dve):
                one = Chain(dve, step_)
                dve.wait_ge(bo_in, 16)
                one(nc.vector.tensor_tensor(g.x_sb[:, :, :], g.x_sb[:, :, :], bo_bc[:, None, :].to_broadcast([P, TT, D]), ALU.add))
                one(nc.vector.reciprocal(rec[:, :, :], g.u[:, :, :, HD]))
                for t in range(TT):
                    b, q = divmod(t, ST)
                    ins = nc.vector.tensor_tensor(co[:, t, :].rearrange("p (h d) -> p h d", d=HD), g.u[:, b * H:(b + 1) * H, q, 0:HD],
                                                  rec[:, b * H:(b + 1) * H, q:q + 1].to_broadcast([P, H, HD]), ALU.mult)
                ins.then_inc(co_made, 1)
                for t in range(TT):
                    dve.wait_ge(o_ready, t // 2 * 2 + 2)
                    ins = nc.vector.tensor_tensor(g.x_sb[:, t, :], ps[:, 4 + t // 2, (t % 2) * D:(t % 2 + 1) * D],
                                                  g.x_sb[:, t, :], ALU.add)
                one(ins)

            @block.tensor
            def _(pe):
                pe.wait_ge(wo_in, 16)
                for c in range(DC):
                    for e in range(DC):
                        ins = nc.tensor.transpose(ps[:, 7, c * D + e * P:c * D + (e + 1) * P], wo_nat[:, e, c * P:(c + 1) * P], g.ident[:, :])
                ins.then_inc(wo_turned, 1)
                pe.wait_ge(co_made, 1)
                for c in range(DC):
                    for half in range(2):
                        for t in range(4):
                            ins = nc.tensor.transpose(ps[:, c * 2 + half, t * P:(t + 1) * P], co[:, half * 4 + t, c * P:(c + 1) * P], g.ident[:, :])
                        ins.then_inc(turned, 1)
                pe.wait_ge(wo_kept, 1)
                pe.wait_ge(kept, 4)
                for t in range(TT):
                    for c in range(DC):
                        ins = nc.tensor.matmul(ps[:, 4 + t // 2, (t % 2) * D:(t % 2 + 1) * D], co_t[:, c, t * P:(t + 1) * P], wo_t[:, c, :],
                                               start=c == 0, stop=c == DC - 1)
                    ins.then_inc(o_ready, 1)

            @block.scalar
            def _(act):
                act.wait_ge(wo_turned, 1)
                nc.scalar.activation(wo_t[:, :, :].rearrange("p c d -> p (c d)"), ps[:, 7, :], ACT.Copy).then_inc(wo_kept, 1)
                for c in range(DC):
                    for half in range(2):
                        act.wait_ge(turned, c * 2 + half + 1)
                        nc.scalar.activation(co_t[:, c, half * 512:(half + 1) * 512], ps[:, c * 2 + half, :], ACT.Copy).then_inc(kept, 1)

        clear_semaphores(nc, mine)


def layer_norm(nc, dve, one, rows, n, stats, mv, stats_made, rstd_made, rstd, out, out_made, count):
    for t in range(n):
        one(nc.vector.bn_stats(stats[:, t, :], rows(t)))
        ins = nc.vector.bn_aggr(mv[:, t, :], stats[:, t, :])
    ins.then_inc(stats_made, 1)
    dve.wait_ge(rstd_made, count)
    for t in range(n):
        ins = nc.vector.tensor_scalar(out[:, t, :], rows(t), mv[:, t, 0:1], rstd[:, t:t + 1], ALU.subtract, ALU.mult)
    ins.then_inc(out_made, 1)


def rstd_steps(nc, pool, one, mv, veps, power, rstd, rstd_made):
    one(nc.gpsimd.tensor_scalar(veps, mv[:, :, 1], EPS_LN, None, ALU.add))
    nc.gpsimd.tensor_tensor(rstd, veps, power, ALU.pow).then_inc(rstd_made, 1)


def stage_delta(nc, g):
    RH = 8
    RD = D // RH
    RG = P // RD
    HG = RH // RG
    NC2 = S // P
    NM = NC2 * HG
    LEVELS = 7
    ctx = ExitStack()
    with ctx:
        def sb(n, s, d=F32):
            return ctx.enter_context(nc.sbuf_tensor(n, s, d))

        mine = []

        def sem(n):
            mine.append(ctx.enter_context(nc.semaphore(n)))
            return mine[-1]

        w = sb("dw", [P, 3, DC, D])
        wb = sb("dwb", [P, DC, RH])
        lnw_bc, lnb_bc = sb("lnw_bc", [P, D]), sb("lnb_bc", [P, D])
        masks = sb("level_masks", [P, LEVELS, P])
        mask0t = sb("mask0t", [P, P])
        upper, upper_in = sb("upper", [P, P]), sb("upper_in", [P, P])
        half = sb("half", [P, NC2 * RH])
        minus_half = sb("minus_half_d", [P, NC2])
        stats, mv, veps, rstd = sb("d_stats", [P, NC2, 6]), sb("d_mv", [P, NC2, 2]), sb("d_veps", [P, NC2]), sb("d_rstd", [P, NC2])
        xn, xn_t, q_t = sb("d_xn", [P, NC2, D]), sb("d_xn_t", [P, DC, S]), sb("d_q_t", [P, DC, S])
        k_raw, v_raw, beta = sb("d_k", [P, NC2, D]), sb("d_v", [P, NC2, D]), sb("d_beta", [P, NC2, RH])
        sq, n2, nrm = sb("d_sq", [P, NC2, D]), sb("d_n2", [P, NC2 * RH]), sb("d_nrm", [P, NC2 * RH])
        ev, vb = sb("d_ev", [P, NC2, D]), sb("d_vb", [P, NC2, D])
        kn, kb, kn_t, kb_t = sb("d_kn", [P, NC2, D]), sb("d_kb", [P, NC2, D]), sb("d_kn_t", [P, DC, S]), sb("d_kb_t", [P, DC, S])
        up, tm, tt, wm, mt = [sb(f"d_{n}", [P, RG, NM, P]) for n in ("up", "tm", "tt", "wm", "mt")]
        u, s1, r1 = sb("d_u", [P, NC2, D]), sb("d_s1", [P, HG, RD]), sb("d_r1", [P, D])
        o, on = sb("d_o", [P, NC2, D]), sb("d_on", [P, NC2, D])
        ps = ctx.enter_context(nc.psum_tensor("ps_d", [P, 8, BANK], F32))

        once_in, once_pool = sem("d_once_in"), sem("d_once_pool")
        names = ("d_dve_step d_pool_step d_stats_made d_rstd_made d_xn_made d_turned d_turned_kept d_projected d_q_kept d_kv_kept "
                 "d_beta_exp d_ev_made d_n2_made d_norm_made d_keys_made d_keys_turned d_keys_kept d_gram d_gram_kept d_mgram d_mgram_kept "
                 "d_w_ready d_w_kept d_z_ready d_z_kept d_u_ready d_u_kept d_s_ready d_s_kept d_r_ready d_r_kept d_o_ready d_o_kept").split()
        m = {n[2:]: sem(n) for n in names}

        with nc.Block() as block:
            @block.sync
            def _(sp):
                for i, src in enumerate((g.dWq, g.dWk, g.dWv)):
                    sp.dma_start(w[:, i], src.rearrange("(c p) d -> p c d", p=P)).then_inc(once_in, 16)
                sp.dma_start(wb[:, :, :], g.dWb.rearrange("(c p) d -> p c d", p=P)).then_inc(once_in, 16)
                sp.dma_start(lnw_bc[:, :], g.lnw[None, :].to_broadcast([P, D])).then_inc(once_in, 16)
                sp.dma_start(lnb_bc[:, :], g.lnb[None, :].to_broadcast([P, D])).then_inc(once_in, 16)
                sp.wait_ge(once_in, 96)

            @block.gpsimd
            def _(pool):
                one = Chain(pool, once_pool)

                def keep(mat, cond, pattern, base, mult):
                    one(pool.affine_select(out=mat, in_=mat, compare_op=cond, fill=0.0, base=base, pattern=pattern,
                                           channel_multiplier=mult))
                one(pool.memset(half[:, :], 0.5))
                one(pool.memset(minus_half[:, :], -0.5))
                one(pool.memset(upper[:, :], 1.0))
                one(pool.memset(upper_in[:, :], 1.0))
                one(pool.memset(masks[:, :, :], 1.0))
                one(pool.memset(mask0t[:, :], 1.0))
                keep(upper[:, :], ALU.is_gt, [[1, P]], 0, -1)
                keep(upper_in[:, :], ALU.is_ge, [[1, P]], 0, -1)
                for lv in range(LEVELS):
                    w2, w1 = 2 << lv, 1 << lv
                    cols = masks[:, lv, :].rearrange("p (a q b) -> p a q b", q=2, b=w1)
                    one(pool.memset(cols[:, :, 1, :], 0.0))
                    first = masks[:, lv, :].rearrange("p (a b) -> p a b", b=w2)
                    keep(first, ALU.is_ge, [[-w2, P // w2], [0, w2]], -w1, 1)
                    keep(first, ALU.is_ge, [[w2, P // w2], [0, w2]], w2 - 1, -1)
                cols = mask0t[:, :].rearrange("p (a b) -> p a b", b=2)
                one(pool.memset(cols[:, :, 0:1], 0.0))
                keep(cols, ALU.is_equal, [[-2, P // 2], [0, 2]], 0, 1)

        with nc.Fori(0, B) as b:
            with nc.Block() as block:
                def rows(c):
                    return g.x_sb[:, bass.ds(b * NC2 + c, 1), :].rearrange("p o d -> p (o d)")

                def head(c, h):
                    hg, hr = divmod(h, RG)
                    return hg, hr, c * HG + hg

                def four(mask):
                    return mask[:, None, :].to_broadcast([P, NM, P])

                @block.gpsimd
                def _(pool):
                    one = Chain(pool, m["pool_step"])
                    pool.wait_ge(m["stats_made"], 1)
                    rstd_steps(nc, pool, one, mv, veps[:, :], minus_half[:, :], rstd[:, :], m["rstd_made"])
                    pool.wait_ge(m["n2_made"], 1)
                    nc.gpsimd.tensor_tensor(nrm[:, :], n2[:, :], half[:, :], ALU.pow).then_inc(m["norm_made"], 1)
                    pool.wait_ge(m["stats_made"], 2)
                    rstd_steps(nc, pool, one, mv, veps[:, :], minus_half[:, :], rstd[:, :], m["rstd_made"])

                @block.vector
                def _(dve):
                    one = Chain(dve, m["dve_step"])
                    layer_norm(nc, dve, one, rows, NC2, stats, mv, m["stats_made"], m["rstd_made"], rstd, xn, m["xn_made"], 1)
                    dve.wait_ge(m["beta_exp"], 1)
                    one(nc.vector.tensor_scalar(beta[:, :, :], beta[:, :, :], 1.0, None, ALU.add))
                    one(nc.vector.reciprocal(beta[:, :, :], beta[:, :, :]))
                    dve.wait_ge(m["kv_kept"], 2)
                    one(nc.vector.tensor_tensor(sq[:, :, :], k_raw[:, :, :], k_raw[:, :, :], ALU.mult))
                    nc.vector.tensor_reduce(n2[:, :], sq[:, :, :].rearrange("p c (h d) -> p (c h) d", d=RD), axis=AX.X,
                                            op=ALU.add).then_inc(m["n2_made"], 1)
                    one(nc.vector.tensor_scalar(ev[:, :, :], ev[:, :, :], 1.0, None, ALU.add))
                    one(nc.vector.reciprocal(ev[:, :, :], ev[:, :, :]))
                    one(nc.vector.tensor_tensor(vb[:, :, :], v_raw[:, :, :], ev[:, :, :], ALU.mult))

                    def heads(x):
                        return x[:, :, :].rearrange("p c (h d) -> p (c h) d", d=RD)
                    b_bc = beta[:, :, :].rearrange("p c h -> p (c h)")[:, :, None].to_broadcast([P, NC2 * RH, RD])
                    one(nc.vector.tensor_tensor(heads(vb), heads(vb), b_bc, ALU.mult))
                    dve.wait_ge(m["norm_made"], 1)
                    one(nc.vector.tensor_scalar(nrm[:, :], nrm[:, :], 1e-12, None, ALU.max))
                    one(nc.vector.reciprocal(nrm[:, :], nrm[:, :]))
                    one(nc.vector.tensor_tensor(heads(kn), heads(k_raw), nrm[:, :, None].to_broadcast([P, NC2 * RH, RD]), ALU.mult))
                    nc.vector.tensor_tensor(heads(kb), heads(kn), b_bc, ALU.mult).then_inc(m["keys_made"], 1)
                    for r in range(RG):
                        dve.wait_ge(m["gram"], r + 1)
                        nc.vector.tensor_tensor(up[:, r], ps[:, r, :].rearrange("p (m c) -> p m c", c=P), four(upper), ALU.mult)
                        one(nc.vector.tensor_tensor(tm[:, r], ps[:, 4 + r, :].rearrange("p (m c) -> p m c", c=P), four(masks[:, 0, :]), ALU.mult))
                        nc.vector.tensor_tensor(tm[:, r], four(g.ident), tm[:, r], ALU.subtract).then_inc(m["gram_kept"], 1)
                        one(nc.vector.tensor_tensor(tt[:, r], up[:, r], four(mask0t), ALU.mult))
                        one(nc.vector.tensor_tensor(tt[:, r], four(g.ident), tt[:, r], ALU.subtract))
                    for r in range(RG):
                        dve.wait_ge(m["mgram"], r + 1)
                        nc.vector.tensor_tensor(mt[:, r], ps[:, r, :].rearrange("p (m c) -> p m c", c=P), four(upper_in), ALU.mult).then_inc(m["mgram_kept"], 1)
                    for lv in range(1, LEVELS):
                        for r in range(RG):
                            dve.wait_ge(m["w_ready"], (lv - 1) * RG + r + 1)
                            nc.vector.tensor_tensor(wm[:, r], ps[:, r, :].rearrange("p (m c) -> p m c", c=P), four(masks[:, lv, :]),
                                                    ALU.mult).then_inc(m["w_kept"], 1)
                        for r in range(RG):
                            dve.wait_ge(m["z_ready"], (lv - 1) * RG + r + 1)
                            if lv < LEVELS - 1:
                                nc.vector.tensor_tensor(tm[:, r], tm[:, r], ps[:, r, :].rearrange("p (m c) -> p m c", c=P), ALU.subtract)
                            nc.vector.tensor_tensor(tt[:, r], tt[:, r], ps[:, 4 + r, :].rearrange("p (m c) -> p m c", c=P),
                                                    ALU.subtract).then_inc(m["z_kept"], 1)
                    dve.wait_ge(m["r_ready"], 1)
                    hv = "p (g r d) -> p r g d"
                    nc.vector.tensor_tensor(r1[:, :].rearrange(hv, r=RG, d=RD), vb[:, 1, :].rearrange(hv, r=RG, d=RD),
                                            ps[:, 2:6, 0:HG * RD].rearrange("p r (g d) -> p r g d", d=RD), ALU.subtract).then_inc(m["r_kept"], 1)
                    dve.wait_ge(m["o_kept"], 1)
                    dve.wait_ge(m["o_ready"], 2)
                    one(nc.vector.tensor_tensor(o[:, 1, :].rearrange(hv, r=RG, d=RD), o[:, 1, :].rearrange(hv, r=RG, d=RD),
                                                ps[:, 2:6, HG * RD:2 * HG * RD].rearrange("p r (g d) -> p r g d", d=RD), ALU.add))
                    layer_norm(nc, dve, one, lambda c: o[:, c, :], NC2, stats, mv, m["stats_made"], m["rstd_made"], rstd, on, m["xn_made"], 2)
                    dve.wait_ge(m["xn_made"], 2)
                    one(nc.vector.tensor_tensor(on[:, :, :], on[:, :, :], lnw_bc[:, None, :].to_broadcast([P, NC2, D]), ALU.mult))
                    one(nc.vector.tensor_tensor(on[:, :, :], on[:, :, :], lnb_bc[:, None, :].to_broadcast([P, NC2, D]), ALU.add))
                    xb = g.x_sb[:, bass.ds(b * NC2, NC2), :]
                    one(nc.vector.tensor_tensor(xb, xb, on[:, :, :], ALU.add))

                @block.scalar
                def _(act):
                    act.wait_ge(m["turned"], 1)
                    nc.scalar.activation(xn_t[:, :, :].rearrange("p c n -> p (c n)"), ps[:, 0, :], ACT.Copy).then_inc(m["turned_kept"], 1)
                    act.wait_ge(m["projected"], 1)
                    nc.scalar.activation(beta[:, :, :].rearrange("p c h -> p (c h)"), ps[:, 4, 0:NC2 * RH], ACT.Exp, scale=-1.0).then_inc(m["beta_exp"], 1)
                    act.wait_ge(m["projected"], 2)
                    nc.scalar.activation(k_raw[:, :, :].rearrange("p c d -> p (c d)"), ps[:, 2, :], ACT.Copy).then_inc(m["kv_kept"], 1)
                    act.wait_ge(m["projected"], 3)
                    nc.scalar.activation(v_raw[:, :, :].rearrange("p c d -> p (c d)"), ps[:, 3, :], ACT.Copy)
                    nc.scalar.activation(ev[:, :, :].rearrange("p c d -> p (c d)"), ps[:, 3, :], ACT.Exp, scale=-1.0).then_inc(m["kv_kept"], 1)
                    act.wait_ge(m["projected"], 4)
                    nc.scalar.activation(q_t[:, :, :].rearrange("p c n -> p (c n)"), ps[:, 1, :], ACT.Copy).then_inc(m["q_kept"], 1)
                    act.wait_ge(m["keys_turned"], 1)
                    nc.scalar.activation(kn_t[:, :, :].rearrange("p c n -> p (c n)"), ps[:, 5, :], ACT.Copy)
                    nc.scalar.activation(kb_t[:, :, :].rearrange("p c n -> p (c n)"), ps[:, 6, :], ACT.Copy).then_inc(m["keys_kept"], 1)
                    act.wait_ge(m["u_ready"], 1)
                    nc.scalar.activation(u[:, 0, :], ps[:, 0, 0:D], ACT.Copy).then_inc(m["u_kept"], 1)
                    act.wait_ge(m["s_ready"], 1)
                    nc.scalar.activation(s1[:, :, :].rearrange("p g d -> p (g d)"), ps[:, 1, 0:HG * RD], ACT.Copy).then_inc(m["s_kept"], 1)
                    act.wait_ge(m["u_ready"], 2)
                    nc.scalar.activation(u[:, 1, :], ps[:, 6, 0:D], ACT.Copy).then_inc(m["u_kept"], 1)
                    act.wait_ge(m["o_ready"], 1)
                    nc.scalar.activation(o[:, :, :].rearrange("p c d -> p (c d)"), ps[:, 7, :], ACT.Copy).then_inc(m["o_kept"], 1)

                @block.tensor
                def _(pe):
                    mm = nc.tensor.matmul
                    pe.wait_ge(m["xn_made"], 1)
                    for c in range(DC):
                        for t in range(NC2):
                            ins = nc.tensor.transpose(ps[:, 0, c * S + t * P:c * S + (t + 1) * P], xn[:, t, c * P:(c + 1) * P], g.ident[:, :])
                    ins.then_inc(m["turned"], 1)
                    pe.wait_ge(m["turned_kept"], 1)
                    for bank, wi in ((4, None), (2, 1), (3, 2)):
                        for t in range(NC2):
                            n = RH if wi is None else D
                            for c in range(DC):
                                ins = mm(ps[:, bank, t * n:(t + 1) * n], xn_t[:, c, t * P:(t + 1) * P],
                                         wb[:, c, :] if wi is None else w[:, wi, c, :], start=c == 0, stop=c == DC - 1)
                        ins.then_inc(m["projected"], 1)
                    for e in range(DC):
                        for c in range(DC):
                            ins = mm(ps[:, 1, e * S:(e + 1) * S], w[:, 0, c, e * P:(e + 1) * P], xn_t[:, c, :], start=c == 0, stop=c == DC - 1)
                    ins.then_inc(m["projected"], 1)
                    pe.wait_ge(m["keys_made"], 1)
                    for bank, src in ((5, kn), (6, kb)):
                        for c in range(DC):
                            for t in range(NC2):
                                ins = nc.tensor.transpose(ps[:, bank, c * S + t * P:c * S + (t + 1) * P], src[:, t, c * P:(c + 1) * P], g.ident[:, :])
                    ins.then_inc(m["keys_turned"], 1)
                    pe.wait_ge(m["keys_kept"], 1)
                    pe.wait_ge(m["q_kept"], 1)

                    def gram(bank, left, right):
                        for hg in range(HG):
                            for c in range(NC2):
                                for r in range(RG):
                                    part = slice(RD * r, RD * (r + 1))
                                    at = (c * HG + hg) * P
                                    ins = mm(ps[:, bank + r, at:at + P], left[part, hg, c * P:(c + 1) * P], right[part, hg, c * P:(c + 1) * P],
                                             start=True, stop=True)
                                    if hg == HG - 1 and c == NC2 - 1:
                                        yield ins
                    for ins in gram(4, kb_t, kn_t):
                        pass
                    for ins in gram(0, kn_t, kb_t):
                        ins.then_inc(m["gram"], 1)
                    pe.wait_ge(m["gram_kept"], RG)
                    for ins in gram(0, kn_t, q_t):
                        ins.then_inc(m["mgram"], 1)
                    pe.wait_ge(m["mgram_kept"], RG)
                    for lv in range(1, LEVELS):
                        for r in range(RG):
                            if lv > 1:
                                pe.wait_ge(m["z_kept"], (lv - 2) * RG + r + 1)
                            for i in range(NM):
                                ins = mm(ps[:, r, i * P:(i + 1) * P], up[:, r, i, :], tm[:, r, i, :], start=True, stop=True)
                            ins.then_inc(m["w_ready"], 1)
                        for r in range(RG):
                            pe.wait_ge(m["w_kept"], (lv - 1) * RG + r + 1)
                            for i in range(NM):
                                if lv < LEVELS - 1:
                                    mm(ps[:, r, i * P:(i + 1) * P], tt[:, r, i, :], wm[:, r, i, :], start=True, stop=True)
                                ins = mm(ps[:, 4 + r, i * P:(i + 1) * P], wm[:, r, i, :], tt[:, r, i, :], start=True, stop=True)
                            ins.then_inc(m["z_ready"], 1)
                    pe.wait_ge(m["z_kept"], (LEVELS - 1) * RG)

                    def col(h):
                        return slice(h * RD, (h + 1) * RD)
                    for h in range(RH):
                        hg, r, i = head(0, h)
                        ins = mm(ps[:, 0, col(h)], tt[:, r, i, :], vb[:, 0, col(h)], start=True, stop=True)
                    ins.then_inc(m["u_ready"], 1)
                    pe.wait_ge(m["u_kept"], 1)
                    for h in range(RH):
                        hg, r, i = head(0, h)
                        ins = mm(ps[RD * r:RD * (r + 1), 1, hg * RD:(hg + 1) * RD], kn[:, 0, col(h)], u[:, 0, col(h)], start=True, stop=True)
                    ins.then_inc(m["s_ready"], 1)
                    pe.wait_ge(m["s_kept"], 1)
                    for h in range(RH):
                        hg, r, i = head(1, h)
                        part = slice(RD * r, RD * (r + 1))
                        ins = mm(ps[:, 2 + r, hg * RD:(hg + 1) * RD], kb_t[part, hg, P:2 * P], s1[part, hg, :], start=True, stop=True)
                    ins.then_inc(m["r_ready"], 1)
                    pe.wait_ge(m["r_kept"], 1)
                    for h in range(RH):
                        hg, r, i = head(1, h)
                        ins = mm(ps[:, 6, col(h)], tt[:, r, i, :], r1[:, col(h)], start=True, stop=True)
                    ins.then_inc(m["u_ready"], 1)
                    pe.wait_ge(m["u_kept"], 2)
                    for c in range(NC2):
                        for h in range(RH):
                            hg, r, i = head(c, h)
                            ins = mm(ps[:, 7, c * D + h * RD:c * D + (h + 1) * RD], mt[:, r, i, :], u[:, c, col(h)], start=True, stop=True)
                    ins.then_inc(m["o_ready"], 1)
                    for h in range(RH):
                        hg, r, i = head(1, h)
                        part = slice(RD * r, RD * (r + 1))
                        ins = mm(ps[:, 2 + r, (HG + hg) * RD:(HG + hg + 1) * RD], q_t[part, hg, P:2 * P], s1[part, hg, :], start=True, stop=True)
                    ins.then_inc(m["o_ready"], 1)

            with nc.Block() as block:
                @block.sync
                def _(sp):
                    for s in m.values():
                        sp.sem_clear(s)

        clear_semaphores(nc, mine)


def stage_experts(nc, g):
    E, F = 8, 1024
    CAP = TOK * 5 // (4 * E)
    FC = F // P
    SLOTS0 = TOK
    SLOTS = SLOTS0 + (E - 1) * CAP
    HALF = CAP // 2
    G0 = 512
    ctx = ExitStack()
    with ctx:
        def sb(n, s, d=F32):
            return ctx.enter_context(nc.sbuf_tensor(n, s, d))

        mine = []

        def sem(n):
            mine.append(ctx.enter_context(nc.semaphore(n)))
            return mine[-1]

        r_nat, r_t = sb("r_nat", [E, D]), sb("r_t", [P, DC, E])
        b1, b2 = sb("b1_sb", [P, E, FC]), sb("b2_sb", [P, E, DC])
        w1, w2 = sb("w1_sb", [P, 2, DC, F]), sb("w2_sb", [P, 2, FC, D])
        power = sb("e_power", [P, TT])
        stats, mv, veps, rstd = sb("e_stats", [P, TT, 6]), sb("e_mv", [P, TT, 2]), sb("e_veps", [P, TT]), sb("e_rstd", [P, TT])
        xn, xn_t = sb("e_xn", [P, TT, D]), sb("e_xn_t", [P, DC, TOK])
        zero = sb("e_zero", [P, D])
        iota_i, iota_e = sb("iota_i", [P, E], I32), sb("iota_e", [P, E])
        lg, mx, ex, sm = sb("logits", [P, TT, E]), sb("e_mx", [P, TT]), sb("e_ex", [P, TT, E]), sb("e_sm", [P, TT])
        prob, pick, idx = sb("prob", [P, TT]), sb("pick", [P, TT, E]), sb("e_idx", [P, TT])
        hot, hot_b = sb("hot", [P, TT, E]), sb("hot_b", [P, TT, E], BF16)
        p_wide, p_row = sb("p_wide", [P, TT, P]), sb("p_row", [P, TOK])
        before, eqm = sb("before", [P, TT, TOK], BF16), sb("eqm", [P, P])
        later = sb("later", [P, P])
        ones_b = sb("ones_b", [P, P], BF16)
        cnt, over_e, pre = sb("e_cnt", [P, E]), sb("e_over", [P, E]), sb("e_pre", [P, E])
        base_i, base, jump = sb("base_i", [P, E], I32), sb("base", [P, E]), sb("jump", [P, E])
        rk, tmp = sb("e_rank", [P, TT]), sb("e_tmp", [P, TT, E])
        sa, sj, ov, slot, slot_u = sb("e_sa", [P, TT]), sb("e_sj", [P, TT]), sb("e_ov", [P, TT]), sb("e_slot", [P, TT]), sb("e_slot_u", [P, TT], mybir.dt.uint32)
        xs0, xs0_t = sb("xs0", [P, 4, D]), sb("xs0_t", [P, DC, G0])
        hid = sb("hid", [P, FC, G0])
        y_t, y_nat = sb("y_t", [P, DC, G0]), sb("y_nat", [P, 4, D])
        got = sb("got", [P, TT, D])
        ps = ctx.enter_context(nc.psum_tensor("ps_e", [P, 8, BANK], F32))

        m = {n: sem("e_" + n) for n in (
            "small_in zero_made zero_out pool_step dve_step stats_made rstd_made xn_made turned turned_kept r_turned r_kept logits_ready "
            "logits_kept exp_made prob_wide p_turned p_kept before_made ranks_ready ranks_kept slots_made scattered x_in x_turned x_kept "
            "h_ready h_kept y_ready y_kept y_turned y_out_kept y_out gathered done stored w1_in w2_in w_done xin_free").split()}
        xs, ys = g.xs, g.ys
        jobs = [(0, s, P, G0 // P) for s in range(0, SLOTS0, G0)] + [(e, SLOTS0 + (e - 1) * CAP, HALF, 2) for e in range(1, E)]

        with nc.Block() as block:
            def store_y(sp, i):
                e, s, rows, n = jobs[i]
                sp.wait_ge(m["y_out_kept"], i + 1)
                sp.dma_start(ys[s:s + rows * n, :].rearrange("(c p) d -> p c d", p=rows), y_nat[0:rows, 0:n, :]).then_inc(m["y_out"], 16)

            @block.sync
            def _(sp):
                sp.dma_start(r_nat[:, :], g.router).then_inc(m["small_in"], 16)
                with nc.allow_non_contiguous_dma("vectors to partitions"):
                    for e in range(E):
                        sp.dma_start(b1[:, e, :], g.b1[e].rearrange("(c p) -> p c", p=P)).then_inc(m["small_in"], 16)
                        sp.dma_start(b2[:, e, :], g.b2[e].rearrange("(c p) -> p c", p=P)).then_inc(m["small_in"], 16)

                def weights(e):
                    if e >= 2:
                        sp.wait_ge(m["w_done"], e - 1)
                    sp.dma_start(w1[:, e % 2], g.W1[e].rearrange("(c p) f -> p c f", p=P)).then_inc(m["w1_in"], 16)
                    sp.dma_start(w2[:, e % 2], g.W2[e].rearrange("(c p) d -> p c d", p=P)).then_inc(m["w2_in"], 16)
                weights(0)
                weights(1)
                sp.wait_ge(m["zero_made"], 1)
                for s in range(0, SLOTS, P):
                    n = min(P, SLOTS - s)
                    sp.dma_start(xs[s:s + n, :], zero[0:n, :]).then_inc(m["zero_out"], 16)
                sp.wait_ge(m["scattered"], 16 * TT)
                for i, (e, s, rows, n) in enumerate(jobs):
                    if i:
                        sp.wait_ge(m["x_turned"], i)
                    sp.dma_start(xs0[0:rows, 0:n, :], xs[s:s + rows * n, :].rearrange("(c p) d -> p c d", p=rows)).then_inc(m["x_in"], 16)
                    if e >= 1 and e + 1 < E:
                        weights(e + 1)
                    if i:
                        store_y(sp, i - 1)
                store_y(sp, len(jobs) - 1)
                sp.wait_ge(m["done"], 1)
                sp.dma_start(g.out.rearrange("(t p) d -> p t d", p=P), g.x_sb[:, :, :]).then_inc(m["stored"], 16)
                sp.wait_ge(m["stored"], 16)

            @block.gpsimd
            def _(pool):
                one = Chain(pool, m["pool_step"])
                nc.gpsimd.memset(zero[:, :], 0.0).then_inc(m["zero_made"], 1)
                one(pool.memset(power[:, :], -0.5))
                one(pool.memset(ones_b[:, :], 1.0))
                one(pool.memset(later[:, :], 1.0))
                one(pool.affine_select(out=later[:, :], in_=later[:, :], compare_op=ALU.is_gt, fill=0.0, base=0, pattern=[[1, P]],
                                       channel_multiplier=-1))
                one(pool.iota(iota_i[:, :], pattern=[[1, E]], base=0, channel_multiplier=0))
                one(pool.iota(base_i[:, :], pattern=[[CAP, E]], base=SLOTS0 - CAP, channel_multiplier=0))
                one(pool.memset(base_i[:, 0:1], 0))
                pool.wait_ge(m["stats_made"], 1)
                rstd_steps(nc, pool, one, mv, veps[:, :], power[:, :], rstd[:, :], m["rstd_made"])
                pool.wait_ge(m["zero_out"], 16 * ((SLOTS + P - 1) // P))
                pool.wait_ge(m["slots_made"], 1)
                for t in range(TT):
                    pool.indirect_dma_start(out=xs, out_offset=bass.IndirectOffsetOnAxis(ap=slot_u[:, t:t + 1], axis=0), in_=xn[:, t, :],
                                            in_offset=None).then_inc(m["scattered"], 16)
                pool.wait_ge(m["scattered"], 16 * TT)
                pool.wait_ge(m["y_out"], 16 * len(jobs))
                for t in range(TT):
                    pool.indirect_dma_start(out=got[:, t, :], out_offset=None, in_=ys,
                                            in_offset=bass.IndirectOffsetOnAxis(ap=slot_u[:, t:t + 1], axis=0)).then_inc(m["gathered"], 16)
                pool.wait_ge(m["gathered"], 16 * TT)

            @block.vector
            def _(dve):
                one = Chain(dve, m["dve_step"])
                tt_ = nc.vector.tensor_tensor
                layer_norm(nc, dve, one, lambda t: g.x_sb[:, t, :], TT, stats, mv, m["stats_made"], m["rstd_made"], rstd, xn, m["xn_made"], 1)
                dve.wait_ge(m["r_turned"], 1)
                nc.vector.tensor_copy(r_t[:, :, :].rearrange("p c e -> p (c e)"), ps[:, 4, 0:DC * E]).then_inc(m["r_kept"], 1)
                dve.wait_ge(m["logits_ready"], 1)
                one(nc.vector.tensor_copy(lg[:, :, :].rearrange("p t e -> p (t e)"), ps[:, 5, 0:TT * E]))
                one(nc.vector.tensor_reduce(mx[:, :], lg[:, :, :], axis=AX.X, op=ALU.max))
                wide = [P, TT, E]
                one(tt_(ex[:, :, :], lg[:, :, :], mx[:, :, None].to_broadcast(wide), ALU.subtract))
                nc.vector.tensor_scalar(pick[:, :, :], ex[:, :, :], 0.0, -float(E), ALU.is_ge, ALU.mult).then_inc(m["logits_kept"], 1)
                dve.wait_ge(m["logits_kept"], 1)
                one(nc.vector.tensor_copy(iota_e[:, :], iota_i[:, :]))
                one(nc.vector.tensor_copy(base[:, :], base_i[:, :]))
                one(tt_(pick[:, :, :], pick[:, :, :], iota_e[:, None, :].to_broadcast(wide), ALU.add))
                one(nc.vector.tensor_reduce(idx[:, :], pick[:, :, :], axis=AX.X, op=ALU.min))
                one(tt_(hot[:, :, :], pick[:, :, :], idx[:, :, None].to_broadcast(wide), ALU.is_equal))
                one(nc.vector.tensor_copy(hot_b[:, :, :], hot[:, :, :]))
                dve.wait_ge(m["exp_made"], 1)
                one(nc.vector.tensor_reduce(sm[:, :], lg[:, :, :], axis=AX.X, op=ALU.add))
                one(nc.vector.reciprocal(prob[:, :], sm[:, :]))
                nc.vector.tensor_copy(p_wide[:, :, :], prob[:, :, None].to_broadcast([P, TT, P])).then_inc(m["prob_wide"], 1)
                dve.wait_ge(m["p_kept"], 2)
                for t in range(TT):
                    pj = prob[:, t:t + 1]
                    if t:
                        nc.vector.tensor_scalar(before[:, t, 0:t * P], p_row[:, 0:t * P], pj, None, ALU.is_lt)
                    if t < TT - 1:
                        nc.vector.tensor_scalar(before[:, t, (t + 1) * P:], p_row[:, (t + 1) * P:], pj, None, ALU.is_le)
                    own = p_row[:, t * P:(t + 1) * P]
                    one(nc.vector.tensor_scalar(eqm[:, :], own, pj, None, ALU.is_equal))
                    one(tt_(eqm[:, :], eqm[:, :], later[:, :], ALU.mult))
                    ins = nc.vector.scalar_tensor_tensor(before[:, t, t * P:(t + 1) * P], own, pj, eqm[:, :], ALU.is_lt, ALU.add)
                    if t < TT - 1:
                        one(ins)
                ins.then_inc(m["before_made"], 1)
                dve.wait_ge(m["ranks_ready"], 1)
                one(tt_(tmp[:, :, :], ps[:, 6, 0:TT * E].rearrange("p (t e) -> p t e", e=E), hot[:, :, :], ALU.mult))
                one(nc.vector.tensor_reduce(rk[:, :], tmp[:, :, :], axis=AX.X, op=ALU.add))
                one(nc.vector.tensor_copy(cnt[:, :], ps[:, 6, TT * E:TT * E + E]))
                one(nc.vector.tensor_scalar(over_e[:, :], cnt[:, :], -float(CAP), 0.0, ALU.add, ALU.max))
                one(nc.vector.tensor_copy(pre[:, 0:2], cnt[:, 0:1].to_broadcast([P, 2])))
                for e in range(2, E):
                    one(tt_(pre[:, e:e + 1], pre[:, e - 1:e], over_e[:, e - 1:e], ALU.add))
                one(tt_(jump[:, :], pre[:, :], base[:, :], ALU.subtract))
                one(nc.vector.tensor_scalar(jump[:, :], jump[:, :], -float(CAP), None, ALU.add))
                one(nc.vector.memset(jump[:, 0:1], 0.0))
                one(tt_(tmp[:, :, :], hot[:, :, :], base[:, None, :].to_broadcast(wide), ALU.mult))
                one(nc.vector.tensor_reduce(sa[:, :], tmp[:, :, :], axis=AX.X, op=ALU.add))
                one(tt_(tmp[:, :, :], hot[:, :, :], jump[:, None, :].to_broadcast(wide), ALU.mult))
                one(nc.vector.tensor_reduce(sj[:, :], tmp[:, :, :], axis=AX.X, op=ALU.add))
                one(nc.vector.tensor_scalar(ov[:, :], rk[:, :], float(CAP), None, ALU.is_ge))
                one(tt_(ov[:, :], ov[:, :], sj[:, :], ALU.mult))
                one(tt_(slot[:, :], sa[:, :], rk[:, :], ALU.add))
                one(tt_(slot[:, :], slot[:, :], ov[:, :], ALU.add))
                nc.vector.tensor_copy(slot_u[:, :], slot[:, :]).then_inc(m["slots_made"], 1)
                for i, (e, s, rows, n) in enumerate(jobs):
                    dve.wait_ge(m["x_turned"], i + 1)
                    if i:
                        dve.wait_ge(m["h_ready"], i * FC)
                    for c in range(DC):
                        ins = nc.vector.tensor_copy(xs0_t[:, c, 0:rows * n], ps[:, c, 0:rows * n])
                    ins.then_inc(m["x_kept"], 1)
                    dve.wait_ge(m["y_turned"], i + 1)
                    if i:
                        dve.wait_ge(m["y_out"], 16 * i)
                    for c in range(n):
                        ins = nc.vector.tensor_copy(y_nat[0:rows, c, :], ps[0:rows, 6 + c // 2, (c % 2) * D:(c % 2 + 1) * D])
                    ins.then_inc(m["y_out_kept"], 1)
                dve.wait_ge(m["gathered"], 16 * TT)
                nc.vector.tensor_tensor(g.x_sb[:, :, :], g.x_sb[:, :, :], got[:, :, :], ALU.add).then_inc(m["done"], 1)

            @block.scalar
            def _(act):
                for c in range(DC):
                    for half in range(2):
                        act.wait_ge(m["turned"], c * 2 + half + 1)
                        nc.scalar.activation(xn_t[:, c, half * 512:(half + 1) * 512], ps[:, c * 2 + half, :], ACT.Copy).then_inc(m["turned_kept"], 1)
                act.wait_ge(m["logits_kept"], 1)
                nc.scalar.activation(lg[:, :, :], ex[:, :, :], ACT.Exp).then_inc(m["exp_made"], 1)
                for q in range(2):
                    act.wait_ge(m["p_turned"], q + 1)
                    nc.scalar.activation(p_row[:, q * 512:(q + 1) * 512], ps[:, 6 + q, :], ACT.Copy).then_inc(m["p_kept"], 1)
                for i, (e, s, rows, n) in enumerate(jobs):
                    w = rows * n
                    for f in range(FC):
                        act.wait_ge(m["h_ready"], i * FC + f + 1)
                        if i and f == 0:
                            act.wait_ge(m["y_ready"], i)
                        nc.scalar.activation(hid[:, f, 0:w], ps[:, 2 + f % 2, 0:w], ACT.Relu, bias=b1[:, e, f:f + 1]).then_inc(m["h_kept"], 1)
                    act.wait_ge(m["y_ready"], i + 1)
                    if i:
                        act.wait_ge(m["y_turned"], i)
                    for c in range(DC):
                        ins = nc.scalar.activation(y_t[:, c, 0:w], ps[:, 4 + c, 0:w], ACT.Identity, bias=b2[:, e, c:c + 1])
                    ins.then_inc(m["y_kept"], 1)

            @block.tensor
            def _(pe):
                mm, tr = nc.tensor.matmul, nc.tensor.transpose
                pe.wait_ge(m["small_in"], 16 * (1 + 2 * E))
                for c in range(DC):
                    ins = tr(ps[:, 4, c * E:(c + 1) * E], r_nat[:, c * P:(c + 1) * P], g.ident[0:E, 0:E])
                ins.then_inc(m["r_turned"], 1)
                pe.wait_ge(m["xn_made"], 1)
                for c in range(DC):
                    for half in range(2):
                        for t in range(4):
                            ins = tr(ps[:, c * 2 + half, t * P:(t + 1) * P], xn[:, half * 4 + t, c * P:(c + 1) * P], g.ident[:, :])
                        ins.then_inc(m["turned"], 1)
                pe.wait_ge(m["r_kept"], 1)
                pe.wait_ge(m["turned_kept"], 4)
                for t in range(TT):
                    for c in range(DC):
                        ins = mm(ps[:, 5, t * E:(t + 1) * E], xn_t[:, c, t * P:(t + 1) * P], r_t[:, c, :], start=c == 0, stop=c == DC - 1)
                ins.then_inc(m["logits_ready"], 1)
                pe.wait_ge(m["prob_wide"], 1)
                for q in range(2):
                    for t in range(4):
                        ins = tr(ps[:, 6 + q, t * P:(t + 1) * P], p_wide[:, q * 4 + t, :], g.ident[:, :])
                    ins.then_inc(m["p_turned"], 1)
                pe.wait_ge(m["before_made"], 1)
                for i in range(TT):
                    for j in range(TT):
                        mm(ps[:, 6, i * E:(i + 1) * E], before[:, j, i * P:(i + 1) * P], hot_b[:, j, :], start=j == 0, stop=j == TT - 1)
                for j in range(TT):
                    ins = mm(ps[:, 6, TT * E:TT * E + E], ones_b[:, :], hot_b[:, j, :], start=j == 0, stop=j == TT - 1)
                ins.then_inc(m["ranks_ready"], 1)
                for i, (e, s, rows, n) in enumerate(jobs):
                    w = rows * n
                    pe.wait_ge(m["x_in"], 16 * (i + 1))
                    if i == 0:
                        pe.wait_ge(m["slots_made"], 1)
                    for c in range(DC):
                        for q in range(n):
                            ins = tr(ps[:, c, q * rows:(q + 1) * rows], xs0[0:rows, q, c * P:(c + 1) * P], g.ident[0:rows, 0:rows])
                    ins.then_inc(m["x_turned"], 1)
                    pe.wait_ge(m["x_kept"], i + 1)
                    pe.wait_ge(m["w1_in"], 16 * (e + 1))
                    for f in range(FC):
                        if i * FC + f >= 2:
                            pe.wait_ge(m["h_kept"], i * FC + f - 1)
                        for c in range(DC):
                            ins = mm(ps[:, 2 + f % 2, 0:w], w1[:, e % 2, c, f * P:(f + 1) * P], xs0_t[:, c, 0:w], start=c == 0, stop=c == DC - 1)
                        ins.then_inc(m["h_ready"], 1)
                    pe.wait_ge(m["w2_in"], 16 * (e + 1))
                    pe.wait_ge(m["h_kept"], (i + 1) * FC)
                    if i:
                        pe.wait_ge(m["y_kept"], i)
                    for c in range(DC):
                        for f in range(FC):
                            ins = mm(ps[:, 4 + c, 0:w], w2[:, e % 2, f, c * P:(c + 1) * P], hid[:, f, 0:w], start=f == 0, stop=f == FC - 1)
                    ins.then_inc(m["y_ready"], 1)
                    if i + 1 == len(jobs) or jobs[i + 1][0] != e:
                        pe.wait_ge(m["y_ready"], i + 1)
                        pe.sem_inc(m["w_done"], 1)
                    pe.wait_ge(m["y_kept"], i + 1)
                    if i:
                        pe.wait_ge(m["y_out_kept"], i)
                    for q in range(n):
                        for c in range(DC):
                            ins = tr(ps[0:rows, 6 + q // 2, (q % 2) * D + c * P:(q % 2) * D + (c + 1) * P], y_t[:, c, q * rows:(q + 1) * rows],
                                     g.ident[:, :])
                    ins.then_inc(m["y_turned"], 1)

        clear_semaphores(nc, mine)


def program(nc, args, out):
    top = ExitStack()
    with top:
        g = Shared()
        (x, ctx_, g.xWq, g.xbq, g.xWk, g.xbk, g.xWv, g.xbv, g.xWo, g.xbo, g.dWq, g.dWk, g.dWv, g.dWb, g.lnw, g.lnb,
         g.router, g.W1, g.b1, g.W2, g.b2) = args
        g.x = x.rearrange("b s d -> (b s) d")
        g.ctx = ctx_.rearrange("b n d -> (b n) d")
        g.out = out.rearrange("b s d -> (b s) d")
        g.qq = nc.dram_tensor("q_parts", (HEADS, PARTS, HD, S), BF16, kind="Internal").ap()
        g.kk = nc.dram_tensor("k_parts", (HEADS, PARTS, HD, N), BF16, kind="Internal").ap()
        g.vv = nc.dram_tensor("v_heads", (HEADS, P, N // P * HD), F32, kind="Internal").ap()

        g.xs = nc.dram_tensor("slot_rows", (TOK + 7 * 160, D), F32, kind="Internal").ap()
        g.ys = nc.dram_tensor("slot_outputs", (TOK + 7 * 160, D), F32, kind="Internal").ap()

        def sb(n, s, d=F32):
            return top.enter_context(nc.sbuf_tensor(n, s, d))
        g.x_sb = sb("x_sb", [P, TT, D])
        g.ident = sb("ident", [P, P])
        g.ident_b = sb("ident_b", [P, P], BF16)
        g.minus_b = sb("minus_b", [P, P], BF16)
        g.flags = sb("flags", [P, HEADS, ST])
        g.u = sb("u", [P, HEADS, ST, HD + 1])
        with ExitStack() as early:
            def sb(n, s, d=F32):
                return early.enter_context(nc.sbuf_tensor(n, s, d))
            g.bq, g.bk, g.bv_bc = sb("bq", [P, DC]), sb("bk", [P, DC]), sb("bv_bc", [P, D])
            g.wk_t, g.wv_t = sb("wk_t", [P, DC, D]), sb("wv_t", [P, DC, D])
            stage_setup(nc, g)
            stage_keys(nc, g)
        stage_attention(nc, g)
        stage_exact(nc, g)
        stage_out(nc, g)
        stage_delta(nc, g)
        stage_experts(nc, g)


_INS = ['x', 'ctx_1024', 'L0_xattn_Wq', 'L0_xattn_bq', 'L0_xattn_Wk', 'L0_xattn_bk', 'L0_xattn_Wv', 'L0_xattn_bv',
        'L0_xattn_Wo', 'L0_xattn_bo', 'L0_attn_Wq', 'L0_attn_Wk', 'L0_attn_Wv', 'L0_attn_Wb', 'L0_attn_ln_w',
        'L0_attn_ln_b', 'L0_ffn_router_w', 'L0_ffn_W1', 'L0_ffn_b1', 'L0_ffn_W2', 'L0_ffn_b2']


def kernel(**inputs):
    import numpy as _np
    import concourse.bacc as _bacc
    from concourse import mybir as _mybir
    from concourse.bass_utils import run_bass_kernel_spmd as _run

    nc = _bacc.Bacc("TRN2", target_bir_lowering=False, num_devices=1)
    arrays, args = {}, []
    for name in _INS:
        a = _np.ascontiguousarray(inputs[name])
        arrays[f"in_{name}"] = a
        args.append(nc.dram_tensor(f"in_{name}", a.shape, _mybir.dt.from_np(a.dtype), kind="ExternalInput").ap())
    out = nc.dram_tensor("out_x", (4, 256, 256), _mybir.dt.float32, kind="ExternalOutput").ap()
    program(nc, args, out)
    r = _run(nc, [arrays], core_ids=[0])
    return r.results[0]["out_x"]
```

```python
import numpy as np
import concourse.bass as bass
from concourse import mybir
from contextlib import ExitStack

F32 = mybir.dt.float32
BF16 = mybir.dt.bfloat16
I32 = mybir.dt.int32
ACT = mybir.ActivationFunctionType
ALU = mybir.AluOpType
AX = mybir.AxisListType

P = 128
B, S, D = 4, 256, 256
N = 4096
H, HD = 16, 16
TOPK = 32
HEADS = B * H
TOK = B * S
TT = TOK // P
DC = D // P
ST = S // P
EPS_LN = 1e-5
NEG = -3.0e38
BIG = 1.0e30

PARTS = 3
KROWS = 6 * HD
TROWS = PARTS
CHUNK = 128
NCH = N // CHUNK
BANK = 512
SB_N = N // BANK
KEYS_T = 512
NKB = B * N // KEYS_T
UNIT = 4
UNITS = N // P // UNIT
VW = 32
FIRST = 3 * NCH
REST = 5 * NCH
CANDS = 8 + FIRST + REST


class Shared:
    pass


class Chain:

    def __init__(self, eng, sem):
        self.eng, self.sem, self.n = eng, sem, 0

    def __call__(self, ins):
        self.n += 1
        ins.then_inc(self.sem, 1)
        self.eng.wait_ge(self.sem, self.n)


class Steps(Chain):

    def __call__(self, ins):
        self.n += 1
        ins.then_inc(self.sem, 1)

    def join(self):
        if self.n:
            self.eng.wait_ge(self.sem, self.n)


def clear_semaphores(nc, sems):
    with nc.Block() as block:
        @block.sync
        def _(sp):
            for s in sems:
                sp.sem_clear(s)


def ident_step(pool, mat, one, sem, fill=1.0):
    one(pool.memset(mat, 0.0))
    one(pool.affine_select(out=mat, in_=mat, compare_op=ALU.not_equal, fill=fill, base=0,
                           pattern=[[-1, P]], channel_multiplier=1))


def stage_setup(nc, g):
    ctx = ExitStack()
    with ctx:
        def sb(n, s, d=F32):
            return ctx.enter_context(nc.sbuf_tensor(n, s, d))

        mine = []

        def sem(n):
            mine.append(ctx.enter_context(nc.semaphore(n)))
            return mine[-1]

        w_nat = sb("w_nat", [P, 3, DC, D])
        wq_t = sb("wq_t", [P, DC, D])
        bq4 = sb("bq4", [P, DC])
        stats = sb("stats", [P, TT, 6])
        mv = sb("mv", [P, TT, 2])
        veps = sb("veps", [P, TT])
        minus_half = sb("minus_half", [P, TT])
        rstd = sb("rstd", [P, TT])
        xn = sb("xn", [P, TT, D])
        xn_t = sb("xn_t", [P, DC, TOK])
        ps = ctx.enter_context(nc.psum_tensor("ps_setup", [P, 8, BANK], F32))

        x_in, w_in, small_in = sem("x_in"), sem("w_in"), sem("small_in")
        pool_step, dve_step = sem("setup_pool_step"), sem("setup_dve_step")
        ident_made, stats_made, rstd_made, xn_made = sem("ident_made"), sem("stats_made"), sem("rstd_made"), sem("xn_made")
        w_turned, w_kept, x_turned, x_kept = sem("w_turned"), sem("w_kept"), sem("x_turned"), sem("x_kept")
        q_ready, q_kept = sem("q_ready"), sem("q_kept")
        bq_scaled = sem("bq_scaled")

        with nc.Block() as block:
            @block.sync
            def _(sp):
                sp.dma_start(g.x_sb[:, :, :], g.x.rearrange("(t p) d -> p t d", p=P)).then_inc(x_in, 16)
                for i, w in enumerate((g.xWq, g.xWk, g.xWv)):
                    sp.dma_start(w_nat[:, i], w.rearrange("(c p) d -> p c d", p=P)).then_inc(w_in, 16)
                with nc.allow_non_contiguous_dma("one column of a vector to each partition"):
                    sp.dma_start(g.bq[:, :], g.xbq.rearrange("(c p) -> p c", p=P)).then_inc(small_in, 16)
                    sp.dma_start(g.bk[:, :], g.xbk.rearrange("(c p) -> p c", p=P)).then_inc(small_in, 16)
                sp.dma_start(g.bv_bc[:, :], g.xbv[None, :].to_broadcast([P, D])).then_inc(small_in, 16)

            @block.gpsimd
            def _(pool):
                one = Chain(pool, pool_step)
                ident_step(pool, g.ident[:, :], one, pool_step)
                ident_step(pool, g.ident_b[:, :], one, pool_step)
                ident_step(pool, g.minus_b[:, :], one, pool_step, fill=-1.0)
                one(pool.memset(minus_half[:, :], -0.5))
                pool.memset(g.flags[:, :, :], 0.0).then_inc(ident_made, 1)
                pool.wait_ge(stats_made, 1)
                one(nc.gpsimd.tensor_scalar(veps[:, :], mv[:, :, 1], EPS_LN, None, ALU.add))
                nc.gpsimd.tensor_tensor(rstd[:, :], veps[:, :], minus_half[:, :], ALU.pow).then_inc(rstd_made, 1)

            @block.vector
            def _(dve):
                one = Chain(dve, dve_step)
                dve.wait_ge(small_in, 48)
                nc.vector.tensor_scalar(bq4[:, :], g.bq[:, :], 0.25, None, ALU.mult).then_inc(bq_scaled, 1)
                dve.wait_ge(x_in, 16)
                for t in range(TT):
                    one(nc.vector.bn_stats(stats[:, t, :], g.x_sb[:, t, :]))
                    ins = nc.vector.bn_aggr(mv[:, t, :], stats[:, t, :])
                    if t == TT - 1:
                        ins.then_inc(stats_made, 1)
                dve.wait_ge(stats_made, 1)
                dve.wait_ge(rstd_made, 1)
                for t in range(TT):
                    ins = nc.vector.tensor_scalar(xn[:, t, :], g.x_sb[:, t, :], mv[:, t, 0:1], rstd[:, t:t + 1],
                                                  ALU.subtract, ALU.mult)
                ins.then_inc(xn_made, 1)

            @block.tensor
            def _(pe):
                pe.wait_ge(ident_made, 1)
                pe.wait_ge(w_in, 48)
                for i in range(3):
                    for c in range(DC):
                        for e in range(DC):
                            ins = nc.tensor.transpose(ps[:, i, c * D + e * P:c * D + (e + 1) * P],
                                                      w_nat[:, i, e, c * P:(c + 1) * P], g.ident[:, :])
                    ins.then_inc(w_turned, 1)
                pe.wait_ge(xn_made, 1)
                for c in range(DC):
                    for half in range(2):
                        for t in range(4):
                            ins = nc.tensor.transpose(ps[:, 4 + c * 2 + half, t * P:(t + 1) * P],
                                                      xn[:, half * 4 + t, c * P:(c + 1) * P], g.ident[:, :])
                        ins.then_inc(x_turned, 1)
                pe.wait_ge(w_kept, 3)
                pe.wait_ge(x_kept, 4)
                for m in range(DC):
                    for half in range(2):
                        for c in range(DC):
                            ins = nc.tensor.matmul(ps[:, m * 2 + half, :], wq_t[:, c, m * P:(m + 1) * P],
                                                   xn_t[:, c, half * 512:(half + 1) * 512], start=c == 0, stop=c == DC - 1)
                        ins.then_inc(q_ready, 1)

            @block.scalar
            def _(act):
                for i, dst in enumerate((wq_t, g.wk_t, g.wv_t)):
                    act.wait_ge(w_turned, i + 1)
                    nc.scalar.activation(dst[:, :, :].rearrange("p c d -> p (c d)"), ps[:, i, :], ACT.Copy).then_inc(w_kept, 1)
                for c in range(DC):
                    for half in range(2):
                        act.wait_ge(x_turned, c * 2 + half + 1)
                        nc.scalar.activation(xn_t[:, c, half * 512:(half + 1) * 512], ps[:, 4 + c * 2 + half, :],
                                             ACT.Copy).then_inc(x_kept, 1)
                act.wait_ge(bq_scaled, 1)
                for m in range(DC):
                    for half in range(2):
                        act.wait_ge(q_ready, m * 2 + half + 1)
                        nc.scalar.activation(g.q32[:, m, half * 512:(half + 1) * 512], ps[:, m * 2 + half, :],
                                             ACT.Identity, bias=bq4[:, m:m + 1], scale=0.25).then_inc(q_kept, 1)

        clear_semaphores(nc, mine)


def split3(nc, dve, one, full, res, parts, done):
    nc.vector.tensor_copy(parts[0], full).then_inc(done, 1)
    dve.wait_ge(done, 1)
    one(nc.vector.tensor_tensor(res, full, parts[0], ALU.subtract))
    nc.vector.tensor_copy(parts[1], res).then_inc(done, 1)
    dve.wait_ge(done, 2)
    nc.vector.tensor_tensor(parts[2], res, parts[1], ALU.subtract).then_inc(done, 1)


def stage_keys(nc, g):
    ctx = ExitStack()
    with ctx:
        def sb(n, s, d=F32):
            return ctx.enter_context(nc.sbuf_tensor(n, s, d))

        mine = []

        def sem(n):
            mine.append(ctx.enter_context(nc.semaphore(n)))
            return mine[-1]

        c_in = sb("c_in", [P, 2, 4, D])
        c_t = sb("c_t", [P, 2, DC, KEYS_T])
        k32 = sb("k32", [P, 2, DC, KEYS_T])
        kres = sb("kres", [P, DC, KEYS_T])
        kp = sb("kp", [P, 2, PARTS, DC, KEYS_T], BF16)
        v_sb = sb("v_sb", [P, 2, H, 4, HD])
        qres = sb("qres", [P, DC, TOK])
        qp = sb("qp", [P, PARTS, DC, TOK], BF16)
        ps_t = ctx.enter_context(nc.psum_tensor("ps_t", [P, DC, KEYS_T], F32))
        ps_k = ctx.enter_context(nc.psum_tensor("ps_k", [P, DC, KEYS_T], F32))
        ps_v = ctx.enter_context(nc.psum_tensor("ps_v", [P, 4, D], F32))
        load_seen = sem("load_seen")
        q_step, q_split, q_out = sem("q_step"), sem("q_split"), sem("q_out")
        ctx_in, turned, turned_kept = [sem("ctx_in0"), sem("ctx_in1")], sem("ctx_turned"), sem("ctx_turned_kept")
        k_ready, v_ready, k_kept = sem("k_ready"), sem("v_ready"), sem("k_kept")
        k1_made, kres_made, k2_made, k_split = sem("k1_made"), sem("kres_made"), sem("k2_made"), sem("k_split")
        v_kept, kv_out = sem("v_kept"), [sem("kv_out0"), sem("kv_out1")]
        OUTS = 16 * (PARTS * DC + 1)

        def steps(eng, step):
            step(0, 0, 0, True, False)
            step(1, 1, 0, True, False)
            with eng.Fori(1, NKB // 2 - 1) as k:
                step(k * 2, 0, k, False, False)
                step(k * 2 + 1, 1, k, False, False)
            k = NKB // 2 - 1
            step(k * 2, 0, k, False, False)
            step(k * 2 + 1, 1, k, False, True)

        with nc.Block() as block:
            @block.sync
            def _(sp):
                sp.wait_ge(q_split, PARTS)
                for j in range(PARTS):
                    for m in range(DC):
                        for b in range(B):
                            sp.dma_start(
                                g.qq[b * H + m * 8:b * H + (m + 1) * 8, j],
                                qp[:, j, m, b * S:(b + 1) * S]).then_inc(q_out, 16)

                def store(b, tb, t, j):
                    sp.wait_ge(k_split, t + 1)
                    for q in range(PARTS):
                        for m in range(DC):
                            sp.dma_start(g.kk[bass.ds(b * H + m * 8, 8), q, :, bass.ds(tb * KEYS_T, KEYS_T)],
                                         kp[:, j, q, m, :]).then_inc(kv_out[j], 16)
                    sp.wait_ge(v_kept, t + 1)
                    sp.dma_start(g.vv[bass.ds(b * H, H), :, bass.ds(tb * 4 * HD, 4 * HD)].rearrange("h p c -> p h c"),
                                 v_sb[:, j].rearrange("p h c d -> p h (c d)")).then_inc(kv_out[j], 16)

                with sp.Fori(0, B) as b:
                    with sp.Fori(0, N // KEYS_T // 2) as k:
                        for j in range(2):
                            store(b, k * 2 + j, b * (N // KEYS_T) + k * 2 + j, j)
                sp.wait_ge(q_out, 16 * PARTS * DC * B)
                sp.wait_ge(kv_out[0], OUTS * NKB // 2)
                sp.wait_ge(kv_out[1], OUTS * NKB // 2)

            @block.gpsimd
            def _(pool):
                def load(t, j):
                    pool.dma_start(c_in[:, j], g.ctx[bass.ds(t * KEYS_T, KEYS_T), :].rearrange("(c p) d -> p c d", p=P)).then_inc(ctx_in[j], 16)

                load(0, 0)
                load(1, 1)
                with pool.Fori(1, NKB // 2) as k:
                    for j in range(2):
                        pool.wait_ge(turned, k * 2 + j - 1)
                        pool.sem_inc(load_seen, 1)
                        load(k * 2 + j, j)

            @block.tensor
            def _(pe):
                def turn(t, j, k, first):
                    pe.wait_ge(ctx_in[j], 16 * (k + 1))
                    if not first:
                        pe.wait_ge(turned_kept, t)
                    for c in range(DC):
                        for n in range(4):
                            ins = nc.tensor.transpose(ps_t[:, c, n * P:(n + 1) * P], c_in[:, j, n, c * P:(c + 1) * P],
                                                      g.ident[:, :])
                    ins.then_inc(turned, 1)

                turn(0, 0, 0, True)

                def step(t, j, k, first, last):
                    if not last:
                        turn(t + 1, 1 - j, k + j, False)
                    pe.wait_ge(turned_kept, t + 1)
                    if not (first and j == 0):
                        pe.wait_ge(k_kept, t)
                    for m in range(DC):
                        for c in range(DC):
                            ins = nc.tensor.matmul(ps_k[:, m, :], g.wk_t[:, c, m * P:(m + 1) * P], c_t[:, j, c, :],
                                                   start=c == 0, stop=c == DC - 1)
                    ins.then_inc(k_ready, 1)
                    if not (first and j == 0):
                        pe.wait_ge(v_kept, t)
                    for n in range(4):
                        for c in range(DC):
                            ins = nc.tensor.matmul(ps_v[:, n, :], c_t[:, j, c, n * P:(n + 1) * P], g.wv_t[:, c, :],
                                                   start=c == 0, stop=c == DC - 1)
                    ins.then_inc(v_ready, 1)
                steps(pe, step)

            @block.scalar
            def _(act):
                def step(t, j, k, first, last):
                    if not first:
                        act.wait_ge(v_ready, t - 1)
                    act.wait_ge(turned, t + 1)
                    nc.scalar.activation(c_t[:, j].rearrange("p c n -> p (c n)"), ps_t[:, :, :].rearrange("p c n -> p (c n)"),
                                         ACT.Copy).then_inc(turned_kept, 1)
                    act.wait_ge(k_ready, t + 1)
                    if not first:
                        act.wait_ge(k_split, t - 1)
                    for m in range(DC):
                        ins = nc.scalar.activation(k32[:, j, m, :], ps_k[:, m, :], ACT.Identity, bias=g.bk[:, m:m + 1])
                    ins.then_inc(k_kept, 1)
                steps(act, step)

            @block.vector
            def _(dve):
                split3(nc, dve, Chain(dve, q_step), g.q32[:, :, :], qres[:, :, :], [qp[:, p] for p in range(PARTS)], q_split)

                def step(t, j, k, first, last):
                    dve.wait_ge(k_kept, t + 1)
                    if not first:
                        dve.wait_ge(kv_out[j], k * OUTS)
                    full = k32[:, j]
                    nc.vector.tensor_copy(kp[:, j, 0], full).then_inc(k1_made, 1)
                    dve.wait_ge(k1_made, t + 1)
                    nc.vector.tensor_tensor(kres[:, :, :], full, kp[:, j, 0], ALU.subtract).then_inc(kres_made, 1)
                    dve.wait_ge(kres_made, t + 1)
                    nc.vector.tensor_copy(kp[:, j, 1], kres[:, :, :]).then_inc(k2_made, 1)
                    dve.wait_ge(k2_made, t + 1)
                    nc.vector.tensor_tensor(kp[:, j, 2], kres[:, :, :], kp[:, j, 1], ALU.subtract).then_inc(k_split, 1)
                    dve.wait_ge(v_ready, t + 1)
                    for n in range(4):
                        ins = nc.vector.tensor_tensor(v_sb[:, j, :, n, :], ps_v[:, n, :].rearrange("p (h d) -> p h d", d=HD),
                                                      g.bv_bc[:, :].rearrange("p (h d) -> p h d", d=HD), ALU.add)
                    ins.then_inc(v_kept, 1)
                    dve.wait_ge(k_split, t + 1)
                steps(dve, step)

        clear_semaphores(nc, mine)


def stage_attention(nc, g):
    ctx = ExitStack()
    with ctx:
        def sb(n, s, d=F32):
            return ctx.enter_context(nc.sbuf_tensor(n, s, d))

        mine = []

        def sem(n):
            mine.append(ctx.enter_context(nc.semaphore(n)))
            return mine[-1]

        SL = 3
        TIE = 2.0 ** -21
        kop = sb("kop", [P, SL, N], BF16)
        qop = sb("qop", [P, SL, S], BF16)
        v_in = sb("v_in", [P, SL, N // P, HD])
        vs = sb("vs", [P, SL, N // P, VW])
        cand = sb("cand", [P, SL, ST, CANDS])
        work = sb("work", [P, ST, 8 + FIRST])
        top = sb("top", [P, SL, ST, 4, 8])
        mag = sb("mag", [P, ST])
        thr = sb("thr", [P, SL, ST])
        thr_res = sb("thr_res", [P, ST])
        thr_p = sb("thr_p", [P, ST, P], BF16)
        pen = sb("pen", [P, 2, UNIT * S], BF16)
        wgt = sb("wgt", [P, 4, UNIT * S])
        o_sb = sb("o_sb", [P, S])
        sel = sb("sel", [P, HD + 1])
        marks = sb("marks", [P, 2, ST, 8 + FIRST + NCH])
        TREE = (68, 34, 17, 16, 8, 4, 2, 1)
        sums = sb("sums", [P, 2 * ST, 68])
        cnt = sb("cnt", [P, 6, ST])
        ring = ctx.enter_context(nc.psum_tensor("ring", [P, 3, BANK], F32))
        d_ps = ctx.enter_context(nc.psum_tensor("d_ps", [P, 2, UNIT * S], F32))
        o_ps = ctx.enter_context(nc.psum_tensor("o_ps", [P, S], F32))

        k_in = [sem(f"k_in{s}") for s in range(SL)]
        q_in = [sem(f"q_in{s}") for s in range(SL)]
        v_loaded = [sem(f"v_loaded{s}") for s in range(SL)]
        consts, pool_step = sem("att_consts"), sem("att_pool_step")
        v_placed, flag_step, flagged, pool_seen = sem("v_placed"), sem("flag_step"), sem("flagged"), sem("pool_seen")
        s_ready = [sem(f"s_ready{s}") for s in range(SL)]
        s_used, seen = sem("s_used"), sem("s_seen")
        dve_step, thr_ready, thr_turned, thr_kept = sem("att_dve_step"), sem("thr_ready"), sem("thr_turned"), sem("thr_kept")
        d_ready, pen_ready, pen_added, w_ready, w_used = sem("d_ready"), sem("pen_ready"), sem("pen_added"), sem("w_ready"), sem("w_used")
        o_kept, u_ready, u_kept = sem("o_kept"), sem("u_ready"), sem("u_kept")


        def steps(eng, step):
            for i in range(SL):
                step(i, i, 0, i)
            with eng.Fori(1, HEADS // SL) as k:
                for j in range(SL):
                    step(k * SL + j, j, k, None)
            for i in range(HEADS // SL * SL, HEADS + 3):
                step(i, i % SL, i // SL, i)

        def has_head(i, back=0):
            return i is None or 0 <= i - back < HEADS

        def pair_of(p):
            return (2, 4 + 2 * p) if p < 2 else (1, 2 * (p - 2))

        order = [("s", 0), ("s", 1), ("u", 0)] + [("s", s) for s in range(2, 7)] + [("t", 0)] + [("s", s) for s in range(7, 16)]
        place = {use: n for n, use in enumerate(order)}

        with nc.Block() as block:
            @block.sync
            def _(sp):
                def step(n, j, k, i):
                    if not has_head(i):
                        return
                    if i is None or i >= SL:
                        sp.wait_ge(d_ready, (n - 2) * UNITS)
                    sp.dma_start(kop[0:3 * HD, j, :], g.kk[bass.ds(n, 1), 0:3].rearrange("o q r n -> (o q r) n")).then_inc(k_in[j], 16)
                    sp.dma_start(kop[3 * HD:5 * HD, j, :], g.kk[bass.ds(n, 1), 0:2].rearrange("o q r n -> (o q r) n")).then_inc(k_in[j], 16)
                    sp.dma_start(kop[5 * HD:6 * HD, j, :], g.kk[bass.ds(n, 1), 0:1].rearrange("o q r n -> (o q r) n")).then_inc(k_in[j], 16)
                    for row, (q, times) in zip((0, 1, 2, 3, 4, 5), ((0, 1), (0, 1), (0, 1), (1, 1), (1, 1), (2, 1))):
                        sp.dma_start(qop[row * HD:(row + 1) * HD, j, :],
                                     g.qq[bass.ds(n, 1), q:q + 1].rearrange("o q r n -> (o q r) n")).then_inc(q_in[j], 16)
                    if i is None or i >= SL:
                        sp.wait_ge(v_placed, n - 2)
                    sp.dma_start(v_in[:, j], g.vv[bass.ds(n, 1)].rearrange("o p (c d) -> (o p) c d", d=HD)).then_inc(v_loaded[j], 16)
                steps(sp, step)

            @block.gpsimd
            def _(pool):
                one = Chain(pool, pool_step)
                one(pool.memset(vs[:, :, :, :], 0.0))
                one(pool.memset(vs[:, :, :, HD:HD + 1], 1.0))
                one(pool.memset(kop[96:P, :, :], -1.0))
                one(pool.memset(thr_p[:, :, :], 0.0))
                one(pool.memset(marks[:, :, :, :], 0.0))
                one(pool.memset(sel[:, :], 0.0))
                for q in range(4):
                    one(pool.affine_select(out=sel[:, :], in_=sel[:, :], compare_op=ALU.not_equal, fill=1.0,
                                           base=-32 * q, pattern=[[-1, HD + 1]], channel_multiplier=1))
                pool.memset(cnt[:, :, :], 0.0).then_inc(consts, 1)
                pool.wait_ge(consts, 1)

                def step(n, j, k, i):
                    def one(ins, c):
                        ins.then_inc(flag_step, 1)
                        pool.wait_ge(flag_step, c)

                    if not has_head(i):
                        return
                    pool.wait_ge(v_loaded[j], 16 * (k + 1))
                    if i is None or i >= SL:
                        pool.wait_ge(w_used, (n - 2) * UNITS)
                    pool.sem_inc(pool_seen, 1)
                    nc.gpsimd.tensor_copy(vs[:, j, :, 0:HD], v_in[:, j]).then_inc(v_placed, 1)
                    pool.wait_ge(thr_ready, n + 1)
                    pool.sem_inc(pool_seen, 1)
                    pool.sem_clear(flag_step)
                    for t in range(ST):
                        nc.gpsimd.tensor_scalar(marks[:, 0, t, 0:8 + FIRST], cand[:, j, t, 0:8 + FIRST], thr[:, j, t:t + 1], None, ALU.is_ge)
                        nc.gpsimd.tensor_scalar(marks[:, 0, t, 8 + FIRST:], cand[:, j, t, CANDS - NCH:], thr[:, j, t:t + 1], 64.0,
                                                ALU.is_ge, ALU.mult)
                        ins = nc.gpsimd.tensor_scalar(marks[:, 1, t, 0:8 + FIRST], cand[:, j, t, 0:8 + FIRST], top[:, j, t, 3, 7:8],
                                                      None, ALU.is_ge)
                    one(ins, 1)
                    src, c = marks[:, :, :, :].rearrange("p k t c -> p (k t) c"), 2
                    for width in TREE:
                        dst = sums[:, :, 0:width]
                        if width == 16:
                            dst, width = sums[:, :, 0:1], 1
                            one(nc.gpsimd.tensor_tensor(dst, src[:, :, 0:1], src[:, :, 16:17], ALU.add), c)
                        else:
                            one(nc.gpsimd.tensor_tensor(dst, src[:, :, 0:width], src[:, :, width:2 * width], ALU.add), c)
                        src, c = sums, c + 1
                    nc.gpsimd.tensor_scalar(cnt[:, 0, :], sums[:, 0:ST, 0], 33.5, None, ALU.is_ge)
                    nc.gpsimd.tensor_scalar(cnt[:, 1, :], sums[:, ST:2 * ST, 0], 32.5, None, ALU.is_ge)
                    nc.gpsimd.tensor_tensor(cnt[:, 2, :], cand[:, j, :, 7], thr[:, j, :], ALU.subtract)
                    one(nc.gpsimd.tensor_tensor(cnt[:, 3, :], top[:, j, :, 0, 0], thr[:, j, :], ALU.subtract), c)
                    nc.gpsimd.tensor_scalar(cnt[:, 2, :], cnt[:, 2, :], 0.0, None, ALU.is_ge)
                    nc.gpsimd.tensor_scalar(cnt[:, 3, :], cnt[:, 3, :], 60.0, None, ALU.is_ge)
                    one(nc.gpsimd.tensor_tensor(cnt[:, 0, :], cnt[:, 0, :], cnt[:, 1, :], ALU.add), c + 1)
                    one(nc.gpsimd.tensor_tensor(cnt[:, 2, :], cnt[:, 2, :], cnt[:, 3, :], ALU.add), c + 2)
                    nc.gpsimd.tensor_tensor(g.flags[:, bass.ds(n, 1), :].rearrange("p o t -> p (o t)"), cnt[:, 0, :], cnt[:, 2, :],
                                            ALU.add).then_inc(flagged, 1)
                    pool.wait_ge(flagged, n + 1)
                    pool.sem_inc(pool_seen, 1)
                steps(pool, step)

            @block.vector
            def _(dve):
                dve.wait_ge(consts, 1)

                def refine(one, r, j, t):
                    row = cand[:, j, t, :]
                    one.join()
                    if r == 0:
                        one(nc.vector.max(row[:, 0:8], row[:, 8 + FIRST:CANDS]))
                    elif r % 2:
                        one(nc.vector.max(top[:, j, t, r // 2, :], row[:, 0:8 + FIRST] if r == 1 else work[:, t, :]))
                    else:
                        one(nc.vector.match_replace(work[:, t, :], top[:, j, t, r // 2 - 1, :],
                                                    row[:, 0:8 + FIRST] if r == 2 else work[:, t, :], NEG))

                def threshold(one, r, n, j, i):
                    v1, v32 = top[:, j, :, 0, 0], top[:, j, :, 3, 7]
                    one.join()
                    if r == 0:
                        one(nc.vector.scalar_tensor_tensor(mag[:, :], v32, -1.0, v1, ALU.mult, ALU.max))
                    elif r == 1:
                        one(nc.vector.scalar_tensor_tensor(thr[:, j, :], mag[:, :], -TIE, v32, ALU.mult, ALU.add))
                    elif r == 2:
                        if has_head(i, 2):
                            dve.wait_ge(thr_turned, n - 1)
                        one(nc.vector.tensor_copy(thr_p[:, :, 96], thr[:, j, :]))
                    elif r == 3:
                        one(nc.vector.tensor_tensor(thr_res[:, :], thr[:, j, :], thr_p[:, :, 96], ALU.subtract))
                    elif r == 4:
                        one(nc.vector.tensor_copy(thr_p[:, :, 97], thr_res[:, :]))
                    else:
                        nc.vector.tensor_tensor(thr_p[:, :, 98], thr_res[:, :], thr_p[:, :, 97], ALU.subtract).then_inc(thr_ready, 1)

                def step(n, j, k, i):
                    if not has_head(i) and not has_head(i, 1):
                        return
                    if has_head(i, 3) and has_head(i):
                        dve.wait_ge(flagged, n - 2)
                        dve.sem_inc(seen, 1)
                    one = Steps(dve, dve_step)
                    before = (j - 1) % SL
                    for t in range(ST):
                        for s in range(SB_N):
                            if has_head(i):
                                dve.wait_ge(s_ready[j], t * SB_N + s + 1)
                            for c in range(BANK // CHUNK):
                                at = 8 + s * (BANK // CHUNK) + c
                                if has_head(i):
                                    ins = nc.vector.max(cand[:, j, t, at:at + 7 * NCH + 1:NCH],
                                                        ring[:, place["s", t * SB_N + s] % 3, c * CHUNK:(c + 1) * CHUNK])
                                    if c == BANK // CHUNK - 1:
                                        ins.then_inc(s_used, 1)
                                r = s * (BANK // CHUNK) + c
                                if t == 0 and has_head(i, 1):
                                    if r < 8:
                                        refine(one, r, before, 1)
                                    elif r < 14:
                                        threshold(one, r - 8, n, before, i)
                                if t == 1 and has_head(i) and r < 8:
                                    refine(one, r, j, 0)
                        if has_head(i):
                            dve.wait_ge(s_used, n * (ST * SB_N) + (t + 1) * SB_N)
                            dve.sem_inc(seen, 1)
                    one.join()
                    dve.sem_clear(dve_step)
                    if has_head(i):
                        dve.sem_clear(s_ready[j])
                steps(dve, step)

            @block.tensor
            def _(pe):
                pe.wait_ge(consts, 1)

                def step(n, j, k, i):
                    def ring_free(use):
                        if i is not None and i >= HEADS:
                            pe.wait_ge(s_used, HEADS * ST * SB_N)
                            pe.wait_ge(thr_kept, min(HEADS, n - 1))
                            pe.wait_ge(u_kept, n - 3 if use[0] == "u" else n - 2)
                            return
                        at = place[use] - 3
                        back = 0 if at >= 0 else 1
                        kind, s = order[at % len(order)]
                        if kind == "s":
                            if has_head(i, back):
                                pe.wait_ge(s_used, (n - back) * (ST * SB_N) + s + 1)
                        elif kind == "t":
                            if has_head(i, back + 1):
                                pe.wait_ge(thr_kept, n - back)
                        elif has_head(i, back + 3):
                            pe.wait_ge(u_kept, n - back - 2)

                    def score(s):
                        if not has_head(i):
                            return
                        if s == 0:
                            pe.wait_ge(k_in[j], 48 * (k + 1))
                            pe.wait_ge(q_in[j], 96 * (k + 1))
                        ring_free(("s", s))
                        t, c = divmod(s, SB_N)
                        nc.tensor.matmul(ring[:, place["s", s] % 3, :], qop[0:KROWS, j, t * P:(t + 1) * P],
                                         kop[0:KROWS, j, c * BANK:(c + 1) * BANK], start=True, stop=True).then_inc(s_ready[j], 1)

                    def turn():
                        if not has_head(i, 1):
                            return
                        pe.wait_ge(thr_ready, n)
                        ring_free(("t", 0))
                        for t in range(ST):
                            ins = nc.tensor.matmul(ring[:, place["t", 0] % 3, t * P:(t + 1) * P], thr_p[:, t, :], g.ident_b[:, :],
                                                   start=True, stop=True)
                        ins.then_inc(thr_turned, 1)

                    def gather():
                        if not has_head(i, 3):
                            return
                        pe.wait_ge(o_kept, n - 2)
                        ring_free(("u", 0))
                        for t in range(ST):
                            ins = nc.tensor.matmul(ring[:, place["u", 0] % 3, t * (HD + 1):(t + 1) * (HD + 1)],
                                                   o_sb[:, t * P:(t + 1) * P], sel[:, :], start=True, stop=True)
                        ins.then_inc(u_ready, 1)

                    def differ(back, u):
                        if not has_head(i, back):
                            return
                        sl = (j - back) % SL
                        unit = (n - back) * UNITS + u
                        if u == 0:
                            pe.wait_ge(thr_kept, n - back + 1)
                        if u >= 2 or has_head(i, back + 1):
                            pe.wait_ge(w_ready, unit - 1)
                        for c in range(UNIT):
                            at = (u * UNIT + c) * P
                            ins = nc.tensor.matmul(d_ps[:, u % 2, c * S:(c + 1) * S], kop[0:KROWS + TROWS, sl, at:at + P],
                                             qop[0:KROWS + TROWS, sl, :], start=c * S % BANK == 0, stop=True,
                                             skip_group_check=True)
                        ins.then_inc(d_ready, 1)

                    def punish(back, u):
                        if not has_head(i, back):
                            return
                        pe.wait_ge(pen_ready, (n - back) * UNITS + u + 1)
                        for c in range(UNIT * S // BANK):
                            ins = nc.tensor.matmul(d_ps[:, u % 2, c * BANK:(c + 1) * BANK], g.minus_b[:, :],
                                                   pen[:, u % 2, c * BANK:(c + 1) * BANK], start=False, stop=True,
                                                   skip_group_check=True)
                        ins.then_inc(pen_added, 1)

                    def weigh(back, u):
                        if not has_head(i, back):
                            return
                        sl = (j - back) % SL
                        if u == 0:
                            pe.wait_ge(v_placed, n - back + 1)
                            if has_head(i, back + 1):
                                pe.wait_ge(o_kept, n - back)
                        pe.wait_ge(w_ready, (n - back) * UNITS + u + 1)
                        for c in range(UNIT):
                            ins = nc.tensor.matmul(o_ps[32 * c:32 * c + VW, :], vs[:, sl, u * UNIT + c, :],
                                                   wgt[:, u % 4, c * S:(c + 1) * S], start=u == 0, stop=u == UNITS - 1)
                        ins.then_inc(w_used, 1)

                    for p in range(4):
                        back, u = pair_of(p)
                        wback, wu = pair_of(p - 1) if p else (2, 2)
                        differ(back, u)
                        score(4 * p)
                        weigh(wback, wu)
                        differ(back, u + 1)
                        score(4 * p + 1)
                        if p == 0:
                            gather()
                        punish(back, u)
                        score(4 * p + 2)
                        if p == 1:
                            turn()
                        weigh(wback, wu + 1)
                        punish(back, u + 1)
                        score(4 * p + 3)
                steps(pe, step)

            @block.scalar
            def _(act):
                def step(n, j, k, i):
                    def penalty(back, u):
                        if not has_head(i, back):
                            return
                        act.wait_ge(d_ready, (n - back) * UNITS + u + 1)
                        nc.scalar.activation(pen[:, u % 2, :], d_ps[:, u % 2, :], ACT.Relu, scale=-BIG).then_inc(pen_ready, 1)

                    def weight(back, u):
                        if not has_head(i, back):
                            return
                        unit = (n - back) * UNITS + u
                        if u >= 4 or has_head(i, back + 1):
                            act.wait_ge(w_used, unit - 3)
                        act.wait_ge(pen_added, unit + 1)
                        nc.scalar.activation(wgt[:, u % 4, :], d_ps[:, u % 2, :], ACT.Exp).then_inc(w_ready, 1)

                    for p in range(4):
                        back, u = pair_of(p)
                        if p == 3 and has_head(i, 2):
                            act.wait_ge(w_used, (n - 1) * UNITS)
                            if has_head(i, 3):
                                act.wait_ge(u_ready, n - 2)
                            nc.scalar.activation(o_sb[:, :], o_ps[:, :], ACT.Copy).then_inc(o_kept, 1)
                        penalty(back, u)
                        penalty(back, u + 1)
                        weight(back, u)
                        if p == 1 and has_head(i, 1):
                            act.wait_ge(thr_turned, n)
                            nc.scalar.activation(qop[96:96 + TROWS, (j - 1) % SL, :], ring[96:96 + TROWS, place["t", 0] % 3, 0:S],
                                                 ACT.Copy).then_inc(thr_kept, 1)
                        if p == 0 and has_head(i, 3):
                            act.wait_ge(u_ready, n - 2)
                            nc.scalar.activation(g.u[:, bass.ds(n - 3, 1), :, :].rearrange("p o t c -> p (o t c)"),
                                                 ring[:, place["u", 0] % 3, 0:ST * (HD + 1)], ACT.Copy).then_inc(u_kept, 1)
                        weight(back, u + 1)
                steps(act, step)

        clear_semaphores(nc, mine)


def stage_exact(nc, g):
    ctx = ExitStack()
    with ctx:
        def sb(n, s, d=F32):
            return ctx.enter_context(nc.sbuf_tensor(n, s, d))

        mine = []

        def sem(n):
            mine.append(ctx.enter_context(nc.semaphore(n)))
            return mine[-1]

        kop, qop = sb("x_kop", [P, N], BF16), sb("x_qop", [P, S], BF16)
        v_in = sb("x_v", [P, N // P, HD])
        sc, left, wgt, wgt_t = sb("x_sc", [P, N]), sb("x_left", [P, N]), sb("x_wgt", [P, N]), sb("x_wgt_t", [P, N // P, P])
        top, neg_max = sb("x_top", [P, TOPK // 8, 8]), sb("x_neg_max", [P, 1])
        f_head, f_all, ones, f_int = sb("x_f_head", [P, HEADS]), sb("x_f_all", [P, 1]), sb("x_ones", [P, P]), sb("x_f_int", [P, HEADS + 1], I32)
        ps = ctx.enter_context(nc.psum_tensor("ps_x", [P, 8, BANK], F32))
        ones_made, flag_sum, f_step = sem("ex_ones_made"), sem("ex_flag_sum"), sem("ex_flag_step")
        names = ("loaded dve_step scored kept exp_done weighed turned turned_kept summed out_kept neg_made head_done").split()
        m = {n: sem("ex_" + n) for n in names}

        with nc.Block() as block:
            @block.gpsimd
            def _(pool):
                pool.memset(ones[:, :], 1.0).then_inc(ones_made, 1)

            @block.vector
            def _(dve):
                one = Chain(dve, f_step)
                dve.wait_ge(flag_sum, 1)
                one(nc.vector.tensor_reduce(f_head[:, :], ps[:, 0, 0:HEADS * ST].rearrange("p (n t) -> p n t", t=ST), axis=AX.X, op=ALU.max))
                one(nc.vector.tensor_reduce(f_all[:, :], f_head[:, :], axis=AX.X, op=ALU.max))
                one(nc.vector.tensor_scalar(f_int[:, 0:HEADS], f_head[:, :], 1.0, None, ALU.min))
                one(nc.vector.tensor_scalar(f_int[:, HEADS:HEADS + 1], f_all[:, :], 1.0, None, ALU.min))

            @block.tensor
            def _(pe):
                pe.wait_ge(ones_made, 1)
                nc.tensor.matmul(ps[:, 0, 0:HEADS * ST], ones[:, :], g.flags[:, :, :].rearrange("p n t -> p (n t)"),
                                 start=True, stop=True).then_inc(flag_sum, 1)

        def flagged_heads(eng, work):
            any_flag = eng.value_load(f_int[0:1, HEADS:HEADS + 1], min_val=0, max_val=1)
            with eng.If(any_flag > 0):
                with eng.Fori(0, HEADS) as n:
                    flag = eng.value_load(f_int[0:1, bass.ds(n, 1)], min_val=0, max_val=1)
                    with eng.If(flag > 0):
                        work(n)

        def last_wait(eng, s, value):
            eng.wait_ge(s, value)
            eng.sem_clear(s)

        with nc.Block() as block:
            @block.sync
            def _(sp):
                def head(n):
                    def rows(q):
                        return g.kk[bass.ds(n, 1), q:q + 1].rearrange("o q r n -> (o q r) n"), \
                            g.qq[bass.ds(n, 1), q:q + 1].rearrange("o q r n -> (o q r) n")
                    for at, (kq, qq) in enumerate(((0, 0), (1, 0), (2, 0), (0, 1), (1, 1), (0, 2))):
                        sp.dma_start(kop[at * HD:(at + 1) * HD, :], rows(kq)[0]).then_inc(m["loaded"], 16)
                        sp.dma_start(qop[at * HD:(at + 1) * HD, :], rows(qq)[1]).then_inc(m["loaded"], 16)
                    sp.dma_start(v_in[:, :, :], g.vv[bass.ds(n, 1)].rearrange("o p (c d) -> (o p) c d", d=HD)).then_inc(m["loaded"], 16)
                    last_wait(sp, m["head_done"], 1)
                flagged_heads(sp, head)

            @block.tensor
            def _(pe):
                def head(n):
                    last_wait(pe, m["loaded"], 16 * 13)
                    for t in range(ST):
                        if t:
                            last_wait(pe, m["out_kept"], 1)
                        for c in range(SB_N):
                            ins = nc.tensor.matmul(ps[:, c, :], qop[0:KROWS, t * P:(t + 1) * P], kop[0:KROWS, c * BANK:(c + 1) * BANK],
                                                   start=True, stop=True)
                        ins.then_inc(m["scored"], 1)
                        last_wait(pe, m["weighed"], 1)
                        for c in range(N // P):
                            ins = nc.tensor.transpose(ps[:, c // 4, (c % 4) * P:(c % 4 + 1) * P], wgt[:, c * P:(c + 1) * P], g.ident[:, :])
                        ins.then_inc(m["turned"], 1)
                        last_wait(pe, m["turned_kept"], 1)
                        for c in range(N // P):
                            ins = nc.tensor.matmul(ps[:, 0, 0:HD], wgt_t[:, c, :], v_in[:, c, :], start=c == 0, stop=c == N // P - 1)
                        ins.then_inc(m["summed"], 1)
                flagged_heads(pe, head)

            @block.scalar
            def _(act):
                def head(n):
                    for t in range(ST):
                        last_wait(act, m["scored"], 1)
                        for c in range(0, SB_N, 4):
                            ins = nc.scalar.activation(sc[:, c * BANK:(c + 4) * BANK], ps[:, c:c + 4, :].rearrange("p c n -> p (c n)"),
                                                       ACT.Copy)
                        ins.then_inc(m["kept"], 1)
                        last_wait(act, m["neg_made"], 1)
                        nc.scalar.activation(wgt[:, :], sc[:, :], ACT.Exp, bias=neg_max[:, :]).then_inc(m["exp_done"], 1)
                        last_wait(act, m["turned"], 1)
                        for c in range(0, SB_N, 4):
                            ins = nc.scalar.activation(wgt_t[:, c * 4:(c + 4) * 4, :].rearrange("p c n -> p (c n)"),
                                                       ps[:, c:c + 4, :].rearrange("p c n -> p (c n)"), ACT.Copy)
                        ins.then_inc(m["turned_kept"], 1)
                flagged_heads(act, head)

            @block.vector
            def _(dve):
                def head(n):
                    dve.sem_clear(m["dve_step"])
                    one = Chain(dve, m["dve_step"])
                    for t in range(ST):
                        last_wait(dve, m["kept"], 1)
                        src = sc
                        for r in range(TOPK // 8):
                            one(nc.vector.max(top[:, r, :], src[:, :]))
                            if r == 0:
                                nc.vector.tensor_scalar(neg_max[:, :], top[:, 0, 0:1], -1.0, None, ALU.mult).then_inc(m["neg_made"], 1)
                            one(nc.vector.match_replace(left[:, :], top[:, r, :], src[:, :], NEG))
                            src = left
                        last_wait(dve, m["exp_done"], 1)
                        one(nc.vector.scalar_tensor_tensor(wgt[:, :], left[:, :], NEG * 0.99, wgt[:, :], ALU.is_le, ALU.mult))
                        nc.vector.tensor_reduce(g.u[:, bass.ds(n, 1), t, HD], wgt[:, :], axis=AX.X, op=ALU.add).then_inc(m["weighed"], 1)
                        last_wait(dve, m["summed"], 1)
                        nc.vector.tensor_copy(g.u[:, bass.ds(n, 1), t, 0:HD].rearrange("p o d -> p (o d)"), ps[:, 0, 0:HD]) \
                            .then_inc(m["out_kept"] if t < ST - 1 else m["head_done"], 1)
                flagged_heads(dve, head)

        clear_semaphores(nc, mine)


def stage_out(nc, g):
    ctx = ExitStack()
    with ctx:
        def sb(n, s, d=F32):
            return ctx.enter_context(nc.sbuf_tensor(n, s, d))

        mine = []

        def sem(n):
            mine.append(ctx.enter_context(nc.semaphore(n)))
            return mine[-1]

        wo_nat = sb("wo_nat", [P, DC, D])
        wo_t = sb("wo_t", [P, DC, D])
        bo_bc = sb("bo_bc", [P, D])
        rec = sb("rec", [P, HEADS, ST])
        co = sb("co", [P, TT, D])
        co_t = sb("co_t", [P, DC, TOK])
        ps = ctx.enter_context(nc.psum_tensor("ps_out", [P, 8, BANK], F32))
        wo_in, bo_in, step_, turned, kept = sem("wo_in"), sem("bo_in"), sem("out_dve_step"), sem("out_turned"), sem("out_kept")
        wo_turned, wo_kept, co_made, o_ready = sem("wo_turned"), sem("wo_kept"), sem("co_made"), sem("proj_ready")
        with nc.Block() as block:
            @block.sync
            def _(sp):
                sp.dma_start(wo_nat[:, :, :], g.xWo.rearrange("(c p) d -> p c d", p=P)).then_inc(wo_in, 16)
                sp.dma_start(bo_bc[:, :], g.xbo[None, :].to_broadcast([P, D])).then_inc(bo_in, 16)
            @block.vector
            def _(dve):
                one = Chain(dve, step_)
                dve.wait_ge(bo_in, 16)
                one(nc.vector.tensor_tensor(g.x_sb[:, :, :], g.x_sb[:, :, :], bo_bc[:, None, :].to_broadcast([P, TT, D]), ALU.add))
                one(nc.vector.reciprocal(rec[:, :, :], g.u[:, :, :, HD]))
                for t in range(TT):
                    b, q = divmod(t, ST)
                    ins = nc.vector.tensor_tensor(co[:, t, :].rearrange("p (h d) -> p h d", d=HD), g.u[:, b * H:(b + 1) * H, q, 0:HD],
                                                  rec[:, b * H:(b + 1) * H, q:q + 1].to_broadcast([P, H, HD]), ALU.mult)
                ins.then_inc(co_made, 1)
                for t in range(TT):
                    dve.wait_ge(o_ready, t // 2 * 2 + 2)
                    ins = nc.vector.tensor_tensor(g.x_sb[:, t, :], ps[:, 4 + t // 2, (t % 2) * D:(t % 2 + 1) * D],
                                                  g.x_sb[:, t, :], ALU.add)
                one(ins)

            @block.tensor
            def _(pe):
                pe.wait_ge(wo_in, 16)
                for c in range(DC):
                    for e in range(DC):
                        ins = nc.tensor.transpose(ps[:, 7, c * D + e * P:c * D + (e + 1) * P], wo_nat[:, e, c * P:(c + 1) * P], g.ident[:, :])
                ins.then_inc(wo_turned, 1)
                pe.wait_ge(co_made, 1)
                for c in range(DC):
                    for half in range(2):
                        for t in range(4):
                            ins = nc.tensor.transpose(ps[:, c * 2 + half, t * P:(t + 1) * P], co[:, half * 4 + t, c * P:(c + 1) * P], g.ident[:, :])
                        ins.then_inc(turned, 1)
                pe.wait_ge(wo_kept, 1)
                pe.wait_ge(kept, 4)
                for t in range(TT):
                    for c in range(DC):
                        ins = nc.tensor.matmul(ps[:, 4 + t // 2, (t % 2) * D:(t % 2 + 1) * D], co_t[:, c, t * P:(t + 1) * P], wo_t[:, c, :],
                                               start=c == 0, stop=c == DC - 1)
                    ins.then_inc(o_ready, 1)

            @block.scalar
            def _(act):
                act.wait_ge(wo_turned, 1)
                nc.scalar.activation(wo_t[:, :, :].rearrange("p c d -> p (c d)"), ps[:, 7, :], ACT.Copy).then_inc(wo_kept, 1)
                for c in range(DC):
                    for half in range(2):
                        act.wait_ge(turned, c * 2 + half + 1)
                        nc.scalar.activation(co_t[:, c, half * 512:(half + 1) * 512], ps[:, c * 2 + half, :], ACT.Copy).then_inc(kept, 1)

        clear_semaphores(nc, mine)


def layer_norm(nc, dve, one, rows, n, stats, mv, stats_made, rstd_made, rstd, out, out_made, count):
    for t in range(n):
        one(nc.vector.bn_stats(stats[:, t, :], rows(t)))
        ins = nc.vector.bn_aggr(mv[:, t, :], stats[:, t, :])
    ins.then_inc(stats_made, 1)
    dve.wait_ge(rstd_made, count)
    for t in range(n):
        ins = nc.vector.tensor_scalar(out[:, t, :], rows(t), mv[:, t, 0:1], rstd[:, t:t + 1], ALU.subtract, ALU.mult)
    ins.then_inc(out_made, 1)


def rstd_steps(nc, pool, one, mv, veps, power, rstd, rstd_made):
    one(nc.gpsimd.tensor_scalar(veps, mv[:, :, 1], EPS_LN, None, ALU.add))
    nc.gpsimd.tensor_tensor(rstd, veps, power, ALU.pow).then_inc(rstd_made, 1)


def stage_delta(nc, g):
    RH = 8
    RD = D // RH
    RG = P // RD
    HG = RH // RG
    NC2 = S // P
    NM = NC2 * HG
    LEVELS = 7
    HALF = 2
    ctx = ExitStack()
    with ctx:
        def sb(n, s, d=F32):
            return ctx.enter_context(nc.sbuf_tensor(n, s, d))

        mine = []

        def sem(n):
            mine.append(ctx.enter_context(nc.semaphore(n)))
            return mine[-1]

        lnw_bc, lnb_bc = sb("lnw_bc", [P, D]), sb("lnb_bc", [P, D])
        masks = sb("level_masks", [P, LEVELS, P])
        mask0t = sb("mask0t", [P, P])
        upper, upper_in = sb("upper", [P, P]), sb("upper_in", [P, P])
        half = sb("half", [P, TT * RH])
        minus_half = sb("minus_half_d", [P, TT])
        stats, mv, veps, rstd = sb("d_stats", [P, TT, 6]), sb("d_mv", [P, TT, 2]), sb("d_veps", [P, TT]), sb("d_rstd", [P, TT])
        q_t, kn_t, kb_t = sb("d_q_t", [P, DC, TOK]), sb("d_kn_t", [P, DC, TOK]), sb("d_kb_t", [P, DC, TOK])
        kn, vb = sb("d_kn", [P, TT, D]), sb("d_vb", [P, TT, D])
        ps = ctx.enter_context(nc.psum_tensor("ps_d", [P, 8, BANK], F32))

        once_in = sem("d_once_in")
        early = ExitStack()
        early_sb = lambda n, s: early.enter_context(nc.sbuf_tensor(n, s, F32))
        w = early_sb("dw", [P, 3, DC, D])
        wb = early_sb("dwb", [P, DC, RH])
        xn, xn_t = early_sb("d_xn", [P, TT, D]), early_sb("d_xn_t", [P, DC, TOK])
        k_raw, v_raw, beta = early_sb("d_k", [P, TT, D]), early_sb("d_v", [P, TT, D]), early_sb("d_beta", [P, TT, RH])
        sq, n2, nrm = early_sb("d_sq", [P, TT, D]), early_sb("d_n2", [P, TT * RH]), early_sb("d_nrm", [P, TT * RH])
        ev, kb = early_sb("d_ev", [P, TT, D]), early_sb("d_kb", [P, TT, D])

        def rows(t):
            return g.x_sb[:, t, :]

        def head(c, h):
            hg, hr = divmod(h, RG)
            return hg, hr, c * HG + hg

        def col(h):
            return slice(h * RD, (h + 1) * RD)

        def four(mask):
            return mask[:, None, :].to_broadcast([P, NM, P])

        def bank4(n):
            return ps[:, n, :].rearrange("p (m c) -> p m c", c=P)

        names = ("dve_step pool_step stats_made rstd_made xn_made turned turned_kept beta_ready beta_exp k_ready k_kept v_ready "
                 "v_kept q_ready q_kept n2_made norm_made kn_made kb_made kn_turned kn_kept kb_turned kb_kept").split()
        m = {n: sem("dp_" + n) for n in names}
        with nc.Block() as block:
            @block.sync
            def _(sp):
                for i, src in enumerate((g.dWq, g.dWk, g.dWv)):
                    sp.dma_start(w[:, i], src.rearrange("(c p) d -> p c d", p=P)).then_inc(once_in, 16)
                sp.dma_start(wb[:, :, :], g.dWb.rearrange("(c p) d -> p c d", p=P)).then_inc(once_in, 16)
                sp.dma_start(lnw_bc[:, :], g.lnw[None, :].to_broadcast([P, D])).then_inc(once_in, 16)
                sp.dma_start(lnb_bc[:, :], g.lnb[None, :].to_broadcast([P, D])).then_inc(once_in, 16)

            @block.gpsimd
            def _(pool):
                one = Chain(pool, m["pool_step"])

                def keep(mat, cond, pattern, base, mult):
                    one(pool.affine_select(out=mat, in_=mat, compare_op=cond, fill=0.0, base=base, pattern=pattern,
                                           channel_multiplier=mult))
                one(pool.memset(half[:, :], 0.5))
                one(pool.memset(minus_half[:, :], -0.5))
                pool.wait_ge(m["stats_made"], 1)
                rstd_steps(nc, pool, one, mv, veps[:, :], minus_half[:, :], rstd[:, :], m["rstd_made"])
                one(pool.memset(upper[:, :], 1.0))
                one(pool.memset(upper_in[:, :], 1.0))
                keep(upper[:, :], ALU.is_gt, [[1, P]], 0, -1)
                keep(upper_in[:, :], ALU.is_ge, [[1, P]], 0, -1)
                pool.wait_ge(m["n2_made"], 1)
                nc.gpsimd.tensor_tensor(nrm[:, :], n2[:, :], half[:, :], ALU.pow).then_inc(m["norm_made"], 1)
                one(pool.memset(masks[:, :, :], 1.0))
                one(pool.memset(mask0t[:, :], 1.0))
                for lv in range(LEVELS):
                    w2, w1 = 2 << lv, 1 << lv
                    cols = masks[:, lv, :].rearrange("p (a q b) -> p a q b", q=2, b=w1)
                    one(pool.memset(cols[:, :, 1, :], 0.0))
                    first = masks[:, lv, :].rearrange("p (a b) -> p a b", b=w2)
                    keep(first, ALU.is_ge, [[-w2, P // w2], [0, w2]], -w1, 1)
                    keep(first, ALU.is_ge, [[w2, P // w2], [0, w2]], w2 - 1, -1)
                cols = mask0t[:, :].rearrange("p (a b) -> p a b", b=2)
                one(pool.memset(cols[:, :, 0:1], 0.0))
                keep(cols, ALU.is_equal, [[-2, P // 2], [0, 2]], 0, 1)

            @block.vector
            def _(dve):
                one = Chain(dve, m["dve_step"])
                layer_norm(nc, dve, one, rows, TT, stats, mv, m["stats_made"], m["rstd_made"], rstd, xn, m["xn_made"], 1)
                dve.wait_ge(m["beta_exp"], 1)
                one(nc.vector.tensor_scalar(beta[:, :, :], beta[:, :, :], 1.0, None, ALU.add))
                one(nc.vector.reciprocal(beta[:, :, :], beta[:, :, :]))
                dve.wait_ge(m["k_kept"], TT // 2)
                one(nc.vector.tensor_tensor(sq[:, :, :], k_raw[:, :, :], k_raw[:, :, :], ALU.mult))
                nc.vector.tensor_reduce(n2[:, :], sq[:, :, :].rearrange("p c (h d) -> p (c h) d", d=RD), axis=AX.X,
                                        op=ALU.add).then_inc(m["n2_made"], 1)

                def heads(x):
                    return x[:, :, :].rearrange("p c (h d) -> p (c h) d", d=RD)
                b_bc = beta[:, :, :].rearrange("p c h -> p (c h)")[:, :, None].to_broadcast([P, TT * RH, RD])
                dve.wait_ge(m["norm_made"], 1)
                one(nc.vector.tensor_scalar(nrm[:, :], nrm[:, :], 1e-12, None, ALU.max))
                one(nc.vector.reciprocal(nrm[:, :], nrm[:, :]))
                nc.vector.tensor_tensor(heads(kn), heads(k_raw), nrm[:, :, None].to_broadcast([P, TT * RH, RD]), ALU.mult).then_inc(m["kn_made"], 1)
                dve.wait_ge(m["kn_made"], 1)
                nc.vector.tensor_tensor(heads(kb), heads(kn), b_bc, ALU.mult).then_inc(m["kb_made"], 1)
                dve.wait_ge(m["v_kept"], TT // 2)
                one(nc.vector.tensor_scalar(ev[:, :, :], ev[:, :, :], 1.0, None, ALU.add))
                one(nc.vector.reciprocal(ev[:, :, :], ev[:, :, :]))
                one(nc.vector.tensor_tensor(vb[:, :, :], v_raw[:, :, :], ev[:, :, :], ALU.mult))
                one(nc.vector.tensor_tensor(heads(vb), heads(vb), b_bc, ALU.mult))

            @block.scalar
            def _(act):
                def two(x, i):
                    return x[:, 2 * i:2 * i + 2, :].rearrange("p t d -> p (t d)")

                def part(x, i):
                    return x[:, i // HALF, i % HALF * BANK:(i % HALF + 1) * BANK]
                for i in range(4):
                    act.wait_ge(m["turned"], i + 1)
                    nc.scalar.activation(part(xn_t, i), ps[:, i, :], ACT.Copy).then_inc(m["turned_kept"], 1)
                act.wait_ge(m["beta_ready"], 1)
                nc.scalar.activation(beta[:, :, :].rearrange("p c h -> p (c h)"), ps[:, 4, 0:TT * RH], ACT.Exp, scale=-1.0).then_inc(m["beta_exp"], 1)
                for i in range(4):
                    act.wait_ge(m["k_ready"], i + 1)
                    nc.scalar.activation(two(k_raw, i), ps[:, i, :], ACT.Copy).then_inc(m["k_kept"], 1)
                for i in range(4):
                    act.wait_ge(m["v_ready"], i + 1)
                    nc.scalar.activation(two(v_raw, i), ps[:, 4 + i, :], ACT.Copy)
                    nc.scalar.activation(two(ev, i), ps[:, 4 + i, :], ACT.Exp, scale=-1.0).then_inc(m["v_kept"], 1)
                for i in range(4):
                    act.wait_ge(m["q_ready"], i + 1)
                    nc.scalar.activation(part(q_t, i), ps[:, i, :], ACT.Copy).then_inc(m["q_kept"], 1)
                for i in range(4):
                    act.wait_ge(m["kn_turned"], i + 1)
                    nc.scalar.activation(part(kn_t, i), ps[:, 4 + i, :], ACT.Copy).then_inc(m["kn_kept"], 1)
                for i in range(4):
                    act.wait_ge(m["kb_turned"], i + 1)
                    nc.scalar.activation(part(kb_t, i), ps[:, i, :], ACT.Copy).then_inc(m["kb_kept"], 1)

            @block.tensor
            def _(pe):
                mm = nc.tensor.matmul

                def turn(base, src, done, free):
                    for i in range(4):
                        c, part = divmod(i, HALF)
                        if free:
                            pe.wait_ge(free, i + 1)
                        for t in range(4):
                            ins = nc.tensor.transpose(ps[:, base + i, t * P:(t + 1) * P], src[:, part * 4 + t, c * P:(c + 1) * P], g.ident[:, :])
                        ins.then_inc(done, 1)
                pe.wait_ge(m["xn_made"], 1)
                turn(0, xn, m["turned"], None)
                pe.wait_ge(m["turned_kept"], 4)
                pe.wait_ge(once_in, 96)
                for t in range(TT):
                    for c in range(DC):
                        ins = mm(ps[:, 4, t * RH:(t + 1) * RH], xn_t[:, c, t * P:(t + 1) * P], wb[:, c, :], start=c == 0, stop=c == DC - 1)
                ins.then_inc(m["beta_ready"], 1)
                for base, wi, done in ((0, 1, "k_ready"), (4, 2, "v_ready")):
                    if wi == 2:
                        pe.wait_ge(m["beta_exp"], 1)
                    for t in range(TT):
                        for c in range(DC):
                            ins = mm(ps[:, base + t // 2, t % 2 * D:(t % 2 + 1) * D], xn_t[:, c, t * P:(t + 1) * P], w[:, wi, c, :],
                                     start=c == 0, stop=c == DC - 1)
                        if t % 2:
                            ins.then_inc(m[done], 1)
                for i in range(4):
                    e, part = divmod(i, HALF)
                    pe.wait_ge(m["k_kept"], i + 1)
                    for c in range(DC):
                        ins = mm(ps[:, i, :], w[:, 0, c, e * P:(e + 1) * P], xn_t[:, c, part * BANK:(part + 1) * BANK], start=c == 0, stop=c == DC - 1)
                    ins.then_inc(m["q_ready"], 1)
                pe.wait_ge(m["kn_made"], 1)
                turn(4, kn, m["kn_turned"], m["v_kept"])
                pe.wait_ge(m["kb_made"], 1)
                turn(0, kb, m["kb_turned"], m["q_kept"])
        clear_semaphores(nc, list(m.values()))
        early.close()

        up, tm, tt, wm = [sb(f"d_{n}", [P, RG, NM, P]) for n in ("up", "tm", "tt", "wm")]
        kn_b, kb_b, q_b = sb("d_kn_b", [P, DC, S]), sb("d_kb_b", [P, DC, S]), sb("d_q_b", [P, DC, S])
        tt_all, mt_all = sb("d_tt_all", [P, B, RG, NM, P]), sb("d_mt_all", [P, B, RG, NM, P])
        names = "kn_b_made kb_b_made q_b_made dve_step pool_step gram up_made tm_made tt_made w_ready w_kept z_ready z_kept mgram mt_kept".split()
        m = {n: sem("ds_" + n) for n in names}
        with nc.Fori(0, B) as b:
            with nc.Block() as block:
                def of_batch(x):
                    return x[:, :, bass.ds(b * S, S)]

                def four_of(x, r):
                    return x[:, bass.ds(b, 1), r].rearrange("p o m c -> p (o m) c")

                @block.gpsimd
                def _(pool):
                    one = Chain(pool, m["pool_step"])
                    for r in range(RG):
                        pool.wait_ge(m["up_made"], r + 1)
                        one(nc.gpsimd.tensor_tensor(tt[:, r], up[:, r], four(mask0t), ALU.mult))
                        nc.gpsimd.tensor_tensor(tt[:, r], four(g.ident), tt[:, r], ALU.subtract).then_inc(m["tt_made"], 1)

                @block.vector
                def _(dve):
                    one = Chain(dve, m["dve_step"])
                    nc.vector.tensor_copy(kb_b[:, :, :], of_batch(kb_t)).then_inc(m["kb_b_made"], 1)
                    dve.wait_ge(m["gram"], RG)
                    for r in range(RG):
                        nc.vector.tensor_tensor(up[:, r], bank4(r), four(upper), ALU.mult).then_inc(m["up_made"], 1)
                        one(nc.vector.tensor_tensor(tm[:, r], bank4(4 + r), four(masks[:, 0, :]), ALU.mult))
                        nc.vector.tensor_tensor(tm[:, r], four(g.ident), tm[:, r], ALU.subtract).then_inc(m["tm_made"], 1)
                    for lv in range(1, LEVELS):
                        last = lv == LEVELS - 1
                        for r in range(RG):
                            dve.wait_ge(m["w_ready"], (lv - 1) * RG + r + 1)
                            nc.vector.tensor_tensor(wm[:, r], bank4(r), four(masks[:, lv, :]), ALU.mult).then_inc(m["w_kept"], 1)
                        for r in range(RG):
                            dve.wait_ge(m["z_ready"], (lv - 1) * RG + r + 1)
                            if not last:
                                nc.vector.tensor_tensor(tm[:, r], tm[:, r], bank4(r), ALU.subtract)
                            nc.vector.tensor_tensor(four_of(tt_all, r) if last else tt[:, r], tt[:, r], bank4(4 + r),
                                                    ALU.subtract).then_inc(m["z_kept"], 1)
                            if last:
                                dve.wait_ge(m["mgram"], r + 1)
                                nc.vector.tensor_tensor(four_of(mt_all, r), bank4(r), four(upper_in), ALU.mult).then_inc(m["mt_kept"], 1)
                    dve.wait_ge(m["z_kept"], (LEVELS - 1) * RG)
                    dve.wait_ge(m["mt_kept"], RG)

                @block.scalar
                def _(act):
                    nc.scalar.activation(kn_b[:, :, :], of_batch(kn_t), ACT.Copy).then_inc(m["kn_b_made"], 1)
                    nc.scalar.activation(q_b[:, :, :], of_batch(q_t), ACT.Copy).then_inc(m["q_b_made"], 1)

                @block.tensor
                def _(pe):
                    mm = nc.tensor.matmul
                    pe.wait_ge(m["kn_b_made"], 1)
                    pe.wait_ge(m["kb_b_made"], 1)

                    def gram(bank, left, right, r, hg, c):
                        part, at = slice(RD * r, RD * (r + 1)), (c * HG + hg) * P
                        return mm(ps[:, bank + r, at:at + P], left[part, hg, c * P:(c + 1) * P],
                                  right[part, hg, c * P:(c + 1) * P], start=True, stop=True)
                    for bank, left, right in ((4, kb_b, kn_b), (0, kn_b, kb_b)):
                        for hg in range(HG):
                            for c in range(NC2):
                                for r in range(RG):
                                    ins = gram(bank, left, right, r, hg, c)
                                    if bank == 0 and hg == HG - 1 and c == NC2 - 1:
                                        ins.then_inc(m["gram"], 1)
                    for lv in range(1, LEVELS):
                        last = lv == LEVELS - 1
                        for r in range(RG):
                            if lv > 1:
                                pe.wait_ge(m["z_kept"], (lv - 2) * RG + r + 1)
                            else:
                                pe.wait_ge(m["tm_made"], r + 1)
                            for i in range(NM):
                                ins = mm(ps[:, r, i * P:(i + 1) * P], up[:, r, i, :], tm[:, r, i, :], start=True, stop=True)
                            ins.then_inc(m["w_ready"], 1)
                        for r in range(RG):
                            pe.wait_ge(m["w_kept"], (lv - 1) * RG + r + 1)
                            if lv == 1:
                                pe.wait_ge(m["tt_made"], r + 1)
                            for i in range(NM):
                                if not last:
                                    mm(ps[:, r, i * P:(i + 1) * P], tt[:, r, i, :], wm[:, r, i, :], start=True, stop=True)
                                ins = mm(ps[:, 4 + r, i * P:(i + 1) * P], wm[:, r, i, :], tt[:, r, i, :], start=True, stop=True)
                            ins.then_inc(m["z_ready"], 1)
                            if last:
                                if r == 0:
                                    pe.wait_ge(m["q_b_made"], 1)
                                for hg in range(HG):
                                    for c in range(NC2):
                                        ins = gram(0, kn_b, q_b, r, hg, c)
                                ins.then_inc(m["mgram"], 1)

            clear_semaphores(nc, list(m.values()))

        u, s1, r1 = sb("d_u", [P, B, NC2, D]), sb("d_s1", [P, B, HG, RD]), sb("d_r1", [P, B, D])
        o, on = sb("d_o", [P, TT, D]), sb("d_on", [P, TT, D])
        O_BANK = (7, 2, 0, 1)
        names = ("pool_step dve_step stats_made rstd_made ln_made u_ready u_kept s_ready s_kept r_ready r_kept o_ready o_kept qs_ready").split()
        m = {n: sem("do_" + n) for n in names}
        with nc.Block() as block:
            @block.gpsimd
            def _(pool):
                one = Chain(pool, m["pool_step"])
                pool.wait_ge(m["stats_made"], 1)
                rstd_steps(nc, pool, one, mv, veps[:, :], minus_half[:, :], rstd[:, :], m["rstd_made"])

            @block.vector
            def _(dve):
                one = Chain(dve, m["dve_step"])
                hv = "p (g r d) -> p r g d"
                dve.wait_ge(m["r_ready"], 1)
                for b in range(B):
                    ins = nc.vector.tensor_tensor(r1[:, b, :].rearrange(hv, r=RG, d=RD), vb[:, b * NC2 + 1, :].rearrange(hv, r=RG, d=RD),
                                                  ps[:, 3:7, b * HG * RD:(b + 1) * HG * RD].rearrange("p r (g d) -> p r g d", d=RD), ALU.subtract)
                ins.then_inc(m["r_kept"], 1)
                dve.wait_ge(m["qs_ready"], 1)
                for b in range(B):
                    dve.wait_ge(m["o_kept"], b + 1)
                    second = o[:, b * NC2 + 1, :].rearrange(hv, r=RG, d=RD)
                    one(nc.vector.tensor_tensor(second, second,
                                                ps[:, 3:7, (B + b) * HG * RD:(B + b + 1) * HG * RD].rearrange("p r (g d) -> p r g d", d=RD), ALU.add))
                layer_norm(nc, dve, one, lambda t: o[:, t, :], TT, stats, mv, m["stats_made"], m["rstd_made"], rstd, on, m["ln_made"], 1)
                dve.wait_ge(m["ln_made"], 1)
                one(nc.vector.tensor_tensor(on[:, :, :], on[:, :, :], lnw_bc[:, None, :].to_broadcast([P, TT, D]), ALU.mult))
                one(nc.vector.tensor_tensor(on[:, :, :], on[:, :, :], lnb_bc[:, None, :].to_broadcast([P, TT, D]), ALU.add))
                one(nc.vector.tensor_tensor(g.x_sb[:, :, :], g.x_sb[:, :, :], on[:, :, :], ALU.add))

            @block.scalar
            def _(act):
                def keep_u(c, count):
                    for i in range(2):
                        act.wait_ge(m["u_ready"], 2 * c + i + 1)
                        nc.scalar.activation(u[:, 2 * i:2 * i + 2, c, :], ps[:, i, :].rearrange("p (b d) -> p b d", d=D), ACT.Copy).then_inc(m["u_kept"], 1)
                keep_u(0, 1)
                act.wait_ge(m["s_ready"], 1)
                nc.scalar.activation(s1[:, :, :, :].rearrange("p b g d -> p (b g d)"), ps[:, 2, 0:B * HG * RD], ACT.Copy).then_inc(m["s_kept"], 1)
                keep_u(1, 2)
                for b in range(B):
                    act.wait_ge(m["o_ready"], b + 1)
                    nc.scalar.activation(o[:, b * NC2:(b + 1) * NC2, :].rearrange("p c d -> p (c d)"), ps[:, O_BANK[b], :], ACT.Copy).then_inc(m["o_kept"], 1)

            @block.tensor
            def _(pe):
                mm = nc.tensor.matmul

                def solve(c, rhs):
                    for b in range(B):
                        for h in range(RH):
                            hg, r, i = head(c, h)
                            ins = mm(ps[:, b // 2, b % 2 * D + h * RD:b % 2 * D + (h + 1) * RD], tt_all[:, b, r, i, :], rhs(b)[:, col(h)], start=True, stop=True)
                        if b % 2:
                            ins.then_inc(m["u_ready"], 1)
                solve(0, lambda b: vb[:, b * NC2, :])
                for b in range(B):
                    if b % 2 == 0:
                        pe.wait_ge(m["u_kept"], b // 2 + 1)
                    for h in range(RH):
                        hg, r, i = head(0, h)
                        at = (b * HG + hg) * RD
                        ins = mm(ps[RD * r:RD * (r + 1), 2, at:at + RD], kn[:, b * NC2, col(h)], u[:, b, 0, col(h)], start=True, stop=True)
                ins.then_inc(m["s_ready"], 1)
                pe.wait_ge(m["s_kept"], 1)

                def times_s1(src, first):
                    for b in range(B):
                        for h in range(RH):
                            hg, r, i = head(1, h)
                            part, at = slice(RD * r, RD * (r + 1)), ((first + b) * HG + hg) * RD
                            ins = mm(ps[:, 3 + r, at:at + RD], src[part, hg, b * S + P:(b + 1) * S], s1[part, b, hg, :], start=True, stop=True)
                    return ins
                times_s1(kb_t, 0).then_inc(m["r_ready"], 1)
                pe.wait_ge(m["r_kept"], 1)
                solve(1, lambda b: r1[:, b, :])
                times_s1(q_t, B).then_inc(m["qs_ready"], 1)
                pe.wait_ge(m["u_kept"], 4)
                for b in range(B):
                    for c in range(NC2):
                        for h in range(RH):
                            hg, r, i = head(c, h)
                            ins = mm(ps[:, O_BANK[b], c * D + h * RD:c * D + (h + 1) * RD], mt_all[:, b, r, i, :], u[:, b, c, col(h)], start=True, stop=True)
                    ins.then_inc(m["o_ready"], 1)

        clear_semaphores(nc, [once_in] + list(m.values()))


def stage_experts(nc, g):
    E, F = 8, 1024
    CAP = TOK * 5 // (4 * E)
    FC = F // P
    SLOTS0 = TOK
    SLOTS = SLOTS0 + (E - 1) * CAP
    HALF = CAP // 2
    G0 = 256
    WS = 4
    ctx = ExitStack()
    with ctx:
        def sb(n, s, d=F32):
            return ctx.enter_context(nc.sbuf_tensor(n, s, d))

        mine = []

        def sem(n):
            mine.append(ctx.enter_context(nc.semaphore(n)))
            return mine[-1]

        r_nat, r_t = sb("r_nat", [E, D]), sb("r_t", [P, DC, E])
        b1, b2 = sb("b1_sb", [P, E, FC]), sb("b2_sb", [P, E, DC])
        w1, w2 = sb("w1_sb", [P, WS, DC, F]), sb("w2_sb", [P, WS, FC, D])
        power = sb("e_power", [P, TT])
        stats, mv, veps, rstd = sb("e_stats", [P, TT, 6]), sb("e_mv", [P, TT, 2]), sb("e_veps", [P, TT]), sb("e_rstd", [P, TT])
        xn, xn_t = sb("e_xn", [P, TT, D]), sb("e_xn_t", [P, DC, TOK])
        zero = sb("e_zero", [P, D])
        iota_i, iota_e = sb("iota_i", [P, E], I32), sb("iota_e", [P, E])
        lg, mx, ex, sm = sb("logits", [P, TT, E]), sb("e_mx", [P, TT]), sb("e_ex", [P, TT, E]), sb("e_sm", [P, TT])
        prob, pick, idx = sb("prob", [P, TT]), sb("pick", [P, TT, E]), sb("e_idx", [P, TT])
        hot, hot_b = sb("hot", [P, TT, E]), sb("hot_b", [P, TT, E], BF16)
        p_wide, p_row = sb("p_wide", [P, TT, P]), sb("p_row", [P, TOK])
        before, eqm = sb("before", [P, TT, TOK], BF16), sb("eqm", [P, P])
        later = sb("later", [P, P])
        ones_b = sb("ones_b", [P, P], BF16)
        cnt, over_e, pre = sb("e_cnt", [P, E]), sb("e_over", [P, E]), sb("e_pre", [P, E])
        base_i, base, jump = sb("base_i", [P, E], I32), sb("base", [P, E]), sb("jump", [P, E])
        rk, tmp = sb("e_rank", [P, TT]), sb("e_tmp", [P, TT, E])
        sa, sj, ov, slot, slot_u = sb("e_sa", [P, TT]), sb("e_sj", [P, TT]), sb("e_ov", [P, TT]), sb("e_slot", [P, TT]), sb("e_slot_u", [P, TT], mybir.dt.uint32)
        more, more_i = sb("e_more", [P, 1]), sb("e_more_i", [P, 1], I32)
        xs0, xs0_t = sb("xs0", [P, 2, D]), sb("xs0_t", [P, DC, G0])
        hid = sb("hid", [P, FC, G0])
        y_t, y_nat = sb("y_t", [P, DC, G0]), sb("y_nat", [P, 2, D])
        got = sb("got", [P, TT, D])
        ps = ctx.enter_context(nc.psum_tensor("ps_e", [P, 8, BANK], F32))

        m = {n: sem("e_" + n) for n in (
            "small_in zero_made zero_out pool_step dve_step stats_made rstd_made xn_made turned turned_kept r_turned r_kept logits_ready "
            "logits_kept exp_made prob_wide p_turned p_kept before_made ranks_ready slots_made scattered x_in x_turned x_kept "
            "h_ready h_kept y_ready y_kept y_turned y_out_kept y_out gathered all_out done stored w1_in w2_in w_done").split()}
        xs, ys = g.xs, g.ys
        jobs = [(e, SLOTS0 + (e - 1) * CAP, HALF) for e in range(1, E)] + [(0, s, P) for s in range(0, SLOTS0, G0)]
        JOBS1 = E
        H_BANKS = (2, 3, 7)
        LOADS = 2

        def batches(eng, run):
            run(0, JOBS1)
            flag = eng.value_load(more_i[0:1, 0:1], min_val=0, max_val=1)
            with eng.If(flag > 0):
                run(JOBS1, len(jobs))

        with nc.Block() as block:
            def store_y(sp, i):
                e, s, rows = jobs[i]
                sp.wait_ge(m["y_out_kept"], i + 1)
                sp.dma_start(ys[s:s + rows * LOADS, :].rearrange("(c p) d -> p c d", p=rows), y_nat[0:rows, :, :]).then_inc(m["y_out"], 16)

            @block.sync
            def _(sp):
                sp.dma_start(r_nat[:, :], g.router).then_inc(m["small_in"], 16)
                with nc.allow_non_contiguous_dma("vectors to partitions"):
                    for e in range(E):
                        sp.dma_start(b1[:, e, :], g.b1[e].rearrange("(c p) -> p c", p=P)).then_inc(m["small_in"], 16)
                        sp.dma_start(b2[:, e, :], g.b2[e].rearrange("(c p) -> p c", p=P)).then_inc(m["small_in"], 16)

                def weights(i):
                    e = jobs[i][0]
                    if i >= WS:
                        sp.wait_ge(m["w_done"], i - WS + 1)
                    sp.dma_start(w1[:, i % WS], g.W1[e].rearrange("(c p) f -> p c f", p=P)).then_inc(m["w1_in"], 16)
                    sp.dma_start(w2[:, i % WS], g.W2[e].rearrange("(c p) d -> p c d", p=P)).then_inc(m["w2_in"], 16)
                sp.wait_ge(m["zero_made"], 1)
                for s in range(0, SLOTS, P):
                    n = min(P, SLOTS - s)
                    sp.dma_start(xs[s:s + n, :], zero[0:n, :]).then_inc(m["zero_out"], 16)
                for s in range(G0, SLOTS0, P):
                    sp.dma_start(ys[s:s + P, :], zero[:, :]).then_inc(m["zero_out"], 16)
                for i in range(WS):
                    weights(i)
                sp.wait_ge(m["scattered"], 16 * TT)

                def run(first, end):
                    for i in range(first, end):
                        e, s, rows = jobs[i]
                        if i:
                            sp.wait_ge(m["x_turned"], i)
                        sp.dma_start(xs0[0:rows, :, :], xs[s:s + rows * LOADS, :].rearrange("(c p) d -> p c d", p=rows)).then_inc(m["x_in"], 16)
                        if i >= first + 2:
                            store_y(sp, i - 2)
                        if 1 <= i and i + WS - 1 < JOBS1:
                            weights(i + WS - 1)
                    store_y(sp, end - 2)
                    store_y(sp, end - 1)
                    sp.wait_ge(m["y_out"], 16 * end)
                batches(sp, run)
                sp.sem_inc(m["all_out"], 1)
                sp.wait_ge(m["done"], 1)
                sp.dma_start(g.out.rearrange("(t p) d -> p t d", p=P), g.x_sb[:, :, :]).then_inc(m["stored"], 16)
                sp.wait_ge(m["stored"], 16)

            @block.gpsimd
            def _(pool):
                one = Chain(pool, m["pool_step"])
                nc.gpsimd.memset(zero[:, :], 0.0).then_inc(m["zero_made"], 1)
                one(pool.memset(power[:, :], -0.5))
                one(pool.memset(ones_b[:, :], 1.0))
                one(pool.memset(later[:, :], 1.0))
                one(pool.affine_select(out=later[:, :], in_=later[:, :], compare_op=ALU.is_gt, fill=0.0, base=0, pattern=[[1, P]],
                                       channel_multiplier=-1))
                one(pool.iota(iota_i[:, :], pattern=[[1, E]], base=0, channel_multiplier=0))
                one(pool.iota(base_i[:, :], pattern=[[CAP, E]], base=SLOTS0 - CAP, channel_multiplier=0))
                one(pool.memset(base_i[:, 0:1], 0))
                pool.wait_ge(m["stats_made"], 1)
                rstd_steps(nc, pool, one, mv, veps[:, :], power[:, :], rstd[:, :], m["rstd_made"])
                pool.wait_ge(m["zero_out"], 16 * ((SLOTS + P - 1) // P + (SLOTS0 - G0) // P))
                pool.wait_ge(m["slots_made"], 1)
                for t in range(TT):
                    pool.indirect_dma_start(out=xs, out_offset=bass.IndirectOffsetOnAxis(ap=slot_u[:, t:t + 1], axis=0), in_=xn[:, t, :],
                                            in_offset=None).then_inc(m["scattered"], 16)
                pool.wait_ge(m["scattered"], 16 * TT)
                pool.wait_ge(m["all_out"], 1)
                for t in range(TT):
                    pool.indirect_dma_start(out=got[:, t, :], out_offset=None, in_=ys,
                                            in_offset=bass.IndirectOffsetOnAxis(ap=slot_u[:, t:t + 1], axis=0)).then_inc(m["gathered"], 16)
                pool.wait_ge(m["gathered"], 16 * TT)

            @block.vector
            def _(dve):
                one = Chain(dve, m["dve_step"])
                tt_ = nc.vector.tensor_tensor
                layer_norm(nc, dve, one, lambda t: g.x_sb[:, t, :], TT, stats, mv, m["stats_made"], m["rstd_made"], rstd, xn, m["xn_made"], 1)
                dve.wait_ge(m["r_turned"], 1)
                nc.vector.tensor_copy(r_t[:, :, :].rearrange("p c e -> p (c e)"), ps[:, 4, 0:DC * E]).then_inc(m["r_kept"], 1)
                dve.wait_ge(m["logits_ready"], 1)
                one(nc.vector.tensor_copy(lg[:, :, :].rearrange("p t e -> p (t e)"), ps[:, 5, 0:TT * E]))
                one(nc.vector.tensor_reduce(mx[:, :], lg[:, :, :], axis=AX.X, op=ALU.max))
                wide = [P, TT, E]
                one(tt_(ex[:, :, :], lg[:, :, :], mx[:, :, None].to_broadcast(wide), ALU.subtract))
                nc.vector.tensor_scalar(pick[:, :, :], ex[:, :, :], 0.0, -float(E), ALU.is_ge, ALU.mult).then_inc(m["logits_kept"], 1)
                dve.wait_ge(m["logits_kept"], 1)
                one(nc.vector.tensor_copy(iota_e[:, :], iota_i[:, :]))
                one(nc.vector.tensor_copy(base[:, :], base_i[:, :]))
                one(tt_(pick[:, :, :], pick[:, :, :], iota_e[:, None, :].to_broadcast(wide), ALU.add))
                one(nc.vector.tensor_reduce(idx[:, :], pick[:, :, :], axis=AX.X, op=ALU.min))
                one(tt_(hot[:, :, :], pick[:, :, :], idx[:, :, None].to_broadcast(wide), ALU.is_equal))
                one(nc.vector.tensor_copy(hot_b[:, :, :], hot[:, :, :]))
                dve.wait_ge(m["exp_made"], 1)
                one(nc.vector.tensor_reduce(sm[:, :], lg[:, :, :], axis=AX.X, op=ALU.add))
                one(nc.vector.reciprocal(prob[:, :], sm[:, :]))
                nc.vector.tensor_copy(p_wide[:, :, :], prob[:, :, None].to_broadcast([P, TT, P])).then_inc(m["prob_wide"], 1)
                dve.wait_ge(m["p_kept"], 2)
                for t in range(TT):
                    pj = prob[:, t:t + 1]
                    if t:
                        nc.vector.tensor_scalar(before[:, t, 0:t * P], p_row[:, 0:t * P], pj, None, ALU.is_lt)
                    if t < TT - 1:
                        nc.vector.tensor_scalar(before[:, t, (t + 1) * P:], p_row[:, (t + 1) * P:], pj, None, ALU.is_le)
                    own = p_row[:, t * P:(t + 1) * P]
                    one(nc.vector.tensor_scalar(eqm[:, :], own, pj, None, ALU.is_equal))
                    one(tt_(eqm[:, :], eqm[:, :], later[:, :], ALU.mult))
                    ins = nc.vector.scalar_tensor_tensor(before[:, t, t * P:(t + 1) * P], own, pj, eqm[:, :], ALU.is_lt, ALU.add)
                    if t < TT - 1:
                        one(ins)
                ins.then_inc(m["before_made"], 1)
                dve.wait_ge(m["ranks_ready"], 1)
                one(tt_(tmp[:, :, :], ps[:, 6, 0:TT * E].rearrange("p (t e) -> p t e", e=E), hot[:, :, :], ALU.mult))
                one(nc.vector.tensor_reduce(rk[:, :], tmp[:, :, :], axis=AX.X, op=ALU.add))
                one(nc.vector.tensor_copy(cnt[:, :], ps[:, 6, TT * E:TT * E + E]))
                one(nc.vector.tensor_scalar(over_e[:, :], cnt[:, :], -float(CAP), 0.0, ALU.add, ALU.max))
                one(nc.vector.tensor_copy(pre[:, 0:2], cnt[:, 0:1].to_broadcast([P, 2])))
                for e in range(2, E):
                    one(tt_(pre[:, e:e + 1], pre[:, e - 1:e], over_e[:, e - 1:e], ALU.add))
                one(tt_(jump[:, :], pre[:, :], base[:, :], ALU.subtract))
                one(nc.vector.tensor_scalar(jump[:, :], jump[:, :], -float(CAP), None, ALU.add))
                one(nc.vector.memset(jump[:, 0:1], 0.0))
                one(tt_(tmp[:, :, :], hot[:, :, :], base[:, None, :].to_broadcast(wide), ALU.mult))
                one(nc.vector.tensor_reduce(sa[:, :], tmp[:, :, :], axis=AX.X, op=ALU.add))
                one(tt_(tmp[:, :, :], hot[:, :, :], jump[:, None, :].to_broadcast(wide), ALU.mult))
                one(nc.vector.tensor_reduce(sj[:, :], tmp[:, :, :], axis=AX.X, op=ALU.add))
                one(nc.vector.tensor_scalar(ov[:, :], rk[:, :], float(CAP), None, ALU.is_ge))
                one(tt_(ov[:, :], ov[:, :], sj[:, :], ALU.mult))
                one(tt_(slot[:, :], sa[:, :], rk[:, :], ALU.add))
                one(tt_(slot[:, :], slot[:, :], ov[:, :], ALU.add))
                one(tt_(more[:, :], pre[:, E - 1:E], over_e[:, E - 1:E], ALU.add))
                one(nc.vector.tensor_scalar(more_i[:, :], more[:, :], float(G0), None, ALU.is_gt))
                nc.vector.tensor_copy(slot_u[:, :], slot[:, :]).then_inc(m["slots_made"], 1)
                dve.wait_ge(m["slots_made"], 1)

                def keep_x(i):
                    w = jobs[i][2] * LOADS
                    dve.wait_ge(m["x_turned"], i + 1)
                    if i:
                        dve.wait_ge(m["h_ready"], i * FC)
                    nc.vector.tensor_copy(xs0_t[:, :, 0:w], ps[:, 0:DC, 0:w]).then_inc(m["x_kept"], 1)

                def keep_y(i):
                    rows = jobs[i][2]
                    dve.wait_ge(m["y_turned"], i + 1)
                    if i:
                        dve.wait_ge(m["y_out"], 16 * i)
                    nc.vector.tensor_copy(y_nat[0:rows, :, :], ps[0:rows, 6, :].rearrange("p (c d) -> p c d", d=D)).then_inc(m["y_out_kept"], 1)

                def run(first, end):
                    keep_x(first)
                    for i in range(first, end):
                        if i > first:
                            keep_y(i - 1)
                        if i + 1 < end:
                            keep_x(i + 1)
                    keep_y(end - 1)
                batches(dve, run)
                dve.wait_ge(m["gathered"], 16 * TT)
                nc.vector.tensor_tensor(g.x_sb[:, :, :], g.x_sb[:, :, :], got[:, :, :], ALU.add).then_inc(m["done"], 1)

            @block.scalar
            def _(act):
                for c in range(DC):
                    for half in range(2):
                        act.wait_ge(m["turned"], c * 2 + half + 1)
                        nc.scalar.activation(xn_t[:, c, half * 512:(half + 1) * 512], ps[:, c * 2 + half, :], ACT.Copy).then_inc(m["turned_kept"], 1)
                act.wait_ge(m["logits_kept"], 1)
                nc.scalar.activation(lg[:, :, :], ex[:, :, :], ACT.Exp).then_inc(m["exp_made"], 1)
                for q in range(2):
                    act.wait_ge(m["p_turned"], q + 1)
                    nc.scalar.activation(p_row[:, q * 512:(q + 1) * 512], ps[:, 6 + q, :], ACT.Copy).then_inc(m["p_kept"], 1)
                act.wait_ge(m["slots_made"], 1)

                def run(first, end):
                    for i in range(first, end):
                        e, s, rows = jobs[i]
                        w = rows * LOADS
                        for f in range(FC):
                            act.wait_ge(m["h_ready"], i * FC + f + 1)
                            if i and f == 0:
                                act.wait_ge(m["y_ready"], i)
                            nc.scalar.activation(hid[:, f, 0:w], ps[:, H_BANKS[f % 3], 0:w], ACT.Relu, bias=b1[:, e, f:f + 1]).then_inc(m["h_kept"], 1)
                        act.wait_ge(m["y_ready"], i + 1)
                        if i:
                            act.wait_ge(m["y_turned"], i)
                        for c in range(DC):
                            ins = nc.scalar.activation(y_t[:, c, 0:w], ps[:, 4 + c, 0:w], ACT.Identity, bias=b2[:, e, c:c + 1])
                        ins.then_inc(m["y_kept"], 1)
                batches(act, run)

            @block.tensor
            def _(pe):
                mm, tr = nc.tensor.matmul, nc.tensor.transpose
                pe.wait_ge(m["small_in"], 16 * (1 + 2 * E))
                for c in range(DC):
                    ins = tr(ps[:, 4, c * E:(c + 1) * E], r_nat[:, c * P:(c + 1) * P], g.ident[0:E, 0:E])
                ins.then_inc(m["r_turned"], 1)
                pe.wait_ge(m["xn_made"], 1)
                for c in range(DC):
                    for half in range(2):
                        for t in range(4):
                            ins = tr(ps[:, c * 2 + half, t * P:(t + 1) * P], xn[:, half * 4 + t, c * P:(c + 1) * P], g.ident[:, :])
                        ins.then_inc(m["turned"], 1)
                pe.wait_ge(m["r_kept"], 1)
                pe.wait_ge(m["turned_kept"], 4)
                for t in range(TT):
                    for c in range(DC):
                        ins = mm(ps[:, 5, t * E:(t + 1) * E], xn_t[:, c, t * P:(t + 1) * P], r_t[:, c, :], start=c == 0, stop=c == DC - 1)
                ins.then_inc(m["logits_ready"], 1)
                pe.wait_ge(m["prob_wide"], 1)
                for q in range(2):
                    for t in range(4):
                        ins = tr(ps[:, 6 + q, t * P:(t + 1) * P], p_wide[:, q * 4 + t, :], g.ident[:, :])
                    ins.then_inc(m["p_turned"], 1)
                pe.wait_ge(m["before_made"], 1)
                for i in range(TT):
                    for j in range(TT):
                        mm(ps[:, 6, i * E:(i + 1) * E], before[:, j, i * P:(i + 1) * P], hot_b[:, j, :], start=j == 0, stop=j == TT - 1)
                for j in range(TT):
                    ins = mm(ps[:, 6, TT * E:TT * E + E], ones_b[:, :], hot_b[:, j, :], start=j == 0, stop=j == TT - 1)
                ins.then_inc(m["ranks_ready"], 1)
                pe.wait_ge(m["slots_made"], 1)

                def turn_x(i):
                    e, s, rows = jobs[i]
                    pe.wait_ge(m["x_in"], 16 * (i + 1))
                    for c in range(DC):
                        for q in range(LOADS):
                            ins = tr(ps[:, c, q * rows:(q + 1) * rows], xs0[0:rows, q, c * P:(c + 1) * P], g.ident[0:rows, 0:rows])
                    ins.then_inc(m["x_turned"], 1)

                def turn_y(i):
                    rows = jobs[i][2]
                    pe.wait_ge(m["y_kept"], i + 1)
                    if i:
                        pe.wait_ge(m["y_out_kept"], i)
                    for q in range(LOADS):
                        for c in range(DC):
                            ins = tr(ps[0:rows, 6, q * D + c * P:q * D + (c + 1) * P], y_t[:, c, q * rows:(q + 1) * rows], g.ident[:, :])
                    ins.then_inc(m["y_turned"], 1)

                def run(first, end):
                    turn_x(first)
                    for i in range(first, end):
                        e, s, rows = jobs[i]
                        w, slot_w = rows * LOADS, min(i, JOBS1 - 1) % WS
                        pe.wait_ge(m["x_kept"], i + 1)
                        pe.wait_ge(m["w1_in"], 16 * min(i + 1, JOBS1))
                        for f in range(FC):
                            if i * FC + f >= 3:
                                pe.wait_ge(m["h_kept"], i * FC + f - 2)
                            for c in range(DC):
                                ins = mm(ps[:, H_BANKS[f % 3], 0:w], w1[:, slot_w, c, f * P:(f + 1) * P], xs0_t[:, c, 0:w], start=c == 0, stop=c == DC - 1)
                            ins.then_inc(m["h_ready"], 1)
                        if i > first:
                            turn_y(i - 1)
                        if i + 1 < end:
                            turn_x(i + 1)
                        pe.wait_ge(m["w2_in"], 16 * min(i + 1, JOBS1))
                        pe.wait_ge(m["h_kept"], (i + 1) * FC)
                        if i:
                            pe.wait_ge(m["y_kept"], i)
                        for c in range(DC):
                            for f in range(FC):
                                ins = mm(ps[:, 4 + c, 0:w], w2[:, slot_w, f, c * P:(c + 1) * P], hid[:, f, 0:w], start=f == 0, stop=f == FC - 1)
                        ins.then_inc(m["y_ready"], 1)
                        if i < JOBS1 - WS:
                            pe.wait_ge(m["y_ready"], i + 1)
                            pe.sem_inc(m["w_done"], 1)
                    turn_y(end - 1)
                batches(pe, run)

        clear_semaphores(nc, mine)


def program(nc, args, out):
    top = ExitStack()
    with top:
        g = Shared()
        (x, ctx_, g.xWq, g.xbq, g.xWk, g.xbk, g.xWv, g.xbv, g.xWo, g.xbo, g.dWq, g.dWk, g.dWv, g.dWb, g.lnw, g.lnb,
         g.router, g.W1, g.b1, g.W2, g.b2) = args
        g.x = x.rearrange("b s d -> (b s) d")
        g.ctx = ctx_.rearrange("b n d -> (b n) d")
        g.out = out.rearrange("b s d -> (b s) d")
        g.qq = nc.dram_tensor("q_parts", (HEADS, PARTS, HD, S), BF16, kind="Internal").ap()
        g.kk = nc.dram_tensor("k_parts", (HEADS, PARTS, HD, N), BF16, kind="Internal").ap()
        g.vv = nc.dram_tensor("v_heads", (HEADS, P, N // P * HD), F32, kind="Internal").ap()

        g.xs = nc.dram_tensor("slot_rows", (TOK + 7 * 160, D), F32, kind="Internal").ap()
        g.ys = nc.dram_tensor("slot_outputs", (TOK + 7 * 160, D), F32, kind="Internal").ap()

        def sb(n, s, d=F32):
            return top.enter_context(nc.sbuf_tensor(n, s, d))
        g.x_sb = sb("x_sb", [P, TT, D])
        g.ident = sb("ident", [P, P])
        g.ident_b = sb("ident_b", [P, P], BF16)
        g.minus_b = sb("minus_b", [P, P], BF16)
        g.flags = sb("flags", [P, HEADS, ST])
        g.u = sb("u", [P, HEADS, ST, HD + 1])
        with ExitStack() as early:
            def sb(n, s, d=F32):
                return early.enter_context(nc.sbuf_tensor(n, s, d))
            g.bq, g.bk, g.bv_bc = sb("bq", [P, DC]), sb("bk", [P, DC]), sb("bv_bc", [P, D])
            g.wk_t, g.wv_t = sb("wk_t", [P, DC, D]), sb("wv_t", [P, DC, D])
            g.q32 = sb("q32", [P, DC, TOK])
            stage_setup(nc, g)
            stage_keys(nc, g)
        stage_attention(nc, g)
        stage_exact(nc, g)
        stage_out(nc, g)
        stage_delta(nc, g)
        stage_experts(nc, g)


_INS = ['x', 'ctx_1024', 'L0_xattn_Wq', 'L0_xattn_bq', 'L0_xattn_Wk', 'L0_xattn_bk', 'L0_xattn_Wv', 'L0_xattn_bv',
        'L0_xattn_Wo', 'L0_xattn_bo', 'L0_attn_Wq', 'L0_attn_Wk', 'L0_attn_Wv', 'L0_attn_Wb', 'L0_attn_ln_w',
        'L0_attn_ln_b', 'L0_ffn_router_w', 'L0_ffn_W1', 'L0_ffn_b1', 'L0_ffn_W2', 'L0_ffn_b2']


def kernel(**inputs):
    import numpy as _np
    import concourse.bacc as _bacc
    from concourse import mybir as _mybir
    from concourse.bass_utils import run_bass_kernel_spmd as _run

    nc = _bacc.Bacc("TRN2", target_bir_lowering=False, num_devices=1)
    arrays, args = {}, []
    for name in _INS:
        a = _np.ascontiguousarray(inputs[name])
        arrays[f"in_{name}"] = a
        args.append(nc.dram_tensor(f"in_{name}", a.shape, _mybir.dt.from_np(a.dtype), kind="ExternalInput").ap())
    out = nc.dram_tensor("out_x", (4, 256, 256), _mybir.dt.float32, kind="ExternalOutput").ap()
    program(nc, args, out)
    r = _run(nc, [arrays], core_ids=[0])
    return r.results[0]["out_x"]
```
